# Optimizing a Trainium2 kernel written in Bass

```python
import numpy as np
import jax
import jax.numpy as jnp

def _softmax(x, axis=-1):
    return jax.nn.softmax(x, axis=axis)

def _gelu(x):
    return jax.nn.gelu(x, approximate=True)

def _silu(x):
    return jax.nn.silu(x)

def _sigmoid(x):
    return jax.nn.sigmoid(x)

def _layernorm(x, axis=-1, eps=1e-05):
    m = jnp.mean(x, axis=axis, keepdims=True)
    v = jnp.var(x, axis=axis, keepdims=True)
    return (x - m) / jnp.sqrt(v + eps)

def _scatter_add(tgt, idx, src, axis=0):
    return tgt.at[idx].add(src)

def _segment_sum(src, seg, n):
    return jax.ops.segment_sum(src, seg, n)
kernel_name = 'mk_decoder_postln_d1_seqx_r8_32a30b'

def setup_inputs(seed: int=0):
    np.random.seed(seed)
    _w = jnp.asarray

    def _rec_inputs():
        import jax
        import jax.numpy as jnp
        _rk = jax.random.key(seed)
        x = -4.161e-06 + 1 * jax.random.normal(jax.random.fold_in(_rk, 1), (16, 64, 256), jnp.float32)
        _lenS = 64 - jax.random.randint(jax.random.fold_in(_rk, 7), (16,), 0, max(1, 64 // 4) + 1, jnp.int32)
        _lenS2 = 64 - jax.random.randint(jax.random.fold_in(_rk, 8), (16,), 0, max(1, 64 // 4) + 1, jnp.int32)
        _ctx_2048P = jax.random.normal(jax.random.fold_in(_rk, 11), (16, 16, 256), jnp.float32)
        _ctx_2048c = jax.random.dirichlet(jax.random.fold_in(_rk, 511), 0.3 * jnp.ones((16,), jnp.float32), (16, 64))
        _ctx_2048t = jnp.einsum('bsk,bkd->bsd', _ctx_2048c, _ctx_2048P)
        _ctx_2048t = _ctx_2048t * jax.lax.rsqrt(jnp.mean(jnp.square(_ctx_2048t)) + 1e-12) * 0.953939
        ctx_2048 = -0.000192764 + 0.999654 * (_ctx_2048t + 0.3 * jax.random.normal(jax.random.fold_in(_rk, 611), (16, 64, 256), jnp.float32))
        return (x, ctx_2048)
    x, ctx_2048 = _rec_inputs()

    def _L0_attn_setup():
        import jax, jax.numpy as jnp
        import numpy as np
        EPS_L2 = 1e-06
        NORM_EPS = 1e-05

        def short_conv(x, w):
            K = w.shape[1]
            T = x.shape[1]
            xp = jnp.pad(x, ((0, 0), (K - 1, 0), (0, 0)))
            y = xp[:, 0:T, :] * w[:, 0]
            for i in range(1, K):
                y = y + xp[:, i:i + T, :] * w[:, i]
            return jax.nn.silu(y)

        def l2norm(x):
            return x * jax.lax.rsqrt(jnp.sum(x * x, axis=-1, keepdims=True) + EPS_L2)

        def gated_delta_rule(q, k, v, g, beta):

            def per_head(qh, kh, vh, gh, bh):

                def step(S, inp):
                    qt, kt, vt, gt, bt = inp
                    S = S * jnp.exp(gt)
                    delta = (vt - kt @ S) * bt
                    S = S + kt[:, None] * delta[None, :]
                    return (S, qt @ S)
                S0 = jnp.zeros((qh.shape[-1], vh.shape[-1]), jnp.float32)
                _, o = jax.lax.scan(jax.checkpoint(step), S0, (qh, kh, vh, gh, bh))
                return o
            fh = jax.vmap(per_head, in_axes=(1, 1, 1, 1, 1), out_axes=1)
            fb = jax.vmap(fh, in_axes=0, out_axes=0)
            return fb(q, k, v, g, beta)
        key = jax.random.key(seed)
        ks = jax.random.split(key, 16)
        B, T, HID = (1, 128, 256)
        H, DK, DV = (12, 128, 32)
        KDIM, VDIM, KS = (H * DK, H * DV, 4)
        s = 0.02
        hidden_states = jax.random.normal(ks[0], (B, T, HID), jnp.float32)
        Wq = jax.random.normal(ks[1], (HID, KDIM), jnp.float32) * s
        Wk = jax.random.normal(ks[2], (HID, KDIM), jnp.float32) * s
        Wv = jax.random.normal(ks[3], (HID, VDIM), jnp.float32) * s
        Wb = jax.random.normal(ks[4], (HID, H), jnp.float32) * s
        Wa = jax.random.normal(ks[5], (HID, H), jnp.float32) * s
        Wg = jax.random.normal(ks[6], (HID, VDIM), jnp.float32) * s
        Wo = jax.random.normal(ks[7], (VDIM, HID), jnp.float32) * s
        conv_wq = jax.random.normal(ks[8], (KDIM, KS), jnp.float32) * 0.1
        conv_wk = jax.random.normal(ks[9], (KDIM, KS), jnp.float32) * 0.1
        conv_wv = jax.random.normal(ks[10], (VDIM, KS), jnp.float32) * 0.1
        A_log = jnp.log(jax.random.uniform(ks[11], (H,), jnp.float32, 0.5, 8.0))
        dt = jnp.exp(jax.random.uniform(ks[12], (H,), jnp.float32) * (np.log(0.1) - np.log(0.001)) + np.log(0.001))
        dt = jnp.clip(dt, 0.0001, None)
        dt_bias = dt + jnp.log(-jnp.expm1(-dt))
        norm_w = jnp.ones((DV,), jnp.float32)
        return {'hidden_states': hidden_states, 'Wq': Wq, 'Wk': Wk, 'Wv': Wv, 'Wb': Wb, 'Wa': Wa, 'Wg': Wg, 'Wo': Wo, 'conv_wq': conv_wq, 'conv_wk': conv_wk, 'conv_wv': conv_wv, 'A_log': A_log, 'dt_bias': dt_bias, 'norm_w': norm_w}
    _L0_attn_all = _L0_attn_setup()
    _L0_attn_in = {k: v for k, v in _L0_attn_all.items() if k in ('Wq', 'Wk', 'Wv', 'Wb', 'Wa', 'Wg', 'Wo', 'conv_wq', 'conv_wk', 'conv_wv', 'A_log', 'dt_bias', 'norm_w')}
    del _L0_attn_all

    def _L0_xattn_setup():
        import jax, jax.numpy as jnp
        import numpy as np
        FP8_MAX = 448.0
        EPS = 1e-05

        def _fp8_roundtrip(x):
            return x.astype(jnp.float8_e4m3fn).astype(jnp.float32)

        def _div_clamp_fp8(x, scale):
            y = jnp.clip(x.astype(jnp.float32) / scale, -FP8_MAX, FP8_MAX)
            y = y.astype(jnp.bfloat16).astype(jnp.float32)
            return _fp8_roundtrip(y)

        def _ln(x, w, b):
            mu = jnp.mean(x, axis=-1, keepdims=True)
            var = jnp.mean(jnp.square(x - mu), axis=-1, keepdims=True)
            return (x - mu) * jax.lax.rsqrt(var + EPS) * w + b

        def _fp8_linear_pertensor(x, wq, w_scale, in_scale):
            xq = _div_clamp_fp8(x, in_scale)
            return jnp.einsum('bsi,oi->bso', xq * in_scale, wq) * w_scale

        def _gqa(q, k, v):
            scale = 1.0 / np.sqrt(q.shape[-1])
            scores = jnp.einsum('bsghd,btgd->bghst', q, k) * scale
            p = jax.nn.softmax(scores, axis=-1)
            return jnp.einsum('bghst,btgd->bsghd', p, v)
        key = jax.random.key(seed)
        ks = jax.random.split(key, 8)
        B, S, SC, H, NH, G, D = (2, 256, 64, 256, 16, 8, 128)

        def qw(k, out_f, in_f):
            w = jax.random.normal(k, (out_f, in_f), jnp.float32) * 0.02
            sc = jnp.max(jnp.abs(w)) / FP8_MAX
            return (_fp8_roundtrip(w / sc), sc.astype(jnp.float32))
        wq, wq_s = qw(ks[0], NH * D, H)
        wqx, wqx_s = qw(ks[1], NH * D, H)
        wk, wk_s = qw(ks[2], G * D, H)
        wv, wv_s = qw(ks[3], G * D, H)
        wproj, wp_s = qw(ks[4], H, 2 * NH * D)
        return {'hidden_states': jax.random.normal(ks[5], (B, S, H), jnp.float32), 'cond': jax.random.normal(ks[6], (B, SC, H), jnp.float32), 'ln_w': jnp.ones((H,), jnp.float32), 'ln_b': jnp.zeros((H,), jnp.float32), 'wq': wq, 'wq_scale': wq_s, 'q_in_scale': jnp.full((H,), 0.05, jnp.float32), 'wqx': wqx, 'wqx_scale': wqx_s, 'qx_in_scale': jnp.full((H,), 0.05, jnp.float32), 'wk': wk, 'wk_scale': wk_s, 'k_in_scale': jnp.full((H,), 0.05, jnp.float32), 'wv': wv, 'wv_scale': wv_s, 'v_in_scale': jnp.full((H,), 0.05, jnp.float32), 'w_kv_x': jax.random.normal(ks[7], (2 * G * D, H), jnp.float32) * 0.02, 'qln_w': jnp.ones((D,), jnp.float32), 'qln_b': jnp.zeros((D,), jnp.float32), 'kln_w': jnp.ones((D,), jnp.float32), 'kln_b': jnp.zeros((D,), jnp.float32), 'qxln_w': jnp.ones((D,), jnp.float32), 'qxln_b': jnp.zeros((D,), jnp.float32), 'kxln_w': jnp.ones((D,), jnp.float32), 'kxln_b': jnp.zeros((D,), jnp.float32), 'wproj': wproj, 'proj_w_scale': wp_s, 'proj_in_scale': jnp.asarray(0.05, jnp.float32), 'proj_smooth': jnp.full((2 * NH * D,), 0.05, jnp.float32)}
    _L0_xattn_all = _L0_xattn_setup()
    _L0_xattn_in = {k: v for k, v in _L0_xattn_all.items() if k in ('ln_w', 'ln_b', 'wq', 'wq_scale', 'q_in_scale', 'wqx', 'wqx_scale', 'qx_in_scale', 'wk', 'wk_scale', 'k_in_scale', 'wv', 'wv_scale', 'v_in_scale', 'w_kv_x', 'qln_w', 'qln_b', 'kln_w', 'kln_b', 'qxln_w', 'qxln_b', 'kxln_w', 'kxln_b', 'wproj', 'proj_w_scale', 'proj_in_scale', 'proj_smooth')}
    del _L0_xattn_all

    def _L0_ffn_setup():
        import jax, jax.numpy as jnp
        import numpy as np
        B, T, C = (2, 128, 256)
        E, TOPK = (8, 2)
        F_MOE = 176
        F_SHARED = 704
        key = jax.random.key(seed)
        ks = jax.random.split(key, 9)
        s = 0.02
        return {'x': jax.random.normal(ks[0], (B, T, C), dtype=jnp.float32), 'gate_w': jax.random.normal(ks[1], (E, C), dtype=jnp.float32) * s, 'expert_fc1': jax.random.normal(ks[2], (E, F_MOE, C), dtype=jnp.float32) * s, 'expert_fc2': jax.random.normal(ks[3], (E, F_MOE, C), dtype=jnp.float32) * s, 'expert_proj': jax.random.normal(ks[4], (E, C, F_MOE), dtype=jnp.float32) * s, 'shared_fc1': jax.random.normal(ks[5], (F_SHARED, C), dtype=jnp.float32) * s, 'shared_fc2': jax.random.normal(ks[6], (F_SHARED, C), dtype=jnp.float32) * s, 'shared_proj': jax.random.normal(ks[7], (C, F_SHARED), dtype=jnp.float32) * s, 'shared_gate_w': jax.random.normal(ks[8], (1, C), dtype=jnp.float32) * s}
    _L0_ffn_all = _L0_ffn_setup()
    _L0_ffn_in = {k: v for k, v in _L0_ffn_all.items() if k in ('gate_w', 'expert_fc1', 'expert_fc2', 'expert_proj', 'shared_fc1', 'shared_fc2', 'shared_proj', 'shared_gate_w')}
    del _L0_ffn_all
    return {'x': x, 'ctx_2048': ctx_2048, 'L0_attn_Wq': _L0_attn_in['Wq'], 'L0_attn_Wk': _L0_attn_in['Wk'], 'L0_attn_Wv': _L0_attn_in['Wv'], 'L0_attn_Wb': _L0_attn_in['Wb'], 'L0_attn_Wa': _L0_attn_in['Wa'], 'L0_attn_Wg': _L0_attn_in['Wg'], 'L0_attn_Wo': _L0_attn_in['Wo'], 'L0_attn_conv_wq': _L0_attn_in['conv_wq'], 'L0_attn_conv_wk': _L0_attn_in['conv_wk'], 'L0_attn_conv_wv': _L0_attn_in['conv_wv'], 'L0_attn_A_log': _L0_attn_in['A_log'], 'L0_attn_dt_bias': _L0_attn_in['dt_bias'], 'L0_attn_norm_w': _L0_attn_in['norm_w'], 'L0_xattn_ln_w': _L0_xattn_in['ln_w'], 'L0_xattn_ln_b': _L0_xattn_in['ln_b'], 'L0_xattn_wq': _L0_xattn_in['wq'], 'L0_xattn_wq_scale': _L0_xattn_in['wq_scale'], 'L0_xattn_q_in_scale': _L0_xattn_in['q_in_scale'], 'L0_xattn_wqx': _L0_xattn_in['wqx'], 'L0_xattn_wqx_scale': _L0_xattn_in['wqx_scale'], 'L0_xattn_qx_in_scale': _L0_xattn_in['qx_in_scale'], 'L0_xattn_wk': _L0_xattn_in['wk'], 'L0_xattn_wk_scale': _L0_xattn_in['wk_scale'], 'L0_xattn_k_in_scale': _L0_xattn_in['k_in_scale'], 'L0_xattn_wv': _L0_xattn_in['wv'], 'L0_xattn_wv_scale': _L0_xattn_in['wv_scale'], 'L0_xattn_v_in_scale': _L0_xattn_in['v_in_scale'], 'L0_xattn_w_kv_x': _L0_xattn_in['w_kv_x'], 'L0_xattn_qln_w': _L0_xattn_in['qln_w'], 'L0_xattn_qln_b': _L0_xattn_in['qln_b'], 'L0_xattn_kln_w': _L0_xattn_in['kln_w'], 'L0_xattn_kln_b': _L0_xattn_in['kln_b'], 'L0_xattn_qxln_w': _L0_xattn_in['qxln_w'], 'L0_xattn_qxln_b': _L0_xattn_in['qxln_b'], 'L0_xattn_kxln_w': _L0_xattn_in['kxln_w'], 'L0_xattn_kxln_b': _L0_xattn_in['kxln_b'], 'L0_xattn_wproj': _L0_xattn_in['wproj'], 'L0_xattn_proj_w_scale': _L0_xattn_in['proj_w_scale'], 'L0_xattn_proj_in_scale': _L0_xattn_in['proj_in_scale'], 'L0_xattn_proj_smooth': _L0_xattn_in['proj_smooth'], 'L0_ffn_gate_w': _L0_ffn_in['gate_w'], 'L0_ffn_expert_fc1': _L0_ffn_in['expert_fc1'], 'L0_ffn_expert_fc2': _L0_ffn_in['expert_fc2'], 'L0_ffn_expert_proj': _L0_ffn_in['expert_proj'], 'L0_ffn_shared_fc1': _L0_ffn_in['shared_fc1'], 'L0_ffn_shared_fc2': _L0_ffn_in['shared_fc2'], 'L0_ffn_shared_proj': _L0_ffn_in['shared_proj'], 'L0_ffn_shared_gate_w': _L0_ffn_in['shared_gate_w']}

def reference(x, ctx_2048, L0_attn_Wq, L0_attn_Wk, L0_attn_Wv, L0_attn_Wb, L0_attn_Wa, L0_attn_Wg, L0_attn_Wo, L0_attn_conv_wq, L0_attn_conv_wk, L0_attn_conv_wv, L0_attn_A_log, L0_attn_dt_bias, L0_attn_norm_w, L0_xattn_ln_w, L0_xattn_ln_b, L0_xattn_wq, L0_xattn_wq_scale, L0_xattn_q_in_scale, L0_xattn_wqx, L0_xattn_wqx_scale, L0_xattn_qx_in_scale, L0_xattn_wk, L0_xattn_wk_scale, L0_xattn_k_in_scale, L0_xattn_wv, L0_xattn_wv_scale, L0_xattn_v_in_scale, L0_xattn_w_kv_x, L0_xattn_qln_w, L0_xattn_qln_b, L0_xattn_kln_w, L0_xattn_kln_b, L0_xattn_qxln_w, L0_xattn_qxln_b, L0_xattn_kxln_w, L0_xattn_kxln_b, L0_xattn_wproj, L0_xattn_proj_w_scale, L0_xattn_proj_in_scale, L0_xattn_proj_smooth, L0_ffn_gate_w, L0_ffn_expert_fc1, L0_ffn_expert_fc2, L0_ffn_expert_proj, L0_ffn_shared_fc1, L0_ffn_shared_fc2, L0_ffn_shared_proj, L0_ffn_shared_gate_w):
    import jax
    import jax.numpy as jnp

    def _L0_attn_ref(hidden_states, Wq, Wk, Wv, Wb, Wa, Wg, Wo, conv_wq, conv_wk, conv_wv, A_log, dt_bias, norm_w):
        import jax, jax.numpy as jnp
        import numpy as np
        EPS_L2 = 1e-06
        NORM_EPS = 1e-05

        def short_conv(x, w):
            K = w.shape[1]
            T = x.shape[1]
            xp = jnp.pad(x, ((0, 0), (K - 1, 0), (0, 0)))
            y = xp[:, 0:T, :] * w[:, 0]
            for i in range(1, K):
                y = y + xp[:, i:i + T, :] * w[:, i]
            return jax.nn.silu(y)

        def l2norm(x):
            return x * jax.lax.rsqrt(jnp.sum(x * x, axis=-1, keepdims=True) + EPS_L2)

        def gated_delta_rule(q, k, v, g, beta):

            def per_head(qh, kh, vh, gh, bh):

                def step(S, inp):
                    qt, kt, vt, gt, bt = inp
                    S = S * jnp.exp(gt)
                    delta = (vt - kt @ S) * bt
                    S = S + kt[:, None] * delta[None, :]
                    return (S, qt @ S)
                S0 = jnp.zeros((qh.shape[-1], vh.shape[-1]), jnp.float32)
                _, o = jax.lax.scan(jax.checkpoint(step), S0, (qh, kh, vh, gh, bh))
                return o
            fh = jax.vmap(per_head, in_axes=(1, 1, 1, 1, 1), out_axes=1)
            fb = jax.vmap(fh, in_axes=0, out_axes=0)
            return fb(q, k, v, g, beta)
        B, T, _ = hidden_states.shape
        H = A_log.shape[0]
        q = short_conv(hidden_states @ Wq, conv_wq)
        k = short_conv(hidden_states @ Wk, conv_wk)
        v = short_conv(hidden_states @ Wv, conv_wv)
        q = l2norm(q.reshape(B, T, H, -1))
        k = l2norm(k.reshape(B, T, H, -1))
        v = v.reshape(B, T, H, -1)
        beta = jax.nn.sigmoid(hidden_states @ Wb)
        g = -jnp.exp(A_log) * jax.nn.softplus(hidden_states @ Wa + dt_bias)
        o = gated_delta_rule(q, k, v, g, beta)
        gg = (hidden_states @ Wg).reshape(B, T, H, -1)
        o_n = o * jax.lax.rsqrt(jnp.mean(o * o, axis=-1, keepdims=True) + NORM_EPS) * norm_w
        o_n = o_n * jax.nn.silu(gg)
        return o_n.reshape(B, T, -1) @ Wo

    def _L0_xattn_ref(hidden_states, cond, ln_w, ln_b, wq, wq_scale, q_in_scale, wqx, wqx_scale, qx_in_scale, wk, wk_scale, k_in_scale, wv, wv_scale, v_in_scale, w_kv_x, qln_w, qln_b, kln_w, kln_b, qxln_w, qxln_b, kxln_w, kxln_b, wproj, proj_w_scale, proj_in_scale, proj_smooth):
        import jax, jax.numpy as jnp
        import numpy as np
        FP8_MAX = 448.0
        EPS = 1e-05

        def _fp8_roundtrip(x):
            return x.astype(jnp.float8_e4m3fn).astype(jnp.float32)

        def _div_clamp_fp8(x, scale):
            y = jnp.clip(x.astype(jnp.float32) / scale, -FP8_MAX, FP8_MAX)
            y = y.astype(jnp.bfloat16).astype(jnp.float32)
            return _fp8_roundtrip(y)

        def _ln(x, w, b):
            mu = jnp.mean(x, axis=-1, keepdims=True)
            var = jnp.mean(jnp.square(x - mu), axis=-1, keepdims=True)
            return (x - mu) * jax.lax.rsqrt(var + EPS) * w + b

        def _fp8_linear_pertensor(x, wq, w_scale, in_scale):
            xq = _div_clamp_fp8(x, in_scale)
            return jnp.einsum('bsi,oi->bso', xq * in_scale, wq) * w_scale

        def _gqa(q, k, v):
            scale = 1.0 / np.sqrt(q.shape[-1])
            scores = jnp.einsum('bsghd,btgd->bghst', q, k) * scale
            p = jax.nn.softmax(scores, axis=-1)
            return jnp.einsum('bghst,btgd->bsghd', p, v)
        b, s, _ = hidden_states.shape
        sc = cond.shape[1]
        d = qln_w.shape[0]
        nh = wq.shape[0] // d
        g = wk.shape[0] // d
        hpg = nh // g
        ln_out = _ln(hidden_states, ln_w, ln_b)
        q = _fp8_linear_pertensor(ln_out, wq, wq_scale, q_in_scale).reshape(b, s, g, hpg, d)
        q = _ln(q, qln_w, qln_b)
        k = _fp8_linear_pertensor(ln_out, wk, wk_scale, k_in_scale).reshape(b, s, g, d)
        k = _ln(k, kln_w, kln_b)
        v = _fp8_linear_pertensor(ln_out, wv, wv_scale, v_in_scale).reshape(b, s, g, d)
        core = _gqa(q, k, v).reshape(b, s, nh * d)
        qx = _fp8_linear_pertensor(ln_out, wqx, wqx_scale, qx_in_scale).reshape(b, s, g, hpg, d)
        qx = _ln(qx, qxln_w, qxln_b)
        kvx = jnp.einsum('bsi,oi->bso', cond, w_kv_x)
        kx, vx = jnp.split(kvx, 2, axis=-1)
        kx = _ln(kx.reshape(b, sc, g, d), kxln_w, kxln_b)
        vx = vx.reshape(b, sc, g, d)
        xout = _gqa(qx, kx, vx).reshape(b, s, nh * d)
        cat = jnp.concatenate([core, xout], axis=-1)
        catq = _div_clamp_fp8(cat, proj_smooth)
        return jnp.einsum('bsi,oi->bso', catq, wproj) * (proj_in_scale * proj_w_scale)

    def _L0_ffn_ref(x, gate_w, expert_fc1, expert_fc2, expert_proj, shared_fc1, shared_fc2, shared_proj, shared_gate_w):
        import jax, jax.numpy as jnp
        import numpy as np
        B, T, C = (2, 128, 256)
        E, TOPK = (8, 2)
        F_MOE = 176
        F_SHARED = 704
        b, t, c = x.shape
        xf = x.reshape(-1, c)
        n = xf.shape[0]
        router = xf @ gate_w.T
        probs = jax.nn.softmax(router.astype(jnp.float32), axis=1).astype(x.dtype)
        top_p, top_i = jax.lax.top_k(probs, TOPK)
        combine = jnp.zeros((n, E), dtype=x.dtype).at[jnp.arange(n)[:, None], top_i].set(top_p)
        h1 = jnp.einsum('nc,efc->enf', xf, expert_fc1)
        h2 = jnp.einsum('nc,efc->enf', xf, expert_fc2)
        h = jax.nn.silu(h1) * h2
        out_e = jnp.einsum('enf,ecf->enc', h, expert_proj)
        y = jnp.einsum('ne,enc->nc', combine, out_e)
        s1 = xf @ shared_fc1.T
        s2 = xf @ shared_fc2.T
        shared = jax.nn.silu(s1) * s2 @ shared_proj.T
        y = y + jax.nn.sigmoid(xf @ shared_gate_w.T) * shared
        return y.reshape(b, t, c)
    x = _layernorm(x + _L0_attn_ref(x, L0_attn_Wq, L0_attn_Wk, L0_attn_Wv, L0_attn_Wb, L0_attn_Wa, L0_attn_Wg, L0_attn_Wo, L0_attn_conv_wq, L0_attn_conv_wk, L0_attn_conv_wv, L0_attn_A_log, L0_attn_dt_bias, L0_attn_norm_w), axis=-1)
    x = _layernorm(x + _L0_xattn_ref(x, ctx_2048, L0_xattn_ln_w, L0_xattn_ln_b, L0_xattn_wq, L0_xattn_wq_scale, L0_xattn_q_in_scale, L0_xattn_wqx, L0_xattn_wqx_scale, L0_xattn_qx_in_scale, L0_xattn_wk, L0_xattn_wk_scale, L0_xattn_k_in_scale, L0_xattn_wv, L0_xattn_wv_scale, L0_xattn_v_in_scale, L0_xattn_w_kv_x, L0_xattn_qln_w, L0_xattn_qln_b, L0_xattn_kln_w, L0_xattn_kln_b, L0_xattn_qxln_w, L0_xattn_qxln_b, L0_xattn_kxln_w, L0_xattn_kxln_b, L0_xattn_wproj, L0_xattn_proj_w_scale, L0_xattn_proj_in_scale, L0_xattn_proj_smooth), axis=-1)
    x = _layernorm(x + _L0_ffn_ref(x, L0_ffn_gate_w, L0_ffn_expert_fc1, L0_ffn_expert_fc2, L0_ffn_expert_proj, L0_ffn_shared_fc1, L0_ffn_shared_fc2, L0_ffn_shared_proj, L0_ffn_shared_gate_w), axis=-1)
    return x

_drawn_inputs = setup_inputs


def setup_inputs(seed=0):
    import zlib

    import numpy as np

    out = dict(_drawn_inputs(seed))
    spreads = {'L0_attn_norm_w': (1.0, 0.6),
     'L0_xattn_ln_w': (1.0, 0.564),
     'L0_xattn_ln_b': (0.0, 0.1),
     'L0_xattn_q_in_scale': (0.05000000074505806, 0.6),
     'L0_xattn_qx_in_scale': (0.05000000074505806, 0.6),
     'L0_xattn_k_in_scale': (0.05000000074505806, 0.6),
     'L0_xattn_v_in_scale': (0.05000000074505806, 0.6),
     'L0_xattn_qln_w': (1.0, 0.6),
     'L0_xattn_qln_b': (0.0, 0.8),
     'L0_xattn_kln_w': (1.0, 0.6),
     'L0_xattn_kln_b': (0.0, 0.8),
     'L0_xattn_qxln_w': (1.0, 0.6),
     'L0_xattn_qxln_b': (0.0, 0.8),
     'L0_xattn_kxln_w': (1.0, 0.6),
     'L0_xattn_kxln_b': (0.0, 0.8),
     'L0_xattn_proj_smooth': (0.05000000074505806, 0.2)}
    factors = {'L0_attn_Wb': 6.989,
     'L0_attn_Wa': 8.0,
     'L0_attn_A_log': 8.0,
     'L0_attn_dt_bias': 3.323,
     'L0_ffn_gate_w': 8.0,
     'L0_ffn_expert_fc1': 8.0,
     'L0_ffn_expert_fc2': 8.0,
     'L0_ffn_expert_proj': 8.0,
     'L0_ffn_shared_fc1': 4.016,
     'L0_ffn_shared_fc2': 3.99,
     'L0_ffn_shared_proj': 3.981,
     'L0_ffn_shared_gate_w': 8.0}
    for name, (base, spread) in spreads.items():
        noise = np.random.default_rng([zlib.crc32(name.encode()), seed]).standard_normal(out[name].shape)
        drawn = base * np.exp(spread * noise) if base else spread * noise
        out[name] = jnp.asarray(drawn.astype(out[name].dtype))
    for name, factor in factors.items():
        out[name] = (out[name] * factor).astype(out[name].dtype)
    return out
```

```python
from contextlib import ExitStack

import numpy as np
import concourse.bass as bass
from concourse import mybir

F32 = mybir.dt.float32
F16 = mybir.dt.float16
BF16 = mybir.dt.bfloat16
U16 = mybir.dt.uint16
U32 = mybir.dt.uint32
ALU = mybir.AluOpType
ACT = mybir.ActivationFunctionType
AX = mybir.AxisListType

P = 128
T = 64
D = 256
KT = D // P
NTOK = 1024
NT = NTOK // P
H = 12
DV = 32
HV = H * DV
NPAIR = H // 2
CH1 = 24 + 2 * H * P + 2 * HV
WS = 64.0
BLK = 16
NBLK = P // BLK
EPS = 1e-5


class Tile:

    def __init__(self, off, reg=None, stride=2):
        self.off, self.reg, self.stride = off, reg, stride

    def value(self, per, k=0):
        base = self.off * per + k
        return base if self.reg is None else self.reg * (self.stride * per) + base

    def before(self, n=1):
        return Tile(self.off - n, self.reg, self.stride)

    @property
    def exists(self):
        return self.reg is not None or self.off >= 0

    @property
    def parity(self):
        return self.off % 2


class Signal:

    def __init__(self, sem, per):
        self.sem, self.per = sem, per

    def wait(self, eng, t, k):
        if t.exists:
            eng.wait_ge(self.sem, t.value(self.per, k))

    def count(self, eng, t, k):
        if t.reg is None:
            return t.value(self.per, k)
        reg = eng.alloc_register(f"count_{eng.bass.next_id()}")
        eng.reg_mov(reg, t.value(self.per, k))
        return eng.snap(reg, min_val=0)


class Chain:

    def __init__(self, eng, sem):
        self.eng, self.sem, self.n = eng, sem, 0

    def __call__(self, ins):
        self.n += 1
        ins.then_inc(self.sem, 1)
        self.eng.wait_ge(self.sem, self.n)


class TileChain:

    def __init__(self, eng, sem):
        self.eng, self.sem, self.per, self.n, self.t = eng, sem, 0, 0, None

    def start(self, t):
        if self.t is not None and self.per == 0:
            self.per = self.n
        self.t, self.n = t, 0

    def mark(self, ins):
        self.n += 1
        ins.then_inc(self.sem, 1)
        return self.n

    def wait(self, n=None):
        self.eng.wait_ge(self.sem, self.t.value(self.per, self.n if n is None else n))

    def __call__(self, ins):
        self.mark(ins)
        self.wait()


def over(ap, axis, shape):
    return ap.unsqueeze(axis).broadcast_to(shape)


def skewed_tiles(eng, front):
    front(Tile(0), None)
    front(Tile(1), Tile(0))
    with eng.Fori(0, (NT - 2) // 2) as i:
        front(Tile(2, i), Tile(1, i))
        front(Tile(3, i), Tile(2, i))
    front(None, Tile(NT - 1))


def stage1(nc, io, X):
    with ExitStack() as ctx:
        def sb(name, shape, dt=F32):
            return ctx.enter_context(nc.sbuf_tensor(name, [P] + shape, dt))

        def pb(name):
            return ctx.enter_context(nc.psum_tensor(name, [P, 512], F32))

        def sem(name):
            return ctx.enter_context(nc.semaphore(name))

        def sig(name, per):
            return Signal(sem(name), per)

        xT32 = sb("xT32", [KT, NTOK])
        xh = sb("xh", [KT, NTOK], F16)
        xl = sb("xl", [KT, NTOK], F16)
        w32 = sb("w32", [KT, CH1])
        wh = sb("wh", [KT, CH1], F16)
        wl = sb("wl", [KT, CH1], F16)
        wo32 = sb("wo32", [3, D])
        woh = sb("woh", [3, D], F16)
        wol = sb("wol", [3, D], F16)
        cw = sb("cw", [27, 4])
        consts = sb("consts", [2 * P + 3 * T])
        ident = consts[:, 0:P]
        later = consts[:, P:2 * P]
        upto = consts[:, 2 * P:2 * P + T]
        incl = consts[:, 2 * P + T:2 * P + 2 * T]
        offblk = consts[:, 2 * P + 2 * T:2 * P + 3 * T]
        eye16 = sb("eye16", [BLK, BLK])
        dtb = sb("dtb", [H])
        alog = sb("alog", [H])
        normw = sb("normw", [DV])
        ones = sb("ones", [1])
        mhalf = sb("mhalf", [2 * H])
        epsc = sb("epsc", [H])
        spare = sb("spare", [1])
        ba = sb("ba", [NT, 2 * H])
        beta = sb("beta", [NT, H])
        g = sb("g", [NT, H])
        s1a = sb("s1a", [NT, H])
        s1b = sb("s1b", [NT, H])
        s1c = sb("s1c", [NT, H])
        gL = sb("gL", [2, H, T])
        F = sb("F", [NT, H, T])
        acc = sb("acc", [2, 4, P])
        kq = sb("kq", [2, 2, 2, P])
        sq = sb("sq", [2, 2, 2, P])
        vT = sb("vT", [3, P])
        UP = sb("UP", [2, H, 2, P])
        Xf = sb("Xf", [H, P])
        Yn = sb("Yn", [BLK, BLK])
        Ue = sb("Ue", [BLK, BLK])
        Yt = sb("Yt", [BLK, BLK])
        n2 = sb("n2", [2, 2 * H])
        rn = sb("rn", [2, 2 * H])
        Bp = sb("Bp", [2, H])
        absk = sb("absk", [2, H])
        V = sb("V", [2, HV])
        w = sb("w", [2, HV])
        gs = sb("gs", [2, HV])
        sqo = sb("sqo", [HV])
        ms = sb("ms", [H])
        rr = sb("rr", [H])
        r2 = sb("r2", [H])
        on = sb("on", [HV])
        onh = sb("onh", [3, P], F16)
        onl = sb("onl", [3, P], F16)
        y = sb("y", [D])
        st = sb("st", [6])
        mv = sb("mv", [2])
        rs = sb("rs", [1])

        proj = [pb("proj0"), pb("proj1")]
        gram = [pb("gram0"), pb("gram1")]
        small = pb("small")
        turn = pb("turn")
        sol = [pb("sol0"), pb("sol1")]

        UD = nc.dram_tensor("ud_dram", (NBLK, H, BLK, BLK), F32, kind="Internal").ap()
        YD = nc.dram_tensor("yd_dram", (NBLK, H, BLK, BLK), F32, kind="Internal").ap()

        s_x, s_X, s_c, s_wo = sem("x_loaded"), sem("xtok_loaded"), sem("consts_loaded"), sem("wo_loaded")
        NW = 4
        wcut = [0, 24 + 512 * 1, 24 + 512 * 3, 24 + 512 * 5, CH1]
        s_w = [sem(f"w1_loaded{i}") for i in range(NW)]
        s_xh, s_xl, s_wh, s_wl = sem("xh_done"), sem("xl_done"), sem("wh_done"), sem("wl_done")
        s_ba, s_ba_ev, s_eb, s_ea, s_g = sem("ba_ready"), sem("ba_done"), sem("expb_done"), sem("expa_done"), sem("g_done")
        s_na, s_ealog = sem("na_done"), sem("expalog_done")
        s_gL, s_D, s_F, s_Fm, s_zero = sem("gL_done"), sem("decay_ready"), sem("decay_exp"), sem("decay_masked"), sem("zero_done")
        s_beta = sem("beta_done")
        dch, dtile, dback = sem("dve_setup"), sem("dve_tile"), sem("dve_back")
        pch, ptile, pback = sem("pool_setup"), sem("pool_tile"), sem("pool_back")
        proj_ready = sig("proj_ready", 7)
        gg_ready, gg_done = sig("gg_ready", 1), sig("gg_done", 1)
        tap_done, conv_done, silu_done = sig("tap_done", 7), sig("conv_done", 7), sig("silu_done", 7)
        sq_done = sig("sq_done", 6)
        gram_ready, gram_used, norm_ready = sig("gram_ready", 6), sig("gram_used", 6), sig("norm_ready", 6)
        n2_done, rn_done = sig("n2_done", 1), sig("rn_done", 1)
        vt_ready, v_done = sig("vt_ready", 1), sig("v_done", 1)
        u_scaled, u_masked = sig("u_scaled", 2), sig("u_masked", 2)
        ud_stored, ue_loaded = sig("ud_stored", 16 * NBLK), sig("ue_loaded", 16)
        y_done, yd_stored, xf_loaded = sig("y_done", 1), sig("yd_stored", 16), sig("xf_loaded", 16 * NBLK)
        sol_ready, sol_used = sig("sol_ready", 8), sig("sol_used", 7)
        sqo_done, ms_done, rr_done = sig("sqo_done", 1), sig("ms_done", 1), sig("rr_done", 1)
        gsn_done, on_done, onT_ready = sig("gsn_done", 1), sig("on_done", 1), sig("onT_ready", 1)
        onh_done, onl_done, wo_ready = sig("onh_done", 1), sig("onl_done", 1), sig("wo_ready", 1)
        mv_done, rs_done, x1_done = sig("mv_done", 1), sig("rs_done", 1), sig("x1_done", 1)

        def unit_cols(u):
            return 24 + 512 * u

        GG = 24 + 512 * NPAIR + HV

        with nc.Block() as block:
            @block.sync
            def _(sp):
                sp.dma_start(xT32[:], io["xT"].rearrange("(k p) n -> p k n", p=P)).then_inc(s_x, 16)
                w1 = io["w1"].rearrange("(k p) n -> p k n", p=P)
                for i in range(NW):
                    sp.dma_start(w32[:, :, wcut[i]:wcut[i + 1]], w1[:, :, wcut[i]:wcut[i + 1]]).then_inc(s_w[i], 16)
                    if i == 0:
                        sp.dma_start(consts[:], io["consts"]).then_inc(s_c, 16)
                        for dst, src in ((eye16[:].rearrange("p a b -> p (a b)"), "eye16"), (cw[:], "convw"), (dtb[:], "dtb"),
                                         (alog[:], "alog"), (normw[:], "normw")):
                            sp.dma_start(dst, io[src]).then_inc(s_c, 16)
                sp.dma_start(X[:], io["x"].rearrange("(t p) d -> p t d", p=P)).then_inc(s_X, 16)
                sp.dma_start(wo32[:], io["wo"].rearrange("(k p) n -> p k n", p=P)).then_inc(s_wo, 16)

                def back(t):
                    b4 = t.before()
                    waits = [(u_scaled, t, 2), (ue_loaded, b4, 16), (ud_stored, t, 16 * NBLK), (y_done, b4, 1),
                             (y_done, t, 1), (xf_loaded, b4, 16 * NBLK), (yd_stored, t, 16), (sol_ready, b4, 7)]
                    scaled, ue_read, stored, y_before, y_now, xf_before, yd_now, sol_before = (
                        (s.sem, s.count(sp, n, k)) if n.exists else None for s, n, k in waits)
                    sp.wait_ge(*scaled)
                    if b4.exists:
                        sp.wait_ge(*ue_read)
                    for b in range(NBLK):
                        c = b * BLK
                        sp.dma_start(UD[b].rearrange("h s t -> s h t"),
                                     UP[c:c + BLK, t.parity, :, 0, c:c + BLK]).then_inc(ud_stored.sem, 16)
                    sp.wait_ge(*stored)
                    if b4.exists:
                        sp.wait_ge(*y_before)
                    sp.dma_start(Ue[0:NBLK * H].rearrange("p s t -> p (s t)"),
                                 UD.rearrange("b h s t -> (b h) (s t)")).then_inc(ue_loaded.sem, 16)
                    sp.wait_ge(*y_now)
                    if b4.exists:
                        sp.wait_ge(*xf_before)
                    sp.dma_start(YD.rearrange("b h s t -> (b h) (s t)"),
                                 Yn[0:NBLK * H].rearrange("p s t -> p (s t)")).then_inc(yd_stored.sem, 16)
                    sp.wait_ge(*yd_now)
                    if b4.exists:
                        sp.wait_ge(*sol_before)
                    else:
                        sp.wait_ge(s_zero, 3)
                    for b in range(NBLK):
                        c = b * BLK
                        sp.dma_start(Xf[c:c + BLK, :, c:c + BLK],
                                     YD[b].rearrange("h s t -> s h t")).then_inc(xf_loaded.sem, 16)

                def front(t, tb):
                    if tb is not None:
                        back(tb)

                skewed_tiles(sp, front)
                ud_stored.wait(sp, Tile(NT - 1), 16 * NBLK)
                yd_stored.wait(sp, Tile(NT - 1), 16)
                xf_loaded.wait(sp, Tile(NT - 1), 16 * NBLK)

            @block.tensor
            def _(pe):
                def split_mm(out, stat_h, stat_l, mov_h, mov_l, start, stop):
                    pe.matmul(out, stat_h, mov_h, start=start, stop=False)
                    pe.matmul(out, stat_h, mov_l, start=False, stop=False)
                    return pe.matmul(out, stat_l, mov_h, start=False, stop=stop)

                pe.wait_ge(s_xh, 1)
                pe.wait_ge(s_xl, 1)
                pe.wait_ge(s_wh, 1)
                pe.wait_ge(s_wl, 1)
                for t in range(NT):
                    tok = slice(t * P, (t + 1) * P)
                    for k in range(KT):
                        mm = split_mm(proj[0][:, t * 24:t * 24 + 24], xh[:, k, tok], xl[:, k, tok],
                                      wh[:, k, 0:24], wl[:, k, 0:24], k == 0, k == KT - 1)
                mm.then_inc(s_ba, 1)
                pe.wait_ge(s_c, 16 * 6)
                for t in range(NT):
                    pe.wait_ge(s_gL, t + 1)
                    if t > 0:
                        pe.wait_ge(s_F, 2 * t)
                    for hh in range(2):
                        pe.matmul(gram[hh][:, 0:6 * T], later,
                                  gL[:, t % 2, hh * 6:hh * 6 + 6, :], start=True, stop=True).then_inc(s_D, 1)

                def project(t, u):
                    if u == 0:
                        conv_done.wait(pe, t.before(), 7)
                        if t.reg is None and t.off == 0:
                            pe.wait_ge(s_ba_ev, 1)
                    elif u == 1:
                        gg_done.wait(pe, t.before(), 1)
                    else:
                        conv_done.wait(pe, t, u - 1)
                    if t.reg is None and t.off == 0 and u in (0, 1, 3, 5):
                        n = {0: 1, 1: 2, 3: 3, 5: 4}[u]
                        pe.wait_ge(s_wh, n)
                        pe.wait_ge(s_wl, n)
                    x0 = t.value(P)
                    bank = proj[u % 2]
                    if u == 7:
                        for k in range(KT):
                            mm = split_mm(bank[:, 0:HV], xh[:, k, bass.ds(x0, P)], xl[:, k, bass.ds(x0, P)],
                                          wh[:, k, GG:GG + HV], wl[:, k, GG:GG + HV], k == 0, k == KT - 1)
                        mm.then_inc(gg_ready.sem, 1)
                        return
                    for c in range(4 if u < 6 else 3):
                        w0 = unit_cols(u) + c * P
                        for k in range(KT):
                            mm = split_mm(bank[:, c * P:(c + 1) * P], wh[:, k, w0:w0 + P], wl[:, k, w0:w0 + P],
                                          xh[:, k, bass.ds(x0, P)], xl[:, k, bass.ds(x0, P)],
                                          k == 0, k == KT - 1)
                    mm.then_inc(proj_ready.sem, 1)

                def grams(t, u):
                    silu_done.wait(pe, t, u + 1)
                    (gram_used.wait(pe, t, u - 1) if u >= 2 else gram_used.wait(pe, t.before(), 5 + u))
                    if t.reg is None and t.off == 0 and u == 0:
                        pe.wait_ge(s_F, 2 * NT)
                    for hh in range(2):
                        mm = pe.matmul(gram[u % 2][:, hh * D:(hh + 1) * D], kq[:, u % 2, hh, 0, :],
                                       kq[:, u % 2, hh, :, :].rearrange("p a n -> p (a n)"), start=True, stop=True)
                    mm.then_inc(gram_ready.sem, 1)

                def norms(t, u):
                    sq_done.wait(pe, t, u + 1)
                    if u == 0:
                        v_done.wait(pe, t.before(), 1)
                    for hh in range(2):
                        for a in range(2):
                            col = t.parity * 24 + a * H + 2 * u + hh
                            mm = pe.matmul(small[:, col:col + 1], sq[:, u % 2, hh, a, :], ones[:, 0:1],
                                           start=True, stop=True)
                    mm.then_inc(norm_ready.sem, 1)

                def v_turn(t):
                    silu_done.wait(pe, t, 7)
                    n2_done.wait(pe, t, 1)
                    for c in range(3):
                        mm = pe.transpose(small[:, T + c * P:T + (c + 1) * P], vT[:, c, :], ident)
                    mm.then_inc(vt_ready.sem, 1)

                def solve(t, k):
                    q = t.parity
                    if k == 1:
                        xf_loaded.wait(pe, t, 16 * NBLK)
                        v_done.wait(pe, t, 1)
                        x1_done.wait(pe, t.before(), 1)
                    else:
                        sol_used.wait(pe, t, k - 1)
                    if k == 2:
                        u_masked.wait(pe, t, 2)
                        on_done.wait(pe, t.before(), 1)
                    rhs = V if k == 1 else w
                    for h in range(H):
                        lhsT = Xf[:, h, :] if k % 2 else UP[:, q, h, 1 if k == 8 else 0, :]
                        r = V[:, q, h * DV:(h + 1) * DV] if k == 1 else w[:, k % 2, h * DV:(h + 1) * DV]
                        mm = pe.matmul(sol[k % 2][:, h * DV:(h + 1) * DV], lhsT, r, start=True, stop=True)
                    mm.then_inc(sol_ready.sem, 1)

                def output(t):
                    on_done.wait(pe, t, 1)
                    onl_done.wait(pe, t.before(), 1)
                    for c in range(3):
                        mm = pe.transpose(turn[:, c * P:(c + 1) * P], on[:, c * P:(c + 1) * P], ident)
                    mm.then_inc(onT_ready.sem, 1)
                    onh_done.wait(pe, t, 1)
                    onl_done.wait(pe, t, 1)
                    if t.reg is None and t.off == 0:
                        pe.wait_ge(s_wh, 5)
                        pe.wait_ge(s_wl, 5)
                    for c in range(3):
                        mm = split_mm(sol[1][:, 0:D], onh[:, c, :], onl[:, c, :], woh[:, c, :], wol[:, c, :],
                                      c == 0, c == 2)
                    mm.then_inc(wo_ready.sem, 1)

                def front(t, tb):
                    steps = {5: 1, 6: 2, 7: 3, 8: 4, 9: 5, 10: 6, 11: 7, 12: 8}

                    def between(slot):
                        if tb is not None and slot in steps:
                            solve(tb, steps[slot])

                    if t is not None:
                        project(t, 0)
                    for u in range(7):
                        if t is not None:
                            project(t, u + 1)
                        between(2 * u)
                        if t is not None:
                            if u < 6:
                                grams(t, u)
                                norms(t, u)
                            else:
                                v_turn(t)
                        between(2 * u + 1)
                    if tb is not None:
                        output(tb)

                skewed_tiles(pe, front)

            @block.scalar
            def _(act):
                act.wait_ge(s_x, 16)
                act.activation(xh[:], xT32[:], ACT.Copy).then_inc(s_xh, 1)
                for i in range(NW):
                    act.wait_ge(s_w[i], 16)
                    act.activation(wh[:, :, wcut[i]:wcut[i + 1]], w32[:, :, wcut[i]:wcut[i + 1]], ACT.Copy,
                                   scale=WS).then_inc(s_wh, 1)
                    if i == 0:
                        act.wait_ge(s_c, 16 * 6)
                        act.activation(s1c[:, 0, :], alog[:], ACT.Exp).then_inc(s_ealog, 1)
                        act.wait_ge(s_na, 1)
                        act.activation(s1a[:], s1a[:], ACT.Exp).then_inc(s_ea, 1)
                        act.wait_ge(s_ba_ev, 1)
                        act.activation(beta[:], ba[:, :, 0:H], ACT.Exp, scale=-1.0).then_inc(s_eb, 1)
                act.wait_ge(s_wo, 16)
                act.activation(woh[:], wo32[:], ACT.Copy, scale=WS).then_inc(s_wh, 1)
                for t in range(NT):
                    for hh in range(2):
                        act.wait_ge(s_D, 2 * t + hh + 1)
                        act.activation(F[:, t, hh * 6:hh * 6 + 6, :].rearrange("p h t -> p (h t)"),
                                       gram[hh][:, 0:6 * T], ACT.Exp).then_inc(s_F, 1)

                def tap0(t, u):
                    proj_ready.wait(act, t, u + 1)
                    for c in range(4 if u < 6 else 3):
                        i = act.activation(acc[:, u % 2, c, :], proj[u % 2][:, c * P:(c + 1) * P], ACT.Copy,
                                           scale=cw[:, 4 * u + c, 3:4])
                    i.then_inc(tap_done.sem, 1)

                def silu(t, u):
                    conv_done.wait(act, t, u + 1)
                    if u < 6:
                        (gram_ready.wait(act, t, u - 1) if u >= 2 else gram_ready.wait(act, t.before(), 5 + u))
                        (sq_done.wait(act, t, u - 1) if u >= 2 else sq_done.wait(act, t.before(), 5 + u))
                        act.activation(kq[:, u % 2].rearrange("p a b n -> p (a b n)"),
                                       acc[:, u % 2].rearrange("p c n -> p (c n)"), ACT.Silu,
                                       scale=1 / WS).then_inc(silu_done.sem, 1)
                    else:
                        vt_ready.wait(act, t.before(), 1)
                        act.activation(vT[:], acc[:, u % 2, 0:3, :], ACT.Silu, scale=1 / WS).then_inc(silu_done.sem, 1)

                def gate(t):
                    gg_ready.wait(act, t, 1)
                    on_done.wait(act, t.before(2), 1)
                    act.activation(gs[:, t.parity, :], proj[1][:, 0:HV], ACT.Silu, scale=1 / WS).then_inc(gg_done.sem, 1)

                def front(t, tb):
                    if t is not None:
                        tap0(t, 0)
                        for u in range(7):
                            if u < 6:
                                tap0(t, u + 1)
                            else:
                                gate(t)
                            silu(t, u)
                    if tb is not None:
                        sol_ready.wait(act, tb, 8)
                        act.activation(sqo[:], sol[0][:, 0:HV], ACT.Square,
                                       scale=DV ** -0.5).then_inc(sqo_done.sem, 1)
                        onT_ready.wait(act, tb, 1)
                        wo_ready.wait(act, tb.before(), 1)
                        act.activation(onh[:].rearrange("p c n -> p (c n)"), turn[:, 0:HV], ACT.Copy).then_inc(onh_done.sem, 1)

                skewed_tiles(act, front)

            @block.gpsimd
            def _(pool):
                ch = Chain(pool, pch)
                pool.memset(ones[:], 1.0)
                pool.memset(epsc[:], EPS)
                ch(pool.memset(mhalf[:], -0.5))
                pool.memset(UP[:, 0], 0.0).then_inc(s_zero, 1)
                pool.memset(UP[:, 1], 0.0).then_inc(s_zero, 1)
                pool.memset(Xf[:], 0.0).then_inc(s_zero, 1)
                pool.wait_ge(s_c, 16 * 6)
                for t in range(NT):
                    pool.wait_ge(s_g, 1)
                    if t >= 2:
                        pool.wait_ge(s_D, 2 * t - 2)
                    pool.tensor_tensor(gL[:, t % 2], over(g[:, t, :], 2, [P, H, T]), over(upto, 1, [P, H, T]),
                                       ALU.mult).then_inc(s_gL, 1)
                    if t > 0:
                        pool.wait_ge(s_F, 2 * t)
                        pool.tensor_tensor(F[:, t - 1], F[:, t - 1], over(incl, 1, [P, H, T]), ALU.mult).then_inc(s_Fm, 1)
                pool.wait_ge(s_F, 2 * NT)
                pool.tensor_tensor(F[:, NT - 1], F[:, NT - 1], over(incl, 1, [P, H, T]), ALU.mult).then_inc(s_Fm, 1)
                fc, bc = TileChain(pool, ptile), TileChain(pool, pback)

                def front(t, tb):
                    if tb is not None:
                        bc.start(tb)
                        q = tb.parity
                        gram_used.wait(pool, tb, 6)
                        rn_done.wait(pool, tb, 1)
                        rs_done.wait(pool, tb.before(), 1)
                        for b in range(2):
                            r = slice(b * T, (b + 1) * T)
                            pool.tensor_tensor(UP[r, q, :, 0, r], UP[r, q, :, 0, r],
                                               over(Bp[r, q, :], 2, [T, H, T]), ALU.mult).then_inc(u_scaled.sem, 1)
                        u_scaled.wait(pool, tb, 2)
                    if t is not None:
                        for u in range(6):
                            silu_done.wait(pool, t, u + 1)
                            (norm_ready.wait(pool, t, u - 1) if u >= 2 else norm_ready.wait(pool, t.before(), 5 + u))
                            src = kq[:, u % 2].rearrange("p a b n -> p (a b n)")
                            pool.tensor_tensor(sq[:, u % 2].rearrange("p a b n -> p (a b n)"), src, src,
                                               ALU.mult).then_inc(sq_done.sem, 1)
                            if u == 0 and tb is not None:
                                sq_done.wait(pool, t, 1)
                                mask_u(tb)
                            if u == 2 and tb is not None:
                                gate_w(tb)
                    elif tb is not None:
                        mask_u(tb)
                        gate_w(tb)
                    if t is not None:
                        fc.start(t)
                        q = t.parity
                        n2_done.wait(pool, t, 1)
                        fc(pool.tensor_tensor(rn[:, q], n2[:, q], mhalf[:], ALU.pow))
                        fc.mark(pool.tensor_tensor(absk[:, q], n2[:, q, 0:H], rn[:, q, 0:H], ALU.mult))
                        fc(pool.tensor_tensor(Bp[:, q], rn[:, q, 0:H], rn[:, q, 0:H], ALU.mult))
                        pool.tensor_tensor(Bp[:, q], Bp[:, q], beta[:, bass.ds(t.value(1), 1), :].rearrange("p a h -> p (a h)"),
                                           ALU.mult).then_inc(rn_done.sem, 1)
                    if tb is not None:
                        q = tb.parity
                        ms_done.wait(pool, tb, 1)
                        bc(pool.tensor_tensor(r2[:], rn[:, q, H:], rn[:, q, H:], ALU.mult))
                        bc(pool.tensor_tensor(r2[:], r2[:], ms[:], ALU.mult))
                        bc(pool.tensor_tensor(r2[:], r2[:], epsc[:], ALU.add))
                        bc(pool.tensor_tensor(r2[:], r2[:], mhalf[:, 0:H], ALU.pow))
                        pool.tensor_tensor(rr[:], r2[:], rn[:, q, H:], ALU.mult).then_inc(rr_done.sem, 1)
                        mv_done.wait(pool, tb, 1)
                        bc(pool.tensor_tensor(rs[:], mv[:, 1:2], epsc[:, 0:1], ALU.add))
                        pool.tensor_tensor(rs[:], rs[:], mhalf[:, 0:1], ALU.pow).then_inc(rs_done.sem, 1)

                def mask_u(tb):
                    ud_stored.wait(pool, tb, 16 * NBLK)
                    for b in range(2):
                        r = slice(b * T, (b + 1) * T)
                        pool.tensor_tensor(UP[r, tb.parity, :, 0, r], UP[r, tb.parity, :, 0, r],
                                           over(offblk[r, :], 1, [T, H, T]), ALU.mult).then_inc(u_masked.sem, 1)
                    u_masked.wait(pool, tb, 2)

                def gate_w(tb):
                    gg_done.wait(pool, tb, 1)
                    v = gs[:, tb.parity].rearrange("p (h d) -> p h d", h=H)
                    pool.tensor_tensor(v, v, over(normw[:], 1, [P, H, DV]), ALU.mult).then_inc(gsn_done.sem, 1)

                skewed_tiles(pool, front)

            @block.vector
            def _(v):
                ch = Chain(v, dch)
                v.wait_ge(s_xh, 1)
                v.tensor_tensor(xl[:], xT32[:], xh[:], ALU.subtract).then_inc(s_xl, 1)

                def w_low(i):
                    v.wait_ge(s_wh, i + 1)
                    c = slice(wcut[i], wcut[i + 1])
                    v.scalar_tensor_tensor(wl[:, :, c], w32[:, :, c], WS, wh[:, :, c], ALU.mult,
                                           ALU.subtract).then_inc(s_wl, 1)

                w_low(0)
                v.wait_ge(s_c, 16 * 6)
                v.wait_ge(s_ba, 1)
                v.tensor_scalar(ba[:].rearrange("p t h -> p (t h)"), proj[0][:, 0:NT * 24], 1 / WS, None,
                                ALU.mult).then_inc(s_ba_ev, 1)
                v.wait_ge(s_ba_ev, 1)
                a = ba[:, :, H:2 * H]
                ch(v.tensor_tensor(a, a, over(dtb[:], 1, [P, NT, H]), ALU.add))
                ch(v.tensor_scalar(s1b[:], a, -1.0, None, ALU.mult))
                v.tensor_tensor(s1a[:], a, s1b[:], ALU.min).then_inc(s_na, 1)
                ch(v.tensor_scalar(g[:], a, 0.0, None, ALU.max))
                v.wait_ge(s_ea, 1)
                ch(v.tensor_scalar(s1b[:], s1a[:], 2.0, None, ALU.add))
                ch(v.reciprocal(s1b[:], s1b[:]))
                ch(v.tensor_tensor(s1a[:], s1a[:], s1b[:], ALU.mult))
                ch(v.tensor_tensor(s1b[:], s1a[:], s1a[:], ALU.mult))
                v.wait_ge(s_ealog, 1)
                ch(v.tensor_scalar(alog[:], s1c[:, 0, :], -1.0, None, ALU.mult))
                ch(v.tensor_scalar(s1c[:], s1b[:], 1 / 17.0, None, ALU.mult))
                for n in (15, 13, 11, 9, 7, 5, 3):
                    ch(v.scalar_tensor_tensor(s1c[:], s1c[:], 1.0 / n, s1b[:], ALU.add, ALU.mult))
                ch(v.scalar_tensor_tensor(s1c[:], s1c[:], 1.0, s1a[:], ALU.add, ALU.mult))
                ch(v.scalar_tensor_tensor(g[:], s1c[:], 2.0, g[:], ALU.mult, ALU.add))
                v.tensor_tensor(g[:], g[:], over(alog[:], 1, [P, NT, H]), ALU.mult).then_inc(s_g, 1)
                v.wait_ge(s_eb, 1)
                ch(v.tensor_scalar(beta[:], beta[:], 1.0, None, ALU.add))
                v.reciprocal(beta[:], beta[:]).then_inc(s_beta, 1)
                for i in range(1, NW):
                    w_low(i)
                v.wait_ge(s_wh, 5)
                v.scalar_tensor_tensor(wol[:], wo32[:], WS, woh[:], ALU.mult, ALU.subtract).then_inc(s_wl, 1)
                v.wait_ge(s_Fm, NT)
                v.wait_ge(s_zero, 3)
                v.wait_ge(s_X, 16)
                v.wait_ge(s_beta, 1)

                cc, bc = TileChain(v, dtile), TileChain(v, dback)
                YP = NBLK * H

                def conv(t, u):
                    tap_done.wait(v, t, u + 1)
                    n = 4 if u < 6 else 3
                    marks = [0] * n
                    for tap in range(1, 4):
                        for c in range(n):
                            if tap > 1:
                                cc.wait(marks[c])
                            src = proj[u % 2][:, c * P:(c + 1) * P].rearrange("p (b t) -> p b t", b=2)[:, :, 0:T - tap]
                            dst = acc[:, u % 2, c, :].rearrange("p (b t) -> p b t", b=2)[:, :, tap:T]
                            i = v.scalar_tensor_tensor(dst, src, cw[:, 4 * u + c, 3 - tap:4 - tap], dst, ALU.mult, ALU.add)
                            if tap < 3:
                                marks[c] = cc.mark(i)
                    i.then_inc(conv_done.sem, 1)

                def gram_use(t, u):
                    gram_ready.wait(v, t, u + 1)
                    q = t.parity
                    if u == 0:
                        sol_ready.wait(v, t.before(2), 8)
                    for b in range(2):
                        r = slice(b * T, (b + 1) * T)
                        for a in range(2):
                            src = gram[u % 2][r, :].rearrange("p (h a n) -> p h a n", h=2, a=2)[:, :, a, r]
                            i = v.tensor_tensor(UP[r, q, 2 * u:2 * u + 2, a, r], src,
                                                F[r, bass.ds(t.value(1), 1), 2 * u:2 * u + 2, :].rearrange("p a h t -> p (a h) t"),
                                                ALU.mult)
                    i.then_inc(gram_used.sem, 1)

                def norms_out(t):
                    norm_ready.wait(v, t, 6)
                    q = t.parity
                    v.tensor_scalar(n2[:, q], small[:, q * 24:q * 24 + 24], 1e-6, None, ALU.add).then_inc(n2_done.sem, 1)

                def v_scale(t):
                    vt_ready.wait(v, t, 1)
                    rn_done.wait(v, t, 1)
                    q = t.parity
                    v.tensor_tensor(V[:, q].rearrange("p (h d) -> p h d", h=H),
                                    small[:, T:T + HV].rearrange("p (h d) -> p h d", h=H),
                                    over(absk[:, q], 2, [P, H, DV]), ALU.mult).then_inc(v_done.sem, 1)

                def eliminate(t, s0, s1):
                    if s0 == 0:
                        ue_loaded.wait(v, t, 16)
                        yd_stored.wait(v, t.before(), 16)
                        bc(v.tensor_copy(Yn[0:YP], eye16[0:YP]))
                    for s in range(s0, s1):
                        n, m = s + 1, BLK - 1 - s
                        bc(v.tensor_tensor(Yt[0:YP, 0:n, 0:m], Yn[0:YP, 0:n, s:s + 1].broadcast_to([YP, n, m]),
                                           Ue[0:YP, s:s + 1, s + 1:].broadcast_to([YP, n, m]), ALU.mult))
                        i = v.tensor_tensor(Yn[0:YP, 0:n, s + 1:], Yn[0:YP, 0:n, s + 1:], Yt[0:YP, 0:n, 0:m], ALU.subtract)
                        if s == BLK - 2:
                            i.then_inc(y_done.sem, 1)
                        else:
                            bc(i)

                def sol_use(t, k):
                    sol_ready.wait(v, t, k)
                    q = t.parity
                    src, dst = sol[k % 2][:, 0:HV], w[:, (k + 1) % 2]
                    if k == 7:
                        i = v.tensor_tensor(dst.rearrange("p (h d) -> p h d", h=H), src.rearrange("p (h d) -> p h d", h=H),
                                            over(Bp[:, q], 2, [P, H, DV]), ALU.mult)
                    elif k % 2:
                        i = v.tensor_copy(dst, src)
                    else:
                        i = v.tensor_tensor(dst, V[:, q], src, ALU.subtract)
                    i.then_inc(sol_used.sem, 1)

                def finish(t):
                    q = t.parity
                    sqo_done.wait(v, t, 1)
                    v.tensor_reduce(ms[:], sqo[:].rearrange("p (h d) -> p h d", h=H), AX.X, ALU.add).then_inc(ms_done.sem, 1)
                    rr_done.wait(v, t, 1)
                    onT_ready.wait(v, t.before(), 1)
                    bc(v.tensor_tensor(on[:].rearrange("p (h d) -> p h d", h=H),
                                       sol[0][:, 0:HV].rearrange("p (h d) -> p h d", h=H),
                                       over(rr[:], 2, [P, H, DV]), ALU.mult))
                    gsn_done.wait(v, t, 1)
                    v.tensor_tensor(on[:], on[:], gs[:, q], ALU.mult).then_inc(on_done.sem, 1)
                    onh_done.wait(v, t, 1)
                    wo_ready.wait(v, t.before(), 1)
                    v.tensor_tensor(onl[:].rearrange("p c n -> p (c n)"), turn[:, 0:HV],
                                    onh[:].rearrange("p c n -> p (c n)"), ALU.subtract).then_inc(onl_done.sem, 1)
                    wo_ready.wait(v, t, 1)
                    xt = X[:, bass.ds(t.value(1), 1), :].rearrange("p a d -> p (a d)")
                    bc(v.scalar_tensor_tensor(y[:], sol[1][:, 0:D], 1 / WS, xt, ALU.mult, ALU.add))
                    bc(v.bn_stats(st[:], y[:]))
                    v.memset(spare[:], 0.0)
                    v.bn_aggr(mv[:], st[:]).then_inc(mv_done.sem, 1)
                    rs_done.wait(v, t, 1)
                    v.tensor_scalar(xt, y[:], mv[:, 0:1], rs[:, 0:1], ALU.subtract, ALU.mult).then_inc(x1_done.sem, 1)

                def front(t, tb):
                    elim = {1: (0, 5), 2: (5, 10), 3: (10, 15)}
                    sols = {6: 1, 7: 2, 8: 3, 9: 4, 10: 5, 11: 6, 12: 7}
                    if t is not None:
                        cc.start(t)
                    if tb is not None:
                        bc.start(tb)

                    def between(slot):
                        if tb is not None:
                            if slot in elim:
                                eliminate(tb, *elim[slot])
                            if slot in sols:
                                sol_use(tb, sols[slot])

                    if t is not None:
                        conv(t, 0)
                    for u in range(7):
                        if t is not None and u < 6:
                            conv(t, u + 1)
                        between(2 * u)
                        if t is not None and u < 6:
                            gram_use(t, u)
                            if u == 5:
                                norms_out(t)
                        between(2 * u + 1)
                    if t is not None:
                        v_scale(t)
                    if tb is not None:
                        finish(tb)

                skewed_tiles(v, front)


G = 8
UN = 4
NH2 = 32
CH2 = 4 * 512
F8MAX = 448.0
QSCALE = P ** -0.5


def skewed_units(eng, ahead, unit):
    ahead(Tile(0))
    for u in range(UN):
        unit(Tile(u), Tile(u + 1), Tile(0))
    with eng.Fori(0, NT - 2) as i:
        for u in range(UN):
            unit(Tile(UN + u, i, UN), Tile(UN + u + 1, i, UN), Tile(1, i, 1))
    for u in range(UN):
        n = UN * (NT - 1) + u
        unit(Tile(n), Tile(n + 1) if u < UN - 1 else None, Tile(NT - 1))


def stage2(nc, io, X):
    with ExitStack() as ctx:
        def sb(name, shape, dt=F32):
            return ctx.enter_context(nc.sbuf_tensor(name, [P] + shape, dt))

        def pb(name):
            return ctx.enter_context(nc.psum_tensor(name, [P, 512], F32))

        def sem(name):
            return ctx.enter_context(nc.semaphore(name))

        def sig(name, per):
            return Signal(sem(name), per)

        NSLOT = 4
        raw = sb("raw", [NSLOT, KT, 512])
        w2h = sb("w2h", [UN, 4, KT, 512], F16)
        w2l = sb("w2l", [UN, 4, KT, 512], F16)
        wp = sb("wp", [NH2, D], F16)
        ch_ = sb("ctxh", [KT, NTOK], F16)
        cl_ = sb("ctxl", [KT, NTOK], F16)
        wmean = sb("wmean", [NSLOT, 8])
        ident = sb("ident2", [P])
        prm = sb("prm", [12 + 8 + 6 + 32])
        lnw, lnb = prm[:, 0:2], prm[:, 2:4]
        insc = prm[:, 4:12]
        lnp = prm[:, 12:20]
        wsc = prm[:, 20:26]
        smooth = prm[:, 26:58]
        rinsc = sb("rinsc", [8])
        rsm = sb("rsm", [NH2])
        pscale = sb("pscale", [1])
        epsw = sb("epsw", [4])
        mhalf = sb("mhalf2", [4])
        xn = sb("xn", [2, D])
        lnT = sb("lnT", [2, KT, P])
        xq = sb("xq", [NT, 4, KT, P], BF16)
        mag = sb("mag", [2, 8, P], BF16)
        st = sb("st2", [2, 6])
        mv = sb("mv2", [2, 2])
        rs = sb("rs2", [2, 1])
        spare = sb("spare2", [1])
        sq = sb("sq2", [3, 512])
        qn = sb("qn", [3, 512])
        ms = sb("ms2", [3, 4])
        rq = sb("rq", [3, 4])
        qT = sb("qT", [2, 4, 2, 2, T])
        kT = sb("kT", [2, 4, P])
        V = sb("V2", [2, 512])
        mx = sb("mx", [8])
        sc = sb("sc", [2, 512])
        sm = sb("sm", [8])
        rc = sb("rc", [8])
        PT = sb("PT", [512])
        cat = sb("cat", [NH2, P], BF16)
        cmag = sb("cmag", [8, P], BF16)
        y = sb("y2", [D])

        pj = [pb("pjA"), pb("pjB"), pb("pjC")]
        tq, scb, ptb = pb("tq"), pb("scb"), pb("ptb")
        pv = [pb("pv0"), pb("pv1")]

        s_prm, s_id = sem("prm_loaded"), sem("ident_loaded")
        NCH = UN * 4 + 2 + 8
        s_raw = [sem(f"raw_loaded{i}") for i in range(NSLOT)]
        s_scaled, s_centered, s_hi, s_lo = sem("w_scaled"), sem("w_centered"), sem("w_hi"), sem("w_lo")
        s_mean = sem("w_mean")
        s_c2 = sem("const2_done")
        s_mv, s_rs, s_xn, s_xT, s_xq = sem("pre_mv"), sem("pre_rs"), sem("pre_xn"), sem("pre_xT"), sem("pre_xq")
        s_ln = sem("pre_ln")
        dch, pch = sem("dve_setup2"), sem("pool_setup2")
        dun, pun, dti, pti = sem("dve_unit"), sem("pool_unit"), sem("dve_tile2"), sem("pool_tile2")
        q_ready, v_ready = sig("q_ready", 3), sig("v_ready", 1)
        sq_done, ms_done, rq_done, qn_done = sig("sq2_done", 3), sig("ms2_done", 3), sig("rq_done", 3), sig("qn_done", 3)
        tq_ready, tq_used, v_used = sig("tq_ready", 3), sig("tq_used", 3), sig("v_used", 1)
        sc_ready, sub_done, exp_done, p_done = sig("sc_ready", 1), sig("sub_done", 1), sig("exp_done", 1), sig("p_done", 1)
        rc_done = sig("rc_done", 1)
        pt_ready, pt_used, pv_ready, y_done, cat_done = (sig("pt_ready", 1), sig("pt_used", 1), sig("pv_ready", 1),
                                                         sig("y2_done", 1), sig("cat_done", 1))
        wp_ready, mv_done, rs_done, x2_done, yt_done = (sig("wp_ready", 1), sig("mv2_done", 1), sig("rs2_done", 1),
                                                        sig("x2_done", 1), sig("yt_done", 1))

        def is_self(u):
            return u < UN // 2

        order = [("w", u, c) for u in range(2) for c in range(4)] + [("ctx", k, 0) for k in range(2)] + \
                [("w", u, c) for u in range(2, 4) for c in range(4)] + [("wp", k, 0) for k in range(8)]
        done_before = {}
        for n, key in enumerate(order):
            done_before[key] = n + 1

        with nc.Block() as block:
            @block.sync
            def _(sp):
                sp.dma_start(prm[:], io["prm2"]).then_inc(s_prm, 16)
                sp.dma_start(ident[:], io["consts"][:, 0:P]).then_inc(s_id, 16)
                w2 = io["w2"].rearrange("(k p) n -> p k n", p=P)
                cx = io["ctxT"].rearrange("(k p) n -> p k n", p=P)
                wpv = io["wproj"].rearrange("(n p) c -> p n c", p=P)
                for n, (what, a, b) in enumerate(order):
                    if n >= NSLOT:
                        last = order[n - NSLOT][0]
                        sp.wait_ge(s_hi if last == "wp" else s_lo, n - NSLOT + 1)
                    slot = raw[:, n % NSLOT]
                    if what == "w":
                        src = w2[:, :, a * CH2 + b * 512:a * CH2 + (b + 1) * 512]
                    elif what == "ctx":
                        src = cx[:, :, a * 512:(a + 1) * 512]
                    else:
                        src = wpv[:, a * 4:(a + 1) * 4, :]
                        slot = slot.rearrange("p k n -> p (k n)").rearrange("p (n c) -> p n c", c=D)
                    sp.dma_start(slot, src).then_inc(s_raw[n % NSLOT], 16)

            def raw_here(eng, n):
                eng.wait_ge(s_raw[n % NSLOT], 16 * (n // NSLOT + 1))

            def centered(what, c):
                return what == "w" and c < 3

            @block.tensor
            def _(pe):
                pe.wait_ge(s_id, 16)
                for t in range(NT):
                    pe.wait_ge(s_xn, t + 1)
                    if t >= 2:
                        pe.wait_ge(s_ln, t - 1)
                    for k in range(KT):
                        i = pe.transpose(pj[t % 2][:, k * P:(k + 1) * P], xn[:, t % 2, k * P:(k + 1) * P], ident[:])
                    i.then_inc(s_xT, 1)

                def chunk(n, c):
                    u = n.off % UN
                    if c == 0:
                        v_used.wait(pe, n.before(), 1)
                    elif c == 3:
                        qn_done.wait(pe, n, 1)
                    else:
                        qn_done.wait(pe, n.before(), c + 1)
                    if n.reg is None and n.off < UN:
                        pe.wait_ge(s_lo, done_before[("w", u, c)])
                        if n.off == 0 and c == 0:
                            pe.wait_ge(s_xq, NT)
                    tile = tile_of(n)
                    if is_self(u):
                        s = (0, 0, 2, 3)[c]
                        terms = [(xq[:, bass.ds(tile, 1), s, k, :].rearrange("p a n -> p (a n)"), w[:, u, c, k, :])
                                 for k in range(KT) for w in (w2h, w2l)]
                    elif c < 2:
                        terms = [(xq[:, bass.ds(tile, 1), 1, k, :].rearrange("p a n -> p (a n)"), w[:, u, c, k, :])
                                 for k in range(KT) for w in (w2h, w2l)]
                    else:
                        tok = bass.ds(tile * P, P)
                        terms = [(x, w) for k in range(KT) for x, w in (
                            (ch_[:, k, tok], w2h[:, u, c, k, :]), (ch_[:, k, tok], w2l[:, u, c, k, :]),
                            (cl_[:, k, tok], w2h[:, u, c, k, :]))]
                    for j, (x, w) in enumerate(terms):
                        i = pe.matmul(pj[c % 3][:], x, w, start=j == 0, stop=j == len(terms) - 1)
                    i.then_inc((v_ready if c == 3 else q_ready).sem, 1)

                def tile_of(n):
                    return n.off // UN if n.reg is None else n.reg + n.off // UN

                def turn(n, c):
                    qn_done.wait(pe, n, c + 1)
                    (tq_used.wait(pe, n, c) if c else tq_used.wait(pe, n.before(), 3))
                    for j in range(4):
                        dst = tq[:, j * P:(j + 1) * P]
                        if c < 2:
                            dst = tq[:, j // 2 * D:(j // 2 + 1) * D].rearrange("p (b h s) -> p h b s", b=2, h=2)[:, j % 2]
                        i = pe.transpose(dst, qn[:, c, j * P:(j + 1) * P], ident[:])
                    i.then_inc(tq_ready.sem, 1)

                def scores(n):
                    tq_used.wait(pe, n, 3)
                    sub_done.wait(pe, n.before(), 1)
                    q = n.parity
                    for g in range(4):
                        for b in range(2):
                            s = slice(b * T, (b + 1) * T)
                            i = pe.matmul(scb[:, g * P + b * T:g * P + (b + 1) * T], qT[:, q, g, b].rearrange("p h s -> p (h s)"),
                                          kT[:, q, g, s], start=True, stop=True)
                    i.then_inc(sc_ready.sem, 1)

                def turn_p(n, t):
                    p_done.wait(pe, n, 1)
                    pt_used.wait(pe, n.before(), 1)
                    if n.off % UN == 0:
                        yt_done.wait(pe, t.before(), 1)
                    for g in range(4):
                        i = pe.transpose(ptb[:, g * P:(g + 1) * P], sc[:, n.parity, g * P:(g + 1) * P], ident[:])
                    i.then_inc(pt_ready.sem, 1)

                def values(n):
                    pt_used.wait(pe, n, 1)
                    v_used.wait(pe, n, 1)
                    y_done.wait(pe, n.before(), 1)
                    for g in range(4):
                        for b in range(2):
                            r = slice(b * T, (b + 1) * T)
                            i = pe.matmul(pv[b][:, g * P:(g + 1) * P], V[r, n.parity, g * P:(g + 1) * P],
                                          PT[r, g * P:(g + 1) * P], start=True, stop=True)
                    i.then_inc(pv_ready.sem, 1)

                def project(n, t):
                    cat_done.wait(pe, n, 1)
                    if t.reg is None and t.off == 0:
                        pe.wait_ge(s_hi, NCH)
                    for h in range(NH2):
                        i = pe.matmul(ptb[:, 0:D], cat[:, h, :], wp[:, h, :], start=h == 0, stop=h == NH2 - 1)
                    i.then_inc(wp_ready.sem, 1)

                def ahead(n):
                    for c in range(4):
                        chunk(n, c)
                    for c in range(3):
                        turn(n, c)

                def unit(n, m, t):
                    scores(n)
                    if m is not None:
                        chunk(m, 0)
                        chunk(m, 1)
                        turn(m, 0)
                    turn_p(n, t)
                    if m is not None:
                        chunk(m, 2)
                        turn(m, 1)
                        chunk(m, 3)
                    values(n)
                    if m is not None:
                        turn(m, 2)
                    if n.off % UN == UN - 1:
                        project(n, t)

                skewed_units(pe, ahead, unit)

            @block.scalar
            def _(act):
                act.wait_ge(s_prm, 16)
                nsc = 0
                for n, (what, a, b) in enumerate(order):
                    raw_here(act, n)
                    slot = raw[:, n % NSLOT]
                    if what == "w" and (is_self(a) or b < 2):
                        s = (1 if not is_self(a) else 0, 1 if not is_self(a) else 0, 2, 3)[b]
                        for k in range(KT):
                            i = act.activation(slot[:, k, :], slot[:, k, :], ACT.Copy, scale=insc[:, 2 * s + k:2 * s + k + 1])
                        i.then_inc(s_scaled, 1)
                        act.wait_ge(s_scaled, n_scaled(order, n))
                    if centered(what, b):
                        act.wait_ge(s_centered, n_centered(order, n))
                    k = WS if what == "w" and not is_self(a) and b >= 2 else 1.0
                    if what == "w":
                        dst = w2h[:, a, b]
                    elif what == "ctx":
                        dst = ch_[:, :, a * 512:(a + 1) * 512]
                    else:
                        dst = wp[:, a * 4:(a + 1) * 4, :].rearrange("p n c -> p (n c)")
                        slot = slot.rearrange("p k n -> p (k n)")
                    act.activation(dst, slot, ACT.Copy, scale=k).then_inc(s_hi, 1)

                def square(n, c):
                    q_ready.wait(act, n, c + 1)
                    ms_done.wait(act, n.before(), c + 1)
                    act.activation(sq[:, c], pj[c][:], ACT.Square, scale=P ** -0.5).then_inc(sq_done.sem, 1)

                def affine(n, c):
                    tq_ready.wait(act, n, c + 1)
                    if c == 0:
                        sc_ready.wait(act, n.before(2), 1)
                    j = (0 if is_self(n.off % UN) else 1) + (2 if c == 2 else 0)
                    if c == 2:
                        dst = kT[:, n.parity].rearrange("p g n -> p (g n)")
                    else:
                        dst = qT[:, n.parity, 2 * c:2 * c + 2].rearrange("p g b h s -> p (g b h s)")
                    act.activation(dst, tq[:], ACT.Identity, bias=lnp[:, 2 * j + 1:2 * j + 2],
                                   scale=lnp[:, 2 * j:2 * j + 1]).then_inc(tq_used.sem, 1)

                def copy_v(n):
                    v_ready.wait(act, n, 1)
                    pv_ready.wait(act, n.before(2), 1)
                    act.activation(V[:, n.parity], pj[0][:], ACT.Copy).then_inc(v_used.sem, 1)

                def ahead(n):
                    for c in range(3):
                        square(n, c)
                    copy_v(n)
                    for c in range(3):
                        affine(n, c)

                def unit(n, m, t):
                    if m is not None:
                        square(m, 0)
                    sub_done.wait(act, n, 1)
                    act.activation(sc[:, n.parity], sc[:, n.parity], ACT.Exp, scale=QSCALE).then_inc(exp_done.sem, 1)
                    if m is not None:
                        square(m, 1)
                        affine(m, 0)
                    pt_ready.wait(act, n, 1)
                    pv_ready.wait(act, n.before(), 1)
                    act.activation(PT[:], ptb[:], ACT.Copy).then_inc(pt_used.sem, 1)
                    if m is not None:
                        square(m, 2)
                        affine(m, 1)
                        copy_v(m)
                        affine(m, 2)

                skewed_units(act, ahead, unit)

            @block.gpsimd
            def _(pool):
                ch = Chain(pool, pch)
                ch(pool.memset(mhalf[:], -0.5))
                pool.wait_ge(s_c2, 1)
                for t in range(NT):
                    pool.wait_ge(s_mv, t + 1)
                    ch(pool.tensor_scalar(rs[:, t % 2], mv[:, t % 2, 1:2], EPS, 1.0, ALU.add, ALU.mult))
                    pool.tensor_tensor(rs[:, t % 2], rs[:, t % 2], mhalf[:, 0:1], ALU.pow).then_inc(s_rs, 1)
                pc = TileChain(pool, pun)

                def inv_dev(n, c):
                    ms_done.wait(pool, n, c + 1)
                    j = (0 if is_self(n.off % UN) else 1) + (2 if c == 2 else 0)
                    pc(pool.tensor_tensor(rq[:, c], ms[:, c], epsw[:, j:j + 1].broadcast_to([P, 4]), ALU.add))
                    pool.tensor_tensor(rq[:, c], rq[:, c], mhalf[:], ALU.pow).then_inc(rq_done.sem, 1)

                def ahead(n):
                    pc.start(n)
                    for c in range(3):
                        inv_dev(n, c)

                tc = TileChain(pool, pti)

                def unit(n, m, t):
                    if m is not None:
                        pc.start(m)
                        inv_dev(m, 0)
                        inv_dev(m, 1)
                    rc_done.wait(pool, n, 1)
                    v = sc[:, n.parity].rearrange("p (g t) -> p g t", t=T)
                    pool.tensor_tensor(v, v, over(rc[:], 2, [P, 8, T]), ALU.mult).then_inc(p_done.sem, 1)
                    if m is not None:
                        inv_dev(m, 2)
                    if n.off % UN == UN - 1:
                        tc.start(t)
                        mv_done.wait(pool, t, 1)
                        tc(pool.tensor_tensor(rs[:, 0], mv[:, 0, 1:2], spare[:], ALU.add))
                        pool.tensor_tensor(rs[:, 0], rs[:, 0], mhalf[:, 0:1], ALU.pow).then_inc(rs_done.sem, 1)

                skewed_units(pool, ahead, unit)

            @block.vector
            def _(v):
                ch = Chain(v, dch)
                v.wait_ge(s_prm, 16)
                v.memset(spare[:], EPS)
                v.reciprocal(rinsc[:], insc)
                v.tensor_tensor(pscale[:], wsc[:, 4:5], wsc[:, 5:6], ALU.mult)
                ch(v.reciprocal(rsm[:], smooth))
                v.tensor_scalar(rsm[:, 16:], rsm[:, 16:], 1 / WS, None, ALU.mult)
                v.tensor_scalar(rsm[:, 0:16], rsm[:, 0:16], wsc[:, 3:4], None, ALU.mult)
                ch(v.tensor_tensor(epsw[:, 0:3], wsc[:, 0:3], wsc[:, 0:3], ALU.mult))
                ch(v.reciprocal(epsw[:, 0:3], epsw[:, 0:3]))
                ch(v.tensor_scalar(epsw[:, 0:3], epsw[:, 0:3], EPS, None, ALU.mult))
                v.memset(epsw[:, 3:4], EPS * WS * WS).then_inc(s_c2, 1)

                def quantise(yv, mg, last):
                    ch2 = last["chain"]
                    ch2(v.tensor_scalar(yv, yv, F8MAX, -F8MAX, ALU.min, ALU.max))
                    ch2(v.tensor_scalar(mg.bitcast(U16), yv.bitcast(U16), 0x7F80, None, ALU.bitwise_and))
                    ch2(v.tensor_scalar(mg, mg, 2.0 ** -6, 24.0, ALU.max, ALU.mult))
                    ch2(v.tensor_tensor(yv, yv, mg, ALU.add))
                    v.tensor_tensor(yv, yv, mg, ALU.subtract).then_inc(last["sem"], 1)

                def stats(t):
                    ch(v.bn_stats(st[:, t % 2], X[:, t, :]))
                    v.bn_aggr(mv[:, t % 2], st[:, t % 2]).then_inc(s_mv, 1)

                def norm(t):
                    v.wait_ge(s_rs, t + 1)
                    if t >= 2:
                        v.wait_ge(s_xT, t - 1)
                    v.tensor_scalar(xn[:, t % 2], X[:, t, :], mv[:, t % 2, 0:1], rs[:, t % 2], ALU.subtract,
                                    ALU.mult).then_inc(s_xn, 1)

                def quant_x(t):
                    v.wait_ge(s_xT, t + 1)
                    for k in range(KT):
                        i = v.tensor_scalar(lnT[:, t % 2, k], pj[t % 2][:, k * P:(k + 1) * P], lnw[:, k:k + 1],
                                            lnb[:, k:k + 1], ALU.mult, ALU.add)
                    i.then_inc(s_ln, 1)
                    v.wait_ge(s_ln, t + 1)
                    yv = xq[:, t].rearrange("p s k n -> p (s k) n")
                    for s in range(4):
                        i = v.tensor_tensor(xq[:, t, s], lnT[:, t % 2],
                                            over(rinsc[:, 2 * s:2 * s + 2], 2, [P, KT, P]), ALU.mult)
                    ch(i)
                    quantise(yv, mag[:, t % 2], {"chain": ch, "sem": s_xq})

                def cut(n):
                    what, a, b = order[n]
                    slot = raw[:, n % NSLOT]
                    raw_here(v, n)
                    if centered(what, b):
                        if is_self(a) or b < 2:
                            v.wait_ge(s_scaled, n_scaled(order, n))
                        heads = slot.rearrange("p k (h d) -> p (k h) d", d=P)
                        ch(v.tensor_reduce(wmean[:, n % NSLOT], heads, AX.X, ALU.add))
                        ch(v.tensor_scalar(wmean[:, n % NSLOT], wmean[:, n % NSLOT], -1.0 / P, None, ALU.mult))
                        v.tensor_tensor(heads, heads, over(wmean[:, n % NSLOT], 2, [P, 8, P]), ALU.add).then_inc(s_centered, 1)
                    v.wait_ge(s_hi, n + 1)
                    k = WS if what == "w" and not is_self(a) and b >= 2 else 1.0
                    hi, lo = (w2h[:, a, b], w2l[:, a, b]) if what == "w" else (
                        ch_[:, :, a * 512:(a + 1) * 512], cl_[:, :, a * 512:(a + 1) * 512])
                    v.scalar_tensor_tensor(lo, slot, k, hi, ALU.mult, ALU.subtract).then_inc(s_lo, 1)

                stats(0)
                for t in range(NT):
                    norm(t)
                    if t + 1 < NT:
                        stats(t + 1)
                    cut(t)
                    quant_x(t)
                for n in range(NT, NCH - 8):
                    cut(n)

                uc, tc = TileChain(v, dun), TileChain(v, dti)

                def reduce(n, c):
                    sq_done.wait(v, n, c + 1)
                    rq_done.wait(v, n.before(), c + 1)
                    v.tensor_reduce(ms[:, c], sq[:, c].rearrange("p (h d) -> p h d", d=P), AX.X, ALU.add).then_inc(ms_done.sem, 1)

                def scale(n, c):
                    rq_done.wait(v, n, c + 1)
                    tq_ready.wait(v, n.before(), c + 1)
                    v.tensor_tensor(qn[:, c].rearrange("p (h d) -> p h d", d=P), pj[c][:].rearrange("p (h d) -> p h d", d=P),
                                    over(rq[:, c], 2, [P, 4, P]), ALU.mult).then_inc(qn_done.sem, 1)

                def ahead(n):
                    for c in range(3):
                        reduce(n, c)
                        scale(n, c)

                def unit(n, m, t):
                    uc.start(n)
                    sc_ready.wait(v, n, 1)
                    s3 = scb[:].rearrange("p (g t) -> p g t", t=T)
                    d3 = sc[:, n.parity].rearrange("p (g t) -> p g t", t=T)
                    uc(v.tensor_reduce(mx[:], s3, AX.X, ALU.max))
                    pt_ready.wait(v, n.before(2), 1)
                    v.tensor_tensor(d3, s3, over(mx[:], 2, [P, 8, T]), ALU.subtract).then_inc(sub_done.sem, 1)
                    if m is not None:
                        reduce(m, 0)
                        reduce(m, 1)
                        scale(m, 0)
                    exp_done.wait(v, n, 1)
                    uc(v.tensor_reduce(sm[:], d3, AX.X, ALU.add))
                    p_done.wait(v, n.before(), 1)
                    v.reciprocal(rc[:], sm[:]).then_inc(rc_done.sem, 1)
                    if m is not None:
                        scale(m, 1)
                        reduce(m, 2)
                        scale(m, 2)
                    pv_ready.wait(v, n, 1)
                    u = n.off % UN
                    if u == 0:
                        wp_ready.wait(v, t.before(), 1)
                    for b in range(2):
                        i = v.tensor_tensor(cat[:, 8 * u:8 * u + 8, b * T:(b + 1) * T],
                                            pv[b][:].rearrange("p (h s) -> p h s", s=T),
                                            over(rsm[:, 8 * u:8 * u + 8], 2, [P, 8, T]), ALU.mult)
                    i.then_inc(y_done.sem, 1)
                    y_done.wait(v, n, 1)
                    quantise(cat[:, 8 * u:8 * u + 8, :], cmag[:], {"chain": uc, "sem": cat_done.sem})
                    if u == UN - 1:
                        tc.start(t)
                        wp_ready.wait(v, t, 1)
                        xt = X[:, bass.ds(t.value(1), 1), :].rearrange("p a d -> p (a d)")
                        v.scalar_tensor_tensor(y[:], ptb[:, 0:D], pscale[:, 0:1], xt, ALU.mult, ALU.add).then_inc(yt_done.sem, 1)
                        yt_done.wait(v, t, 1)
                        tc(v.bn_stats(st[:, 0], y[:]))
                        v.memset(mx[:, 0:1], 0.0)
                        v.bn_aggr(mv[:, 0], st[:, 0]).then_inc(mv_done.sem, 1)
                        rs_done.wait(v, t, 1)
                        v.tensor_scalar(xt, y[:], mv[:, 0, 0:1], rs[:, 0], ALU.subtract, ALU.mult).then_inc(x2_done.sem, 1)

                skewed_units(v, ahead, unit)


def n_scaled(order, n):
    return sum(w == "w" and (u < UN // 2 or c < 2) for w, u, c in order[:n + 1])


def n_centered(order, n):
    return sum(w == "w" and c < 3 for w, u, c in order[:n + 1])


E = 8
FE = 176
FC = 2 * FE
NC3 = 6
FF = NC3 * FC
NB3 = -(-FF // P)
NG3 = -(-NB3 // 4)


def stage3(nc, io, X, out):
    with ExitStack() as ctx:
        def sb(name, shape, dt=F32):
            return ctx.enter_context(nc.sbuf_tensor(name, [P] + shape, dt))

        def pb(name):
            return ctx.enter_context(nc.psum_tensor(name, [P, 512], F32))

        def sem(name):
            return ctx.enter_context(nc.semaphore(name))

        def sig(name, per):
            return Signal(sem(name), per)

        NSLOT = 4
        raw = sb("raw3", [NSLOT, 2 * 2 * FC])
        wuh = sb("wuh", [NC3, KT, 2 * FC], F16)
        wul = sb("wul", [NC3, KT, 2 * FC], F16)
        wdh = sb("wdh", [NG3 * 4, D], F16)
        wdl = sb("wdl", [NG3 * 4, D], F16)
        wr32 = sb("wr32", [KT, E + 1])
        wrh = sb("wrh", [KT, E + 1], F16)
        wrl = sb("wrl", [KT, E + 1], F16)
        ident = sb("ident3", [P])
        iota = sb("iota3", [E])
        xh = sb("x3h", [KT, NTOK], F16)
        xl = sb("x3l", [KT, NTOK], F16)
        lg = sb("lg", [NT, E + 1])
        pr = sb("pr", [NT, E])
        mx = sb("mx3", [NT])
        top = sb("top", [NT, 8])
        idx = sb("idx", [NT, 8], U32)
        idf = sb("idf", [NT, 8])
        m1 = sb("m1", [NT, E])
        m2 = sb("m2", [NT, E])
        gate = sb("gate", [NT, E + 1])
        s1 = sb("s1", [2, FC])
        h = sb("h3", [2, NB3 * P])
        hTh = sb("hTh", [2, 512], F16)
        hTl = sb("hTl", [2, 512], F16)
        y = sb("y3", [D])
        st = sb("st3", [6])
        mv = sb("mv3", [2])
        rs = sb("rs3", [1])
        epsc = sb("eps3", [1])
        mhalf = sb("mhalf3", [1])
        spare = sb("spare3", [1])
        ob = sb("ob", [2, D])

        h1b = [pb("h1a"), pb("h1b")]
        h2b = [pb("h2a"), pb("h2b")]
        tb_ = [pb("tA"), pb("tB")]
        yb = [pb("yA"), pb("yB")]

        s_id, s_wr = sem("ident3_loaded"), sem("wr_loaded")
        NU = NC3 + NG3
        s_raw = [sem(f"raw3_loaded{i}") for i in range(NSLOT)]
        s_hi, s_lo, s_wrh, s_wrl = sem("w3_hi"), sem("w3_lo"), sem("wr_hi"), sem("wr_lo")
        s_xT, s_xh, s_xl, s_lg = sem("x3T"), sem("x3_hi"), sem("x3_lo"), sem("logits")
        s_mx, s_e, s_z, s_ze, s_gate, s_zero = (sem("soft_in"), sem("soft_exp"), sem("gate_in"), sem("gate_exp"),
                                                sem("gates_done"), sem("zero3"))
        dch, dti, pti, pch = sem("dve_setup3"), sem("dve_tile3"), sem("pool_tile3"), sem("pool_setup3")
        up_ready, silu_done, h_done = sig("up_ready", NC3), sig("silu3_done", NC3), sig("h_done", NC3)
        t_ready, hi_done, lo_done, down_done = (sig("t_ready", NG3), sig("hi3_done", NG3), sig("lo3_done", NG3),
                                                sig("down_done", NG3))
        yt_done, mv_done, rs_done, out_ready, stored = (sig("y3_done", 1), sig("mv3_done", 1), sig("rs3_done", 1),
                                                        sig("out_ready", 1), sig("out_stored", 16))

        def raw_here(eng, n):
            eng.wait_ge(s_raw[n % NSLOT], 16 * (n // NSLOT + 1))

        def two_before(eng, s, t, k, per):
            if t.reg is not None or t.off * per + k - 1 > 0:
                eng.wait_ge(s.sem, t.value(per, k - 1))

        with nc.Block() as block:
            @block.sync
            def _(sp):
                sp.dma_start(ident[:], io["consts"][:, 0:P]).then_inc(s_id, 16)
                sp.dma_start(iota[:], io["iota"]).then_inc(s_id, 16)
                sp.dma_start(wr32[:], io["wr"].rearrange("(k p) n -> p k n", p=P)).then_inc(s_wr, 16)
                wu = io["wu"].rearrange("(k p) n -> p k n", p=P)
                wd = io["wd"].rearrange("(n p) c -> p n c", p=P)
                for n in range(NU):
                    if n >= NSLOT:
                        sp.wait_ge(s_lo, n - NSLOT + 1)
                    if n < NC3:
                        sp.dma_start(raw[:, n % NSLOT, 0:4 * FC].rearrange("p (k n) -> p k n", k=KT),
                                     wu[:, :, n * 2 * FC:(n + 1) * 2 * FC]).then_inc(s_raw[n % NSLOT], 16)
                    else:
                        b = 4 * (n - NC3)
                        m = min(4, NB3 - b)
                        sp.dma_start(raw[:, n % NSLOT, 0:m * D].rearrange("p (n c) -> p n c", c=D),
                                     wd[:, b:b + m, :]).then_inc(s_raw[n % NSLOT], 16)

                def store(t):
                    ready, before = out_ready.count(sp, t, 1), t.before()
                    landed = stored.count(sp, before, 16) if before.exists else None
                    row = t.value(P) if t.reg is None else sp.snap(t.value(P))
                    sp.wait_ge(out_ready.sem, ready)
                    if before.exists:
                        sp.wait_ge(stored.sem, landed)
                    sp.dma_start(out[bass.ds(row, P), :], ob[:, t.parity]).then_inc(stored.sem, 16)

                def front(t, tb):
                    if tb is not None:
                        store(tb)

                skewed_tiles(sp, front)
                stored.wait(sp, Tile(NT - 1), 16)

            @block.tensor
            def _(pe):
                pe.wait_ge(s_id, 32)
                for t in range(NT):
                    if t >= 2:
                        pe.wait_ge(s_xl, t - 1)
                    for k in range(KT):
                        i = pe.transpose(tb_[t % 2][:, k * P:(k + 1) * P], X[:, t, k * P:(k + 1) * P], ident[:])
                    i.then_inc(s_xT, 1)
                pe.wait_ge(s_xl, NT)
                pe.wait_ge(s_wrl, 1)
                for t in range(NT):
                    tok = slice(t * P, (t + 1) * P)
                    for k in range(KT):
                        for j, (a, b) in enumerate(((xh, wrh), (xl, wrh), (xh, wrl))):
                            i = pe.matmul(yb[0][:, t * (E + 1):(t + 1) * (E + 1)], a[:, k, tok], b[:, k, :],
                                          start=k == 0 and j == 0, stop=k == KT - 1 and j == 2)
                i.then_inc(s_lg, 1)

                def up(t, c):
                    two_before(pe, h_done, t, c, NC3)
                    if t.reg is None and t.off == 0:
                        pe.wait_ge(s_lo, c + 1)
                    tok = bass.ds(t.value(P), P)
                    for bank, w0 in ((h1b[c % 2], 0), (h2b[c % 2], FC)):
                        for k in range(KT):
                            for j, (a, b) in enumerate(((xh, wuh), (xh, wul), (xl, wuh))):
                                i = pe.matmul(bank[:, 0:FC], a[:, k, tok], b[:, c, k, w0:w0 + FC],
                                              start=k == 0 and j == 0, stop=k == KT - 1 and j == 2)
                    i.then_inc(up_ready.sem, 1)

                def turn(t, g):
                    h_done.wait(pe, t, NC3)
                    two_before(pe, lo_done, t, g, NG3)
                    for j in range(min(4, NB3 - 4 * g)):
                        b = 4 * g + j
                        i = pe.transpose(tb_[(t.parity + g) % 2][:, j * P:(j + 1) * P], h[:, t.parity, b * P:(b + 1) * P],
                                         ident[:])
                    i.then_inc(t_ready.sem, 1)

                def down(t, g):
                    lo_done.wait(pe, t, g + 1)
                    if g == 0:
                        yt_done.wait(pe, t.before(2), 1)
                        if t.reg is None and t.off == 0:
                            pe.wait_ge(s_lo, NU)
                            pe.wait_ge(s_gate, 1)
                    q = (t.parity + g) % 2
                    m = min(4, NB3 - 4 * g)
                    for j in range(m):
                        b = 4 * g + j
                        c = slice(j * P, (j + 1) * P)
                        for x, (a, w) in enumerate(((hTh, wdh), (hTh, wdl), (hTl, wdh))):
                            i = pe.matmul(yb[t.parity][:, 0:D], a[:, q, c], w[:, b, :], start=b == 0 and x == 0,
                                          stop=b == NB3 - 1 and x == 2)
                    i.then_inc(down_done.sem, 1)

                def front(t, tb):
                    for c in range(NC3):
                        if t is not None:
                            up(t, c)
                        if tb is not None:
                            if c < NG3:
                                turn(tb, c)
                            if c > 0:
                                down(tb, c - 1)

                skewed_tiles(pe, front)

            @block.scalar
            def _(act):
                act.wait_ge(s_wr, 16)
                act.activation(wrh[:], wr32[:], ACT.Copy, scale=WS).then_inc(s_wrh, 1)

                def cut(n):
                    raw_here(act, n)
                    if n < NC3:
                        dst, src = wuh[:, n].rearrange("p k n -> p (k n)"), raw[:, n % NSLOT, 0:4 * FC]
                    else:
                        b = 4 * (n - NC3)
                        m = min(4, NB3 - b)
                        dst, src = wdh[:, b:b + m].rearrange("p n c -> p (n c)"), raw[:, n % NSLOT, 0:m * D]
                    act.activation(dst, src, ACT.Copy, scale=WS).then_inc(s_hi, 1)

                for t in range(NT):
                    act.wait_ge(s_xT, t + 1)
                    act.activation(xh[:, :, t * P:(t + 1) * P], tb_[t % 2][:, 0:D].rearrange("p (k n) -> p k n", k=KT),
                                   ACT.Copy).then_inc(s_xh, 1)
                    if t < 4:
                        cut(t)
                act.wait_ge(s_mx, 1)
                act.activation(pr[:], pr[:], ACT.Exp).then_inc(s_e, 1)
                act.wait_ge(s_z, 1)
                act.activation(mx[:], lg[:, :, E], ACT.Exp, scale=-1.0).then_inc(s_ze, 1)
                for n in range(4, NU):
                    cut(n)

                def silu(t, c):
                    up_ready.wait(act, t, c + 1)
                    two_before(act, h_done, t, c, NC3)
                    act.activation(s1[:, c % 2], h1b[c % 2][:, 0:FC], ACT.Silu, scale=1 / WS).then_inc(silu_done.sem, 1)

                def high(t, g):
                    t_ready.wait(act, t, g + 1)
                    two_before(act, down_done, t, g, NG3)
                    q, n = (t.parity + g) % 2, min(4, NB3 - 4 * g) * P
                    act.activation(hTh[:, q, 0:n], tb_[q][:, 0:n], ACT.Copy).then_inc(hi_done.sem, 1)

                def front(t, tb):
                    for c in range(NC3):
                        if t is not None:
                            silu(t, c)
                        if tb is not None and c < NG3:
                            high(tb, c)

                skewed_tiles(act, front)

            @block.gpsimd
            def _(pool):
                pool.memset(epsc[:], EPS)
                pool.memset(mhalf[:], -0.5).then_inc(pch, 1)
                pool.memset(h[:, :, FF:], 0.0).then_inc(s_zero, 1)
                pool.wait_ge(pch, 1)
                pc = TileChain(pool, pti)

                def front(t, tb):
                    if tb is not None:
                        pc.start(tb)
                        mv_done.wait(pool, tb, 1)
                        pc(pool.tensor_tensor(rs[:], mv[:, 1:2], epsc[:], ALU.add))
                        pool.tensor_tensor(rs[:], rs[:], mhalf[:], ALU.pow).then_inc(rs_done.sem, 1)

                skewed_tiles(pool, front)

            @block.vector
            def _(v):
                ch = Chain(v, dch)
                v.wait_ge(s_wrh, 1)
                v.scalar_tensor_tensor(wrl[:], wr32[:], WS, wrh[:], ALU.mult, ALU.subtract).then_inc(s_wrl, 1)

                def cut(n):
                    v.wait_ge(s_hi, n + 1)
                    if n < NC3:
                        c = slice(0, 4 * FC)
                        hi, lo = (w[:, n].rearrange("p k n -> p (k n)") for w in (wuh, wul))
                    else:
                        b = 4 * (n - NC3)
                        m = min(4, NB3 - b)
                        c = slice(0, m * D)
                        hi, lo = (w[:, b:b + m].rearrange("p n c -> p (n c)") for w in (wdh, wdl))
                    v.scalar_tensor_tensor(lo, raw[:, n % NSLOT, c], WS, hi, ALU.mult, ALU.subtract).then_inc(s_lo, 1)

                for t in range(NT):
                    v.wait_ge(s_xh, t + 1)
                    tok = slice(t * P, (t + 1) * P)
                    v.tensor_tensor(xl[:, :, tok], tb_[t % 2][:, 0:D].rearrange("p (k n) -> p k n", k=KT), xh[:, :, tok],
                                    ALU.subtract).then_inc(s_xl, 1)
                    if t < 4:
                        cut(t)
                v.wait_ge(s_lg, 1)
                v.tensor_scalar(lg[:].rearrange("p t e -> p (t e)"), yb[0][:, 0:NT * (E + 1)], 1 / WS, None,
                                ALU.mult).then_inc(s_z, 1)
                v.wait_ge(s_z, 1)
                ch(v.tensor_reduce(m1[:, :, 0], lg[:, :, 0:E], AX.X, ALU.max))
                v.tensor_tensor(pr[:], lg[:, :, 0:E], over(m1[:, :, 0], 2, [P, NT, E]), ALU.subtract).then_inc(s_mx, 1)
                v.wait_ge(s_e, 1)
                ch(v.tensor_reduce(m2[:, :, 0], pr[:], AX.X, ALU.add))
                ch(v.reciprocal(m2[:, :, 1], m2[:, :, 0]))
                ch(v.tensor_tensor(pr[:], pr[:], over(m2[:, :, 1], 2, [P, NT, E]), ALU.mult))
                for t in range(NT):
                    i = v.max(top[:, t], pr[:, t])
                ch(i)
                for t in range(NT):
                    i = v.max_index(idx[:, t], top[:, t], pr[:, t])
                ch(i)
                ch(v.tensor_copy(idf[:], idx[:]))
                v.wait_ge(s_id, 32)
                v.tensor_tensor(m1[:], over(iota[:], 1, [P, NT, E]), idf[:, :, 0:1].broadcast_to([P, NT, E]), ALU.is_equal)
                ch(v.tensor_tensor(m2[:], over(iota[:], 1, [P, NT, E]), idf[:, :, 1:2].broadcast_to([P, NT, E]), ALU.is_equal))
                ch(v.tensor_tensor(m1[:], m1[:], m2[:], ALU.add))
                v.scalar_tensor_tensor(gate[:, :, 0:E], pr[:], 1 / WS, m1[:], ALU.mult, ALU.mult)
                v.wait_ge(s_ze, 1)
                ch(v.tensor_scalar(mx[:], mx[:], 1.0, None, ALU.add))
                ch(v.reciprocal(mx[:], mx[:]))
                v.tensor_scalar(gate[:, :, E], mx[:], 1 / WS, None, ALU.mult).then_inc(s_gate, 1)
                for n in range(4, NU):
                    cut(n)
                v.wait_ge(s_gate, 1)
                v.wait_ge(s_zero, 1)
                vc = TileChain(v, dti)

                def gated(t, c):
                    silu_done.wait(v, t, c + 1)
                    if c == 0:
                        t_ready.wait(v, t.before(2), NG3)
                    gt = gate[:, bass.ds(t.value(1), 1), :].rearrange("p a e -> p (a e)")
                    for j in range(2 if c < E // 2 else 1):
                        e, n = (2 * c + j, FE) if c < E // 2 else (E, FC)
                        i = v.scalar_tensor_tensor(h[:, t.parity, c * FC + j * FE:c * FC + j * FE + n],
                                                   h2b[c % 2][:, j * FE:j * FE + n], gt[:, e:e + 1],
                                                   s1[:, c % 2, j * FE:j * FE + n], ALU.mult, ALU.mult)
                    i.then_inc(h_done.sem, 1)

                def low(t, g):
                    hi_done.wait(v, t, g + 1)
                    two_before(v, down_done, t, g, NG3)
                    q, n = (t.parity + g) % 2, min(4, NB3 - 4 * g) * P
                    v.tensor_tensor(hTl[:, q, 0:n], tb_[q][:, 0:n], hTh[:, q, 0:n], ALU.subtract).then_inc(lo_done.sem, 1)

                def finish(t):
                    down_done.wait(v, t, NG3)
                    vc.start(t)
                    xt = X[:, bass.ds(t.value(1), 1), :].rearrange("p a d -> p (a d)")
                    v.scalar_tensor_tensor(y[:], yb[t.parity][:, 0:D], 1 / WS, xt, ALU.mult, ALU.add).then_inc(yt_done.sem, 1)
                    yt_done.wait(v, t, 1)
                    vc(v.bn_stats(st[:], y[:]))
                    v.memset(spare[:], 0.0)
                    v.bn_aggr(mv[:], st[:]).then_inc(mv_done.sem, 1)
                    rs_done.wait(v, t, 1)
                    stored.wait(v, t.before(2), 16)
                    v.tensor_scalar(ob[:, t.parity], y[:], mv[:, 0:1], rs[:, 0:1], ALU.subtract,
                                    ALU.mult).then_inc(out_ready.sem, 1)

                def front(t, tb):
                    for c in range(NC3):
                        if t is not None:
                            gated(t, c)
                        if tb is not None and c < NG3:
                            low(tb, c)
                    if tb is not None:
                        finish(tb)

                skewed_tiles(v, front)


def program(nc, io, outs):
    with ExitStack() as ctx:
        X = ctx.enter_context(nc.sbuf_tensor("X", [P, NT, D], F32))
        stage1(nc, io, X)
        stage2(nc, io, X)
        stage3(nc, io, X, outs[0])


def kernel(**inputs):
    import concourse.bacc as bacc
    from concourse.bass_utils import run_bass_kernel_spmd as run

    A = {k: np.asarray(v) for k, v in inputs.items()}
    L = lambda n: A["L0_attn_" + n]
    rows = lambda a: np.ascontiguousarray(np.broadcast_to(a.reshape(1, -1), (P, a.size)))
    cuts = lambda a: [a[:, h * P:(h + 1) * P] for h in range(H)]
    q, k = cuts(L("Wq")), cuts(L("Wk"))
    cq, ck = [c.reshape(H, P, 4) for c in (L("conv_wq"), L("conv_wk"))]
    w1 = [L("Wb"), L("Wa")]
    cw = []
    for h in range(H):
        w1 += [k[h], q[h]]
        cw += [ck[h], cq[h]]
    w1 += [L("Wv"), L("Wg")]
    cw += list(L("conv_wv").reshape(3, P, 4))
    u = np.arange(P)[:, None]
    s, t = np.arange(P)[None, :], np.arange(T)[None, :]
    consts = np.concatenate([
        u == s, (u > s) & (u // T == s // T), u % T <= t, t >= u % T, t // BLK > (u % T) // BLK,
    ], axis=1).astype(np.float32)
    x = A["x"].reshape(NTOK, D)
    arrays = {
        "x": x, "xT": x.T, "w1": np.concatenate(w1, axis=1), "wo": L("Wo"),
        "convw": np.stack(cw, axis=1),
        "dtb": rows(L("dt_bias")), "alog": rows(L("A_log")), "normw": rows(L("norm_w")),
        "consts": consts, "eye16": np.ascontiguousarray(np.broadcast_to(np.eye(BLK, dtype=np.float32).reshape(1, -1), (P, BLK * BLK))),
    }
    Y = lambda n: A["L0_xattn_" + n]
    wqT, wqxT, wkT, wvT, wkvxT = (Y(n).T for n in ("wq", "wqx", "wk", "wv", "w_kv_x"))
    w2 = []
    for q_, k_, v_ in ((wqT, wkT, wvT), (wqxT, wkvxT[:, :G * P], wkvxT[:, G * P:])):
        for half in range(2):
            w2 += [q_[:, half * 1024:(half + 1) * 1024], k_[:, half * 512:(half + 1) * 512],
                   v_[:, half * 512:(half + 1) * 512]]
    cols = lambda a, n: a.reshape(n, P).T
    prm2 = [cols(Y("ln_w"), 2), cols(Y("ln_b"), 2)]
    prm2 += [cols(Y(n + "_in_scale"), 2) for n in ("q", "qx", "k", "v")]
    for n in ("q", "qx", "k", "kx"):
        prm2 += [cols(Y(n + "ln_w"), 1), cols(Y(n + "ln_b"), 1)]
    prm2 += [rows(Y(n)) for n in ("wq_scale", "wqx_scale", "wk_scale", "wv_scale", "proj_in_scale", "proj_w_scale")]
    prm2 += [cols(Y("proj_smooth"), NH2)]
    arrays.update({"w2": np.concatenate(w2, axis=1), "wproj": Y("wproj").T, "ctxT": A["ctx_2048"].reshape(NTOK, D).T,
                   "prm2": np.concatenate(prm2, axis=1)})
    Z = lambda n: A["L0_ffn_" + n]
    e1, e2 = Z("expert_fc1").reshape(E * FE, D).T, Z("expert_fc2").reshape(E * FE, D).T
    f1, f2 = np.concatenate([e1, Z("shared_fc1").T], axis=1), np.concatenate([e2, Z("shared_fc2").T], axis=1)
    wu = [w[:, c * FC:(c + 1) * FC] for c in range(NC3) for w in (f1, f2)]
    wd = np.concatenate([Z("expert_proj").transpose(0, 2, 1).reshape(E * FE, D), Z("shared_proj").T,
                         np.zeros((NB3 * P - FF, D), np.float32)])
    arrays.update({"wu": np.concatenate(wu, axis=1), "wd": wd,
                   "wr": np.concatenate([Z("gate_w").T, Z("shared_gate_w").T], axis=1),
                   "iota": rows(np.arange(E, dtype=np.float32))})
    nc = bacc.Bacc("TRN2", target_bir_lowering=False, num_devices=1)
    feed, io = {}, {}
    for n, a in arrays.items():
        a = np.ascontiguousarray(a)
        feed["in_" + n] = a
        io[n] = nc.dram_tensor("in_" + n, a.shape, F32, kind="ExternalInput").ap()
    out = nc.dram_tensor("out_0", (NTOK, D), F32, kind="ExternalOutput").ap()
    program(nc, io, [out])
    r = run(nc, [feed], core_ids=[0])
    return r.results[0]["out_0"].reshape(16, T, D)
```

```python
from contextlib import ExitStack
from itertools import chain

import numpy as np
import concourse.bass as bass
from concourse import mybir

F32 = mybir.dt.float32
F16 = mybir.dt.float16
BF16 = mybir.dt.bfloat16
U16 = mybir.dt.uint16
U32 = mybir.dt.uint32
ALU = mybir.AluOpType
ACT = mybir.ActivationFunctionType
AX = mybir.AxisListType

P = 128
T = 64
D = 256
KT = D // P
NTOK = 1024
NT = NTOK // P
H = 12
DV = 32
HV = H * DV
NPAIR = H // 2
CH1 = 24 + 2 * H * P + 2 * HV
WS = 64.0
BLK = 32
NBLK = P // BLK
YP = NBLK * H
SOLVE = 4
EPS = 1e-5


class Tile:

    def __init__(self, off, reg=None, stride=2):
        self.off, self.reg, self.stride = off, reg, stride

    def value(self, per, k=0):
        base = self.off * per + k
        return base if self.reg is None else self.reg * (self.stride * per) + base

    def before(self, n=1):
        return Tile(self.off - n, self.reg, self.stride)

    @property
    def exists(self):
        return self.reg is not None or self.off >= 0

    @property
    def parity(self):
        return self.off % 2


class Signal:

    def __init__(self, sem, per):
        self.sem, self.per = sem, per

    def wait(self, eng, t, k):
        if t.exists:
            eng.wait_ge(self.sem, t.value(self.per, k))

    def count(self, eng, t, k):
        if t.reg is None:
            return t.value(self.per, k)
        reg = eng.alloc_register(f"count_{eng.bass.next_id()}")
        eng.reg_mov(reg, t.value(self.per, k))
        return eng.snap(reg, min_val=0)


class Chain:

    def __init__(self, eng, sem):
        self.eng, self.sem, self.n = eng, sem, 0

    def __call__(self, ins):
        self.n += 1
        ins.then_inc(self.sem, 1)
        self.eng.wait_ge(self.sem, self.n)


class TileChain:

    def __init__(self, eng, sem):
        self.eng, self.sem, self.per, self.n, self.t = eng, sem, 0, 0, None

    def start(self, t):
        if self.t is not None and self.per == 0:
            self.per = self.n
        self.t, self.n = t, 0

    def mark(self, ins):
        self.n += 1
        ins.then_inc(self.sem, 1)
        return self.n

    def wait(self, n=None):
        self.eng.wait_ge(self.sem, self.t.value(self.per, self.n if n is None else n))

    def __call__(self, ins):
        self.mark(ins)
        self.wait()


def over(ap, axis, shape):
    return ap.unsqueeze(axis).broadcast_to(shape)


def woven_tiles(eng, front):
    front(Tile(0), None, None)
    front(Tile(1), Tile(0), None)
    front(Tile(2), Tile(1), Tile(0))
    with eng.Fori(0, (NT - 4) // 2) as i:
        front(Tile(3, i), Tile(2, i), Tile(1, i))
        front(Tile(4, i), Tile(3, i), Tile(2, i))
    front(Tile(NT - 1), Tile(NT - 2), Tile(NT - 3))
    front(None, Tile(NT - 1), Tile(NT - 2))
    front(None, None, Tile(NT - 1))


def weave(*programs):
    programs = list(programs)
    while programs:
        for p in list(programs):
            if next(p, "end") == "end":
                programs.remove(p)


def stage1(nc, io, X):
    with ExitStack() as ctx:
        def sb(name, shape, dt=F32):
            return ctx.enter_context(nc.sbuf_tensor(name, [P] + shape, dt))

        def pb(name):
            return ctx.enter_context(nc.psum_tensor(name, [P, 512], F32))

        def sem(name):
            return ctx.enter_context(nc.semaphore(name))

        def sig(name, per):
            return Signal(sem(name), per)

        xT32 = sb("xT32", [KT, NTOK])
        xh = sb("xh", [KT, NTOK], F16)
        xl = sb("xl", [KT, NTOK], F16)
        w32 = sb("w32", [KT, CH1])
        wh = sb("wh", [KT, CH1], F16)
        wl = sb("wl", [KT, CH1], F16)
        wo32 = sb("wo32", [3, D])
        woh = sb("woh", [3, D], F16)
        wol = sb("wol", [3, D], F16)
        cw = sb("cw", [27, 4])
        consts = sb("consts", [2 * P + 3 * T])
        ident = consts[:, 0:P]
        later = consts[:, P:2 * P]
        upto = consts[:, 2 * P:2 * P + T]
        incl = consts[:, 2 * P + T:2 * P + 2 * T]
        offblk = consts[:, 2 * P + 2 * T:2 * P + 3 * T]
        eyes = sb("eyes", [BLK // 2, BLK])
        dtb = sb("dtb", [H])
        alog = sb("alog", [H])
        normw = sb("normw", [DV])
        ones = sb("ones", [1])
        mhalf = sb("mhalf", [2 * H])
        epsc = sb("epsc", [H])
        spare = sb("spare", [1])
        ba = sb("ba", [NT, 2 * H])
        beta = sb("beta", [NT, H])
        g = sb("g", [NT, H])
        s1a = sb("s1a", [NT, H])
        s1b = sb("s1b", [NT, H])
        s1c = sb("s1c", [NT, H])
        gL = sb("gL", [2, H, T])
        F = sb("F", [NT, H, T])
        acc = sb("acc", [2, 4, P])
        far = sb("far", [2, 4, P])
        kq = sb("kq", [2, 2, 2, P])
        sq = sb("sq", [2, 2, 2, P])
        vT = sb("vT", [3, P])
        UP = sb("UP", [2, H, 2, P])
        Xf = sb("Xf", [H, P])
        Yn = sb("Yn", [BLK // 2, BLK])
        Ue = sb("Ue", [BLK, BLK])
        Yt = sb("Yt", [BLK // 2, BLK])
        n2 = sb("n2", [2, 2 * H])
        rn = sb("rn", [2, 2 * H])
        Bp = sb("Bp", [2, H])
        absk = sb("absk", [2, H])
        V = sb("V", [2, HV])
        w = sb("w", [2, HV])
        gs = sb("gs", [2, HV])
        sqo = sb("sqo", [HV])
        ms = sb("ms", [H])
        rr = sb("rr", [H])
        r2 = sb("r2", [H])
        on = sb("on", [HV])
        onh = sb("onh", [3, P], F16)
        onl = sb("onl", [3, P], F16)
        y = sb("y", [D])
        st = sb("st", [6])
        mv = sb("mv", [2])
        rs = sb("rs", [1])

        proj = [pb("proj0"), pb("proj1")]
        gram = [pb("gram0"), pb("gram1")]
        small = pb("small")
        turn = pb("turn")
        sol = [pb("sol0"), pb("sol1")]

        UD = nc.dram_tensor("ud_dram", (NBLK, H, BLK, BLK), F32, kind="Internal").ap()
        YD = nc.dram_tensor("yd_dram", (NBLK, H, BLK, BLK), F32, kind="Internal").ap()

        s_x, s_X, s_c, s_wo = sem("x_loaded"), sem("xtok_loaded"), sem("consts_loaded"), sem("wo_loaded")
        NW = 4
        wcut = [0, 24 + 512 * 1, 24 + 512 * 3, 24 + 512 * 5, CH1]
        s_w = [sem(f"w1_loaded{i}") for i in range(NW)]
        s_xh, s_xl, s_wh, s_wl = sem("xh_done"), sem("xl_done"), sem("wh_done"), sem("wl_done")
        s_ba, s_ba_ev, s_eb, s_ea, s_g = sem("ba_ready"), sem("ba_done"), sem("expb_done"), sem("expa_done"), sem("g_done")
        s_na, s_ealog = sem("na_done"), sem("expalog_done")
        s_gL, s_D, s_F, s_Fm, s_zero = sem("gL_done"), sem("decay_ready"), sem("decay_exp"), sem("decay_masked"), sem("zero_done")
        s_beta = sem("beta_done")
        dch, dtile, dback, dend = sem("dve_setup"), sem("dve_tile"), sem("dve_back"), sem("dve_end")
        pch, ptile, pend = sem("pool_setup"), sem("pool_tile"), sem("pool_end")
        proj_ready = sig("proj_ready", 7)
        gg_ready, gg_done = sig("gg_ready", 1), sig("gg_done", 1)
        tap_done, conv_done, summed, silu_done = sig("tap_done", 7), sig("conv_done", 7), sig("conv_summed", 7), sig("silu_done", 7)
        sq_done = sig("sq_done", 6)
        gram_ready, gram_used, norm_ready = sig("gram_ready", 6), sig("gram_used", 6), sig("norm_ready", 6)
        n2_done, bp_done, rn_done = sig("n2_done", 1), sig("bp_done", 1), sig("rn_done", 1)
        vt_ready, v_done = sig("vt_ready", 1), sig("v_done", 1)
        u_scaled, u_masked = sig("u_scaled", 2), sig("u_masked", 2)
        ud_stored, ue_loaded = sig("ud_stored", 16 * NBLK), sig("ue_loaded", 32)
        y_done, yd_stored, xf_loaded = sig("y_done", 1), sig("yd_stored", 32), sig("xf_loaded", 16 * NBLK)
        sol_ready, sol_used = sig("sol_ready", SOLVE), sig("sol_used", SOLVE - 1)
        sqo_done, ms_done, rr_done = sig("sqo_done", 1), sig("ms_done", 1), sig("rr_done", 1)
        gsn_done, on_done, onT_ready = sig("gsn_done", 1), sig("on_done", 1), sig("onT_ready", 1)
        onh_done, onl_done, wo_ready = sig("onh_done", 1), sig("onl_done", 1), sig("wo_ready", 1)
        res_done, mv_done, rs_done, x1_done = sig("res_done", 1), sig("mv_done", 1), sig("rs_done", 1), sig("x1_done", 1)

        def unit_cols(u):
            return 24 + 512 * u

        GG = 24 + 512 * NPAIR + HV

        with nc.Block() as block:
            @block.sync
            def _(sp):
                sp.dma_start(xT32[:], io["xT"].rearrange("(k p) n -> p k n", p=P)).then_inc(s_x, 16)
                w1 = io["w1"].rearrange("(k p) n -> p k n", p=P)
                for i in range(NW):
                    sp.dma_start(w32[:, :, wcut[i]:wcut[i + 1]], w1[:, :, wcut[i]:wcut[i + 1]]).then_inc(s_w[i], 16)
                    if i == 0:
                        sp.dma_start(consts[:], io["consts"]).then_inc(s_c, 16)
                        for dst, src in ((eyes[:].rearrange("p a b -> p (a b)"), "eyes"), (cw[:], "convw"), (dtb[:], "dtb"),
                                         (alog[:], "alog"), (normw[:], "normw")):
                            sp.dma_start(dst, io[src]).then_inc(s_c, 16)
                sp.dma_start(X[:], io["x"].rearrange("(t p) d -> p t d", p=P)).then_inc(s_X, 16)
                sp.dma_start(wo32[:], io["wo"].rearrange("(k p) n -> p k n", p=P)).then_inc(s_wo, 16)

                def back(t):
                    b4 = t.before()
                    waits = [(u_scaled, t, 2), (ue_loaded, b4, 32), (ud_stored, t, 16 * NBLK), (y_done, b4, 1),
                             (y_done, t, 1), (xf_loaded, b4, 16 * NBLK), (yd_stored, t, 32), (sol_ready, b4, SOLVE - 1)]
                    scaled, ue_read, stored, y_before, y_now, xf_before, yd_now, sol_before = (
                        (s.sem, s.count(sp, n, k)) if n.exists else None for s, n, k in waits)
                    sp.wait_ge(*scaled)
                    if b4.exists:
                        sp.wait_ge(*ue_read)
                    for b in range(NBLK):
                        c = b * BLK
                        sp.dma_start(UD[b].rearrange("h s t -> s h t"),
                                     UP[c:c + BLK, t.parity, :, 0, c:c + BLK]).then_inc(ud_stored.sem, 16)
                    sp.wait_ge(*stored)
                    if b4.exists:
                        sp.wait_ge(*y_before)
                    for odd in range(2):
                        sp.dma_start(Ue[odd * YP:(odd + 1) * YP].rearrange("p s t -> p (s t)"),
                                     UD.rearrange("b h s t -> (b h) (s t)")).then_inc(ue_loaded.sem, 16)
                    sp.wait_ge(*y_now)
                    if b4.exists:
                        sp.wait_ge(*xf_before)
                    for odd in range(2):
                        sp.dma_start(YD.rearrange("b h (s a) t -> a (b h) s t", a=2)[odd],
                                     Yn[odd * YP:(odd + 1) * YP]).then_inc(yd_stored.sem, 16)
                    sp.wait_ge(*yd_now)
                    if b4.exists:
                        sp.wait_ge(*sol_before)
                    else:
                        sp.wait_ge(s_zero, 3)
                    for b in range(NBLK):
                        c = b * BLK
                        sp.dma_start(Xf[c:c + BLK, :, c:c + BLK],
                                     YD[b].rearrange("h s t -> s h t")).then_inc(xf_loaded.sem, 16)

                def front(t, tb, tf):
                    if tb is not None:
                        back(tb)

                woven_tiles(sp, front)
                ud_stored.wait(sp, Tile(NT - 1), 16 * NBLK)
                yd_stored.wait(sp, Tile(NT - 1), 32)
                xf_loaded.wait(sp, Tile(NT - 1), 16 * NBLK)

            @block.tensor
            def _(pe):
                def split_mm(out, stat_h, stat_l, mov_h, mov_l, start, stop):
                    pe.matmul(out, stat_h, mov_h, start=start, stop=False)
                    pe.matmul(out, stat_h, mov_l, start=False, stop=False)
                    return pe.matmul(out, stat_l, mov_h, start=False, stop=stop)

                pe.wait_ge(s_xh, 1)
                pe.wait_ge(s_xl, 1)
                pe.wait_ge(s_wh, 1)
                pe.wait_ge(s_wl, 1)
                for t in range(NT):
                    tok = slice(t * P, (t + 1) * P)
                    for k in range(KT):
                        mm = split_mm(proj[0][:, t * 24:t * 24 + 24], xh[:, k, tok], xl[:, k, tok],
                                      wh[:, k, 0:24], wl[:, k, 0:24], k == 0, k == KT - 1)
                mm.then_inc(s_ba, 1)
                pe.wait_ge(s_c, 16 * 6)
                for t in range(NT):
                    pe.wait_ge(s_gL, t + 1)
                    if t > 0:
                        pe.wait_ge(s_F, 2 * t)
                    for hh in range(2):
                        pe.matmul(gram[hh][:, 0:6 * T], later,
                                  gL[:, t % 2, hh * 6:hh * 6 + 6, :], start=True, stop=True).then_inc(s_D, 1)

                def project(t, u):
                    if u == 0:
                        conv_done.wait(pe, t.before(), 7)
                        if t.reg is None and t.off == 0:
                            pe.wait_ge(s_ba_ev, 1)
                    elif u == 1:
                        gg_done.wait(pe, t.before(), 1)
                    else:
                        conv_done.wait(pe, t, u - 1)
                    if t.reg is None and t.off == 0 and u in (0, 1, 3, 5):
                        n = {0: 1, 1: 2, 3: 3, 5: 4}[u]
                        pe.wait_ge(s_wh, n)
                        pe.wait_ge(s_wl, n)
                    x0 = t.value(P)
                    bank = proj[u % 2]
                    if u == 7:
                        for k in range(KT):
                            mm = split_mm(bank[:, 0:HV], xh[:, k, bass.ds(x0, P)], xl[:, k, bass.ds(x0, P)],
                                          wh[:, k, GG:GG + HV], wl[:, k, GG:GG + HV], k == 0, k == KT - 1)
                        mm.then_inc(gg_ready.sem, 1)
                        return
                    for c in range(4 if u < 6 else 3):
                        w0 = unit_cols(u) + c * P
                        for k in range(KT):
                            mm = split_mm(bank[:, c * P:(c + 1) * P], wh[:, k, w0:w0 + P], wl[:, k, w0:w0 + P],
                                          xh[:, k, bass.ds(x0, P)], xl[:, k, bass.ds(x0, P)],
                                          k == 0, k == KT - 1)
                    mm.then_inc(proj_ready.sem, 1)

                def grams(t, u):
                    silu_done.wait(pe, t, u + 1)
                    (gram_used.wait(pe, t, u - 1) if u >= 2 else gram_used.wait(pe, t.before(), 5 + u))
                    if t.reg is None and t.off == 0 and u == 0:
                        pe.wait_ge(s_F, 2 * NT)
                    for hh in range(2):
                        mm = pe.matmul(gram[u % 2][:, hh * D:(hh + 1) * D], kq[:, u % 2, hh, 0, :],
                                       kq[:, u % 2, hh, :, :].rearrange("p a n -> p (a n)"), start=True, stop=True)
                    mm.then_inc(gram_ready.sem, 1)

                def norms(t, u):
                    sq_done.wait(pe, t, u + 1)
                    if u == 0:
                        v_done.wait(pe, t.before(), 1)
                    for hh in range(2):
                        for a in range(2):
                            col = t.parity * 24 + a * H + 2 * u + hh
                            mm = pe.matmul(small[:, col:col + 1], sq[:, u % 2, hh, a, :], ones[:, 0:1],
                                           start=True, stop=True)
                    mm.then_inc(norm_ready.sem, 1)

                def v_turn(t):
                    silu_done.wait(pe, t, 7)
                    n2_done.wait(pe, t, 1)
                    for c in range(3):
                        mm = pe.transpose(small[:, T + c * P:T + (c + 1) * P], vT[:, c, :], ident)
                    mm.then_inc(vt_ready.sem, 1)

                def solve(t, k):
                    q = t.parity
                    if k == 1:
                        xf_loaded.wait(pe, t, 16 * NBLK)
                        v_done.wait(pe, t, 1)
                        res_done.wait(pe, t.before(), 1)
                    else:
                        sol_used.wait(pe, t, k - 1)
                    if k == 2:
                        u_masked.wait(pe, t, 2)
                        on_done.wait(pe, t.before(), 1)
                    rhs = V if k == 1 else w
                    for h in range(H):
                        lhsT = Xf[:, h, :] if k % 2 else UP[:, q, h, 1 if k == SOLVE else 0, :]
                        r = V[:, q, h * DV:(h + 1) * DV] if k == 1 else w[:, k % 2, h * DV:(h + 1) * DV]
                        mm = pe.matmul(sol[k % 2][:, h * DV:(h + 1) * DV], lhsT, r, start=True, stop=True)
                    mm.then_inc(sol_ready.sem, 1)

                def turn_o(t):
                    on_done.wait(pe, t, 1)
                    onl_done.wait(pe, t.before(), 1)
                    for c in range(3):
                        mm = pe.transpose(turn[:, c * P:(c + 1) * P], on[:, c * P:(c + 1) * P], ident)
                    mm.then_inc(onT_ready.sem, 1)

                def output(t):
                    onh_done.wait(pe, t, 1)
                    onl_done.wait(pe, t, 1)
                    if t.reg is None and t.off == 0:
                        pe.wait_ge(s_wh, 5)
                        pe.wait_ge(s_wl, 5)
                    sol_used.wait(pe, t, SOLVE - 1)
                    for c in range(3):
                        mm = split_mm(sol[1][:, 0:D], onh[:, c, :], onl[:, c, :], woh[:, c, :], wol[:, c, :],
                                      c == 0, c == 2)
                    mm.then_inc(wo_ready.sem, 1)

                def front(t, tb, tf):
                    for u in range(7):
                        if t is not None and u == 0:
                            project(t, 0)
                        if tf is not None and u == 0:
                            solve(tf, 1)
                        if t is not None:
                            project(t, u + 1)
                        if tf is not None and u == 0:
                            solve(tf, 2)
                        if tb is not None and u == 0:
                            v_turn(tb)
                        if tf is not None and u < 2:
                            solve(tf, 3 + u)
                        if tf is not None and u == 4:
                            turn_o(tf)
                        if t is not None and u > 0:
                            grams(t, u - 1)
                            norms(t, u - 1)
                        if tf is not None and u == 5:
                            output(tf)

                woven_tiles(pe, front)

            @block.scalar
            def _(act):
                act.wait_ge(s_x, 16)
                act.activation(xh[:], xT32[:], ACT.Copy).then_inc(s_xh, 1)
                for i in range(NW):
                    act.wait_ge(s_w[i], 16)
                    act.activation(wh[:, :, wcut[i]:wcut[i + 1]], w32[:, :, wcut[i]:wcut[i + 1]], ACT.Copy,
                                   scale=WS).then_inc(s_wh, 1)
                    if i == 0:
                        act.wait_ge(s_c, 16 * 6)
                        act.activation(s1c[:, 0, :], alog[:], ACT.Exp).then_inc(s_ealog, 1)
                        act.wait_ge(s_na, 1)
                        act.activation(s1a[:], s1a[:], ACT.Exp).then_inc(s_ea, 1)
                        act.wait_ge(s_ba_ev, 1)
                        act.activation(beta[:], ba[:, :, 0:H], ACT.Exp, scale=-1.0).then_inc(s_eb, 1)
                act.wait_ge(s_wo, 16)
                act.activation(woh[:], wo32[:], ACT.Copy, scale=WS).then_inc(s_wh, 1)
                for t in range(NT):
                    for hh in range(2):
                        act.wait_ge(s_D, 2 * t + hh + 1)
                        act.activation(F[:, t, hh * 6:hh * 6 + 6, :].rearrange("p h t -> p (h t)"),
                                       gram[hh][:, 0:6 * T], ACT.Exp).then_inc(s_F, 1)

                def taps(t, u):
                    proj_ready.wait(act, t, u + 1)
                    (silu_done.wait(act, t, u - 1) if u >= 2 else silu_done.wait(act, t.before(), 7))
                    for dst, tap in ((acc, 0), (far, 3)):
                        for c in range(4 if u < 6 else 3):
                            i = act.activation(dst[:, u % 2, c, :], proj[u % 2][:, c * P:(c + 1) * P], ACT.Copy,
                                               scale=cw[:, 4 * u + c, 3 - tap:4 - tap])
                    i.then_inc(tap_done.sem, 1)

                def silu(t, u):
                    summed.wait(act, t, u + 1)
                    if u < 6:
                        (gram_ready.wait(act, t, u - 1) if u >= 2 else gram_ready.wait(act, t.before(), 5 + u))
                        (sq_done.wait(act, t, u - 1) if u >= 2 else sq_done.wait(act, t.before(), 5 + u))
                        act.activation(kq[:, u % 2].rearrange("p a b n -> p (a b n)"),
                                       acc[:, u % 2].rearrange("p c n -> p (c n)"), ACT.Silu,
                                       scale=1 / WS).then_inc(silu_done.sem, 1)
                    else:
                        vt_ready.wait(act, t.before(), 1)
                        act.activation(vT[:], acc[:, u % 2, 0:3, :], ACT.Silu, scale=1 / WS).then_inc(silu_done.sem, 1)

                def square(t, u):
                    silu_done.wait(act, t, u + 1)
                    (norm_ready.wait(act, t, u - 1) if u >= 2 else norm_ready.wait(act, t.before(), 5 + u))
                    act.activation(sq[:, u % 2], kq[:, u % 2], ACT.Square).then_inc(sq_done.sem, 1)

                def gate(t):
                    gg_ready.wait(act, t, 1)
                    on_done.wait(act, t.before(2), 1)
                    act.activation(gs[:, t.parity, :], proj[1][:, 0:HV], ACT.Silu, scale=1 / WS).then_inc(gg_done.sem, 1)

                def front(t, tb, tf):
                    if t is not None:
                        taps(t, 0)
                    for u in range(7):
                        if t is not None:
                            if u < 6:
                                taps(t, u + 1)
                            else:
                                gate(t)
                        if tf is not None and u == 4:
                            onT_ready.wait(act, tf, 1)
                            wo_ready.wait(act, tf.before(), 1)
                            act.activation(onh[:].rearrange("p c n -> p (c n)"), turn[:, 0:HV], ACT.Copy).then_inc(onh_done.sem, 1)
                        if t is not None:
                            silu(t, u)
                            if u < 6:
                                square(t, u)
                        if tf is not None and u == 1:
                            sol_ready.wait(act, tf, SOLVE)
                            act.activation(sqo[:], sol[0][:, 0:HV], ACT.Square,
                                           scale=DV ** -0.5).then_inc(sqo_done.sem, 1)

                woven_tiles(act, front)

            @block.gpsimd
            def _(pool):
                ch = Chain(pool, pch)
                pool.memset(ones[:], 1.0)
                pool.memset(epsc[:], EPS)
                ch(pool.memset(mhalf[:], -0.5))
                pool.memset(UP[:, 0], 0.0).then_inc(s_zero, 1)
                pool.memset(UP[:, 1], 0.0).then_inc(s_zero, 1)
                pool.memset(Xf[:], 0.0).then_inc(s_zero, 1)
                pool.wait_ge(s_c, 16 * 6)
                for t in range(NT):
                    pool.wait_ge(s_g, 1)
                    if t >= 2:
                        pool.wait_ge(s_D, 2 * t - 2)
                    pool.tensor_tensor(gL[:, t % 2], over(g[:, t, :], 2, [P, H, T]), over(upto, 1, [P, H, T]),
                                       ALU.mult).then_inc(s_gL, 1)
                fc, ec = TileChain(pool, ptile), TileChain(pool, pend)

                def scale_u(tb):
                    gram_used.wait(pool, tb, 6)
                    bp_done.wait(pool, tb, 1)
                    summed.wait(pool, tb, 7)
                    rs_done.wait(pool, tb.before(2), 1)
                    q = tb.parity
                    for b in range(2):
                        r = slice(b * T, (b + 1) * T)
                        pool.tensor_tensor(UP[r, q, :, 0, r], UP[r, q, :, 0, r],
                                           over(Bp[r, q, :], 2, [T, H, T]), ALU.mult).then_inc(u_scaled.sem, 1)
                    u_scaled.wait(pool, tb, 2)

                def sum_taps(t, u):
                    conv_done.wait(pool, t, u + 1)
                    n = 4 if u < 6 else 3
                    a, f = (x[:, u % 2, 0:n].rearrange("p c (b t) -> p (c b) t", b=2) for x in (acc, far))
                    pool.tensor_tensor(a[:, :, 3:], a[:, :, 3:], f[:, :, 0:T - 3], ALU.add).then_inc(summed.sem, 1)

                def head_scales(t):
                    fc.start(t)
                    q = t.parity
                    n2_done.wait(pool, t, 1)
                    fc(pool.tensor_tensor(rn[:, q], n2[:, q], mhalf[:], ALU.pow))
                    pool.tensor_tensor(absk[:, q], n2[:, q, 0:H], rn[:, q, 0:H], ALU.mult).then_inc(rn_done.sem, 1)

                def rms(tf):
                    ec.start(tf)
                    q = tf.parity
                    ms_done.wait(pool, tf, 1)
                    ec(pool.tensor_tensor(r2[:], rn[:, q, H:], rn[:, q, H:], ALU.mult))
                    ec(pool.tensor_tensor(r2[:], r2[:], ms[:], ALU.mult))
                    ec(pool.tensor_tensor(r2[:], r2[:], epsc[:], ALU.add))
                    ec(pool.tensor_tensor(r2[:], r2[:], mhalf[:, 0:H], ALU.pow))
                    pool.tensor_tensor(rr[:], r2[:], rn[:, q, H:], ALU.mult).then_inc(rr_done.sem, 1)

                def deviation(tf):
                    mv_done.wait(pool, tf, 1)
                    ec(pool.tensor_tensor(rs[:], mv[:, 1:2], epsc[:, 0:1], ALU.add))
                    pool.tensor_tensor(rs[:], rs[:], mhalf[:, 0:1], ALU.pow).then_inc(rs_done.sem, 1)

                def front(t, tb, tf):
                    if tb is not None:
                        scale_u(tb)
                        head_scales(tb)
                    if t is not None:
                        sum_taps(t, 0)
                        sum_taps(t, 1)
                        sum_taps(t, 2)
                    if tf is not None:
                        rms(tf)
                    if t is not None:
                        sum_taps(t, 3)
                    if tb is not None:
                        if t is not None:
                            summed.wait(pool, t, 4)
                        else:
                            rr_done.wait(pool, tf, 1)
                        mask_u(tb)
                    if t is not None:
                        sum_taps(t, 4)
                    if tb is not None:
                        gate_w(tb)
                    if t is not None:
                        sum_taps(t, 5)
                        sum_taps(t, 6)
                    if tf is not None:
                        deviation(tf)

                def mask_u(tb):
                    ud_stored.wait(pool, tb, 16 * NBLK)
                    for b in range(2):
                        r = slice(b * T, (b + 1) * T)
                        pool.tensor_tensor(UP[r, tb.parity, :, 0, r], UP[r, tb.parity, :, 0, r],
                                           over(offblk[r, :], 1, [T, H, T]), ALU.mult).then_inc(u_masked.sem, 1)
                    u_masked.wait(pool, tb, 2)

                def gate_w(tb):
                    gg_done.wait(pool, tb, 1)
                    v = gs[:, tb.parity].rearrange("p (h d) -> p h d", h=H)
                    pool.tensor_tensor(v, v, over(normw[:], 1, [P, H, DV]), ALU.mult).then_inc(gsn_done.sem, 1)

                woven_tiles(pool, front)

            @block.vector
            def _(v):
                ch = Chain(v, dch)
                v.wait_ge(s_xh, 1)
                v.tensor_tensor(xl[:], xT32[:], xh[:], ALU.subtract).then_inc(s_xl, 1)

                def w_low(i):
                    v.wait_ge(s_wh, i + 1)
                    c = slice(wcut[i], wcut[i + 1])
                    v.scalar_tensor_tensor(wl[:, :, c], w32[:, :, c], WS, wh[:, :, c], ALU.mult,
                                           ALU.subtract).then_inc(s_wl, 1)

                w_low(0)
                v.wait_ge(s_c, 16 * 6)
                v.wait_ge(s_ba, 1)
                v.tensor_scalar(ba[:].rearrange("p t h -> p (t h)"), proj[0][:, 0:NT * 24], 1 / WS, None,
                                ALU.mult).then_inc(s_ba_ev, 1)
                v.wait_ge(s_ba_ev, 1)
                a = ba[:, :, H:2 * H]
                ch(v.tensor_tensor(a, a, over(dtb[:], 1, [P, NT, H]), ALU.add))
                ch(v.tensor_scalar(s1b[:], a, -1.0, None, ALU.mult))
                v.tensor_tensor(s1a[:], a, s1b[:], ALU.min).then_inc(s_na, 1)
                ch(v.tensor_scalar(g[:], a, 0.0, None, ALU.max))
                v.wait_ge(s_ea, 1)
                ch(v.tensor_scalar(s1b[:], s1a[:], 2.0, None, ALU.add))
                ch(v.reciprocal(s1b[:], s1b[:]))
                ch(v.tensor_tensor(s1a[:], s1a[:], s1b[:], ALU.mult))
                ch(v.tensor_tensor(s1b[:], s1a[:], s1a[:], ALU.mult))
                v.wait_ge(s_ealog, 1)
                ch(v.tensor_scalar(alog[:], s1c[:, 0, :], -1.0, None, ALU.mult))
                ch(v.tensor_scalar(s1c[:], s1b[:], 1 / 17.0, None, ALU.mult))
                for n in (15, 13, 11, 9, 7, 5, 3):
                    ch(v.scalar_tensor_tensor(s1c[:], s1c[:], 1.0 / n, s1b[:], ALU.add, ALU.mult))
                ch(v.scalar_tensor_tensor(s1c[:], s1c[:], 1.0, s1a[:], ALU.add, ALU.mult))
                ch(v.scalar_tensor_tensor(g[:], s1c[:], 2.0, g[:], ALU.mult, ALU.add))
                v.tensor_tensor(g[:], g[:], over(alog[:], 1, [P, NT, H]), ALU.mult).then_inc(s_g, 1)
                v.wait_ge(s_eb, 1)
                ch(v.tensor_scalar(beta[:], beta[:], 1.0, None, ALU.add))
                v.reciprocal(beta[:], beta[:]).then_inc(s_beta, 1)
                for i in range(1, NW):
                    w_low(i)
                v.wait_ge(s_wh, 5)
                v.scalar_tensor_tensor(wol[:], wo32[:], WS, woh[:], ALU.mult, ALU.subtract).then_inc(s_wl, 1)
                for t in range(NT):
                    v.wait_ge(s_F, 2 * t + 2)
                    i = v.tensor_tensor(F[:, t], F[:, t], over(incl, 1, [P, H, T]), ALU.mult)
                i.then_inc(s_Fm, 1)
                v.wait_ge(s_Fm, 1)
                v.wait_ge(s_zero, 3)
                v.wait_ge(s_X, 16)
                v.wait_ge(s_beta, 1)

                cc, bc, ec = TileChain(v, dtile), TileChain(v, dback), TileChain(v, dend)

                def conv(t, u):
                    tap_done.wait(v, t, u + 1)
                    n = 4 if u < 6 else 3
                    marks = [0] * n
                    for tap in range(1, 3):
                        for c in range(n):
                            if tap > 1:
                                cc.wait(marks[c])
                            src = proj[u % 2][:, c * P:(c + 1) * P].rearrange("p (b t) -> p b t", b=2)[:, :, 0:T - tap]
                            dst = acc[:, u % 2, c, :].rearrange("p (b t) -> p b t", b=2)[:, :, tap:T]
                            i = v.scalar_tensor_tensor(dst, src, cw[:, 4 * u + c, 3 - tap:4 - tap], dst, ALU.mult, ALU.add)
                            if tap < 2:
                                marks[c] = cc.mark(i)
                            elif c == n - 1:
                                i.then_inc(conv_done.sem, 1)
                            yield

                def gram_use(t, u):
                    gram_ready.wait(v, t, u + 1)
                    q = t.parity
                    if u == 0:
                        sol_ready.wait(v, t.before(2), SOLVE)
                    for b in range(2):
                        r = slice(b * T, (b + 1) * T)
                        for a in range(2):
                            src = gram[u % 2][r, :].rearrange("p (h a n) -> p h a n", h=2, a=2)[:, :, a, r]
                            i = v.tensor_tensor(UP[r, q, 2 * u:2 * u + 2, a, r], src,
                                                F[r, bass.ds(t.value(1), 1), 2 * u:2 * u + 2, :].rearrange("p a h t -> p (a h) t"),
                                                ALU.mult)
                            if b == a == 1:
                                i.then_inc(gram_used.sem, 1)
                            yield

                def norms_out(t):
                    norm_ready.wait(v, t, 6)
                    q = t.parity
                    v.tensor_scalar(n2[:, q], small[:, q * 24:q * 24 + 24], 1e-6, None, ALU.add).then_inc(n2_done.sem, 1)
                    n2_done.wait(v, t, 1)
                    cc(v.reciprocal(Bp[:, q], n2[:, q, 0:H]))
                    v.tensor_tensor(Bp[:, q], Bp[:, q], beta[:, bass.ds(t.value(1), 1), :].rearrange("p a h -> p (a h)"),
                                    ALU.mult).then_inc(bp_done.sem, 1)

                def v_scale(t):
                    vt_ready.wait(v, t, 1)
                    rn_done.wait(v, t, 1)
                    q = t.parity
                    v.tensor_tensor(V[:, q].rearrange("p (h d) -> p h d", h=H),
                                    small[:, T:T + HV].rearrange("p (h d) -> p h d", h=H),
                                    over(absk[:, q], 2, [P, H, DV]), ALU.mult).then_inc(v_done.sem, 1)

                def eliminate(t, s0, s1):
                    if s0 == 0:
                        ue_loaded.wait(v, t, 32)
                        yd_stored.wait(v, t.before(), 32)
                        bc.mark(v.tensor_copy(Yn[0:2 * YP], eyes[0:2 * YP]))
                        yield
                    for s in range(s0, s1):
                        n, m = s // 2 + 1, BLK - 1 - s
                        bc.wait()
                        bc.mark(v.tensor_tensor(Yt[0:2 * YP, 0:n, 0:m], Yn[0:2 * YP, 0:n, s:s + 1].broadcast_to([2 * YP, n, m]),
                                                Ue[0:2 * YP, s:s + 1, s + 1:].broadcast_to([2 * YP, n, m]), ALU.mult))
                        yield
                        bc.wait()
                        i = v.tensor_tensor(Yn[0:2 * YP, 0:n, s + 1:], Yn[0:2 * YP, 0:n, s + 1:], Yt[0:2 * YP, 0:n, 0:m],
                                            ALU.subtract)
                        if s == BLK - 2:
                            i.then_inc(y_done.sem, 1)
                        else:
                            bc.mark(i)
                        yield

                def sol_use(t, k):
                    sol_ready.wait(v, t, k)
                    q = t.parity
                    src, dst = sol[k % 2][:, 0:HV], w[:, (k + 1) % 2]
                    if k == SOLVE - 1:
                        i = v.tensor_tensor(dst.rearrange("p (h d) -> p h d", h=H), src.rearrange("p (h d) -> p h d", h=H),
                                            over(Bp[:, q], 2, [P, H, DV]), ALU.mult)
                    elif k % 2:
                        i = v.tensor_copy(dst, src)
                    else:
                        i = v.tensor_tensor(dst, V[:, q], src, ALU.subtract)
                    i.then_inc(sol_used.sem, 1)

                def end(t, part):
                    q = t.parity
                    xt = X[:, bass.ds(t.value(1), 1), :].rearrange("p a d -> p (a d)")
                    if part == 1:
                        ec.start(t)
                        sqo_done.wait(v, t, 1)
                        v.tensor_reduce(ms[:], sqo[:].rearrange("p (h d) -> p h d", h=H), AX.X, ALU.add).then_inc(ms_done.sem, 1)
                    elif part == 2:
                        rr_done.wait(v, t, 1)
                        onT_ready.wait(v, t.before(), 1)
                        ec(v.tensor_tensor(on[:].rearrange("p (h d) -> p h d", h=H),
                                           sol[0][:, 0:HV].rearrange("p (h d) -> p h d", h=H),
                                           over(rr[:], 2, [P, H, DV]), ALU.mult))
                        gsn_done.wait(v, t, 1)
                        v.tensor_tensor(on[:], on[:], gs[:, q], ALU.mult).then_inc(on_done.sem, 1)
                    elif part == 3:
                        onh_done.wait(v, t, 1)
                        wo_ready.wait(v, t.before(), 1)
                        v.tensor_tensor(onl[:].rearrange("p c n -> p (c n)"), turn[:, 0:HV],
                                        onh[:].rearrange("p c n -> p (c n)"), ALU.subtract).then_inc(onl_done.sem, 1)
                    elif part == 4:
                        wo_ready.wait(v, t, 1)
                        v.scalar_tensor_tensor(y[:], sol[1][:, 0:D], 1 / WS, xt, ALU.mult, ALU.add).then_inc(res_done.sem, 1)
                        res_done.wait(v, t, 1)
                        ec(v.bn_stats(st[:], y[:]))
                        v.memset(spare[:], 0.0)
                        v.bn_aggr(mv[:], st[:]).then_inc(mv_done.sem, 1)
                    else:
                        rs_done.wait(v, t, 1)
                        v.tensor_scalar(xt, y[:], mv[:, 0:1], rs[:, 0:1], ALU.subtract, ALU.mult).then_inc(x1_done.sem, 1)

                def ending(tf, part):
                    if tf is not None:
                        end(tf, part)
                        yield

                def front(t, tb, tf):
                    elim = {0: (5, 9), 1: (9, 16), 2: (16, 22), 3: (22, 27), 4: (27, 31)}
                    ends = {2: 2, 6: 5}
                    early_ends = {5: 3, 6: 4}
                    if t is not None:
                        cc.start(t)
                    if tb is not None:
                        bc.start(tb)
                    for u in range(7):
                        if tf is not None and u == 0:
                            sol_use(tf, 1)
                        if t is not None and u == 0:
                            weave(conv(t, 0))
                        if tf is not None and u == 0:
                            sol_use(tf, 2)
                        if u == 0:
                            weave(conv(t, 1) if t is not None else iter(()),
                                  eliminate(tb, 0, 5) if tb is not None else iter(()))
                        if tf is not None and u == 0:
                            sol_use(tf, 3)
                        if tb is not None and u == 0:
                            v_scale(tb)
                        if tf is not None and u in early_ends:
                            end(tf, early_ends[u])
                        work = []
                        if t is not None and u > 0:
                            work.append(chain(conv(t, u + 1) if u < 6 else (), ending(tf, 1) if u == 1 else (),
                                              gram_use(t, u - 1)))
                        elif u == 1:
                            weave(ending(tf, 1))
                        if tb is not None and u in elim:
                            work.append(eliminate(tb, *elim[u]))
                        weave(*work)
                        if t is not None and u == 6:
                            norms_out(t)
                        if tf is not None and u in ends:
                            end(tf, ends[u])

                woven_tiles(v, front)


G = 8
UN = 4
NH2 = 32
CH2 = 4 * 512
F8MAX = 448.0
QSCALE = P ** -0.5


def skewed_units(eng, ahead, unit):
    ahead(Tile(0))

    def whole(n):
        t = n // UN
        unit(Tile(n - 1) if n else None, Tile(n), Tile(n + 1) if n + 1 < UN * NT else None,
             Tile(t - 1) if n % UN == 1 and t else None)

    for n in range(2 * UN):
        whole(n)
    with eng.Fori(0, NT - 3) as i:
        for u in range(2 * UN, 3 * UN):
            unit(Tile(u - 1, i, UN), Tile(u, i, UN), Tile(u + 1, i, UN), Tile(1, i, 1) if u % UN == 1 else None)
    for n in range(UN * (NT - 1), UN * NT):
        whole(n)
    unit(Tile(UN * NT - 1), None, None, None)
    unit(None, None, None, Tile(NT - 1))


def last_unit(t):
    return Tile(t.off * UN + UN - 1, t.reg, UN)


def stage2(nc, io, X):
    with ExitStack() as ctx:
        def sb(name, shape, dt=F32):
            return ctx.enter_context(nc.sbuf_tensor(name, [P] + shape, dt))

        def pb(name):
            return ctx.enter_context(nc.psum_tensor(name, [P, 512], F32))

        def sem(name):
            return ctx.enter_context(nc.semaphore(name))

        def sig(name, per):
            return Signal(sem(name), per)

        NSLOT = 4
        raw = sb("raw", [NSLOT, KT, 512])
        w2h = sb("w2h", [UN, 4, KT, 512], F16)
        w2l = sb("w2l", [UN, 4, KT, 512], F16)
        wp = sb("wp", [NH2, D], F16)
        ch_ = sb("ctxh", [KT, NTOK], F16)
        cl_ = sb("ctxl", [KT, NTOK], F16)
        wmean = sb("wmean", [NSLOT, 8])
        ident = sb("ident2", [P])
        prm = sb("prm", [12 + 8 + 6 + 32])
        lnw, lnb = prm[:, 0:2], prm[:, 2:4]
        insc = prm[:, 4:12]
        lnp = prm[:, 12:20]
        wsc = prm[:, 20:26]
        smooth = prm[:, 26:58]
        rinsc = sb("rinsc", [8])
        rsm = sb("rsm", [NH2])
        pscale = sb("pscale", [1])
        epsw = sb("epsw", [4])
        mhalf = sb("mhalf2", [4])
        xn = sb("xn", [NT, D])
        lnT = sb("lnT", [NT, KT, P])
        xq = sb("xq", [NT, 4, KT, P], BF16)
        mag = sb("mag", [8, P], BF16)
        st = sb("st2", [NT, 6])
        mv = sb("mv2", [NT, 2])
        rs = sb("rs2", [NT, 1])
        spare = sb("spare2", [1])
        sq = sb("sq2", [3, 4, P])
        qn = sb("qn", [3, 512])
        ms = sb("ms2", [3, 4])
        rq = sb("rq", [3, 4])
        qT = sb("qT", [2, 4, 2, 2, T])
        kT = sb("kT", [2, 4, P])
        V = sb("V2", [2, 512])
        mx = sb("mx", [8])
        sc = sb("sc", [2, 512])
        sm = sb("sm", [8])
        rc = sb("rc", [8])
        PT = sb("PT", [512])
        cat = sb("cat", [NH2, P], BF16)
        cmag = sb("cmag", [8, P], BF16)
        y = sb("y2", [D])

        pj = [pb("pjA"), pb("pjB"), pb("pjC")]
        tq, scb, ptb = pb("tq"), pb("scb"), pb("ptb")
        pv = [pb("pv0"), pb("pv1")]

        s_prm, s_id = sem("prm_loaded"), sem("ident_loaded")
        NCH = UN * 4 + 2 + 8
        s_raw = [sem(f"raw_loaded{i}") for i in range(NSLOT)]
        s_scaled, s_centered, s_hi, s_lo = sem("w_scaled"), sem("w_centered"), sem("w_hi"), sem("w_lo")
        s_mean, s_xs = sem("w_mean"), sem("x_by_input")
        s_c2 = sem("const2_done")
        s_mv, s_rs, s_xn, s_xT, s_xq = sem("pre_mv"), sem("pre_rs"), sem("pre_xn"), sem("pre_xT"), sem("pre_xq")
        s_ln = sem("pre_ln")
        dch, pch = sem("dve_setup2"), sem("pool_setup2")
        dun, pun, dti, pti = sem("dve_unit"), sem("pool_unit"), sem("dve_tile2"), sem("pool_tile2")
        dqu = sem("dve_quantise")
        q_ready, v_ready = sig("q_ready", 3), sig("v_ready", 1)
        ms_done, rq_done, qn_done = sig("ms2_done", 3), sig("rq_done", 3), sig("qn_done", 3)
        tq_ready, tq_used, v_used = sig("tq_ready", 3), sig("tq_used", 3), sig("v_used", 1)
        sc_ready, sub_done, exp_done, p_done = sig("sc_ready", 1), sig("sub_done", 1), sig("exp_done", 1), sig("p_done", 1)
        rc_done = sig("rc_done", 1)
        pt_ready, pt_used, pv_ready, y_done, cat_done = (sig("pt_ready", 1), sig("pt_used", 1), sig("pv_ready", 1),
                                                         sig("y2_done", 1), sig("cat_done", 1))
        wp_ready, mv_done, rs_done, x2_done, yt_done = (sig("wp_ready", 1), sig("mv2_done", 1), sig("rs2_done", 1),
                                                        sig("x2_done", 1), sig("yt_done", 1))

        def turned(c):
            return pj[c] if c else tq

        def is_self(u):
            return u < UN // 2

        order = [("w", u, c) for u in range(2) for c in range(4)] + [("ctx", k, 0) for k in range(2)] + \
                [("w", u, c) for u in range(2, 4) for c in range(4)] + [("wp", k, 0) for k in range(8)]
        done_before = {}
        for n, key in enumerate(order):
            done_before[key] = n + 1

        chunks = lambda what, *units: [n for n, k in enumerate(order) if k[0] == what and (k[1] in units or not units)]
        cuts = {0: chunks("w", 1), 1: chunks("ctx") + chunks("w", 2), 2: chunks("w", 3)}
        proj_cuts = {3 + j: chunks("wp")[4 * j:4 * j + 4] for j in range(2)}
        quants = {2: [1], 3: [2], 4: [3, 4], 5: [5], 6: [6, 7]}

        def with_setup(step, unit):
            def both(l, n, m, te):
                if n is not None and n.reg is None:
                    step(n.off)
                unit(l, n, m, te)
            return both

        with nc.Block() as block:
            @block.sync
            def _(sp):
                sp.dma_start(prm[:], io["prm2"]).then_inc(s_prm, 16)
                sp.dma_start(ident[:], io["consts"][:, 0:P]).then_inc(s_id, 16)
                w2 = io["w2"].rearrange("(k p) n -> p k n", p=P)
                cx = io["ctxT"].rearrange("(k p) n -> p k n", p=P)
                wpv = io["wproj"].rearrange("(n p) c -> p n c", p=P)
                for n, (what, a, b) in enumerate(order):
                    if n >= NSLOT:
                        last = order[n - NSLOT][0]
                        sp.wait_ge(s_hi if last == "wp" else s_lo, n - NSLOT + 1)
                    slot = raw[:, n % NSLOT]
                    if what == "w":
                        src = w2[:, :, a * CH2 + b * 512:a * CH2 + (b + 1) * 512]
                    elif what == "ctx":
                        src = cx[:, :, a * 512:(a + 1) * 512]
                    else:
                        src = wpv[:, a * 4:(a + 1) * 4, :]
                        slot = slot.rearrange("p k n -> p (k n)").rearrange("p (n c) -> p n c", c=D)
                    sp.dma_start(slot, src).then_inc(s_raw[n % NSLOT], 16)

            def raw_here(eng, n):
                eng.wait_ge(s_raw[n % NSLOT], 16 * (n // NSLOT + 1))

            def centered(what, c):
                return what == "w" and c < 3

            @block.tensor
            def _(pe):
                pe.wait_ge(s_id, 16)
                for t in range(NT):
                    pe.wait_ge(s_xn, t + 1)
                    if t >= 2:
                        pe.wait_ge(s_ln, t - 1)
                    for k in range(KT):
                        i = pe.transpose(pj[t % 2][:, k * P:(k + 1) * P], xn[:, t, k * P:(k + 1) * P], ident[:])
                    i.then_inc(s_xT, 1)

                def chunk(n, c):
                    u = n.off % UN
                    if c == 0:
                        v_used.wait(pe, n.before(), 1)
                    elif c == 3:
                        qn_done.wait(pe, n, 1)
                    else:
                        tq_used.wait(pe, n.before(), c + 1)
                    if n.reg is None and n.off < UN:
                        pe.wait_ge(s_lo, done_before[("w", u, c)])
                    if n.reg is None and c == 0 and n.off % UN == 0 and n.off <= 2 * UN:
                        pe.wait_ge(s_xq, n.off // UN + 1 if n.off < 2 * UN else NT)
                    tile = tile_of(n)
                    if is_self(u):
                        s = (0, 0, 2, 3)[c]
                        terms = [(xq[:, bass.ds(tile, 1), s, k, :].rearrange("p a n -> p (a n)"), w[:, u, c, k, :])
                                 for k in range(KT) for w in (w2h, w2l)]
                    elif c < 2:
                        terms = [(xq[:, bass.ds(tile, 1), 1, k, :].rearrange("p a n -> p (a n)"), w[:, u, c, k, :])
                                 for k in range(KT) for w in (w2h, w2l)]
                    else:
                        tok = bass.ds(tile * P, P)
                        terms = [(x, w) for k in range(KT) for x, w in (
                            (ch_[:, k, tok], w2h[:, u, c, k, :]), (ch_[:, k, tok], w2l[:, u, c, k, :]),
                            (cl_[:, k, tok], w2h[:, u, c, k, :]))]
                    for j, (x, w) in enumerate(terms):
                        i = pe.matmul(pj[c % 3][:], x, w, start=j == 0, stop=j == len(terms) - 1)
                    i.then_inc((v_ready if c == 3 else q_ready).sem, 1)

                def tile_of(n):
                    return n.off // UN if n.reg is None else n.reg + n.off // UN

                def turn(n, c):
                    qn_done.wait(pe, n, c + 1)
                    if c == 0:
                        tq_used.wait(pe, n.before(), 1)
                    bank = turned(c)
                    for j in range(4):
                        dst = bank[:, j * P:(j + 1) * P]
                        if c < 2:
                            dst = bank[:, j // 2 * D:(j // 2 + 1) * D].rearrange("p (b h s) -> p h b s", b=2, h=2)[:, j % 2]
                        i = pe.transpose(dst, qn[:, c, j * P:(j + 1) * P], ident[:])
                    i.then_inc(tq_ready.sem, 1)

                def scores(n):
                    tq_used.wait(pe, n, 3)
                    sub_done.wait(pe, n.before(), 1)
                    q = n.parity
                    for g in range(4):
                        for b in range(2):
                            s = slice(b * T, (b + 1) * T)
                            i = pe.matmul(scb[:, g * P + b * T:g * P + (b + 1) * T], qT[:, q, g, b].rearrange("p h s -> p (h s)"),
                                          kT[:, q, g, s], start=True, stop=True)
                    i.then_inc(sc_ready.sem, 1)

                def turn_p(n, te):
                    p_done.wait(pe, n, 1)
                    pt_used.wait(pe, n.before(), 1)
                    if te is not None:
                        yt_done.wait(pe, te, 1)
                    for g in range(4):
                        i = pe.transpose(ptb[:, g * P:(g + 1) * P], sc[:, n.parity, g * P:(g + 1) * P], ident[:])
                    i.then_inc(pt_ready.sem, 1)

                def values(n):
                    pt_used.wait(pe, n, 1)
                    v_used.wait(pe, n, 1)
                    y_done.wait(pe, n.before(), 1)
                    for g in range(4):
                        for b in range(2):
                            r = slice(b * T, (b + 1) * T)
                            i = pe.matmul(pv[b][:, g * P:(g + 1) * P], V[r, n.parity, g * P:(g + 1) * P],
                                          PT[r, g * P:(g + 1) * P], start=True, stop=True)
                    i.then_inc(pv_ready.sem, 1)

                def project(te, l):
                    cat_done.wait(pe, last_unit(te), 1)
                    pt_used.wait(pe, last_unit(te) if l is None else l, 1)
                    if te.reg is None and te.off == 0:
                        pe.wait_ge(s_hi, NCH)
                    for h in range(NH2):
                        i = pe.matmul(ptb[:, 0:D], cat[:, h, :], wp[:, h, :], start=h == 0, stop=h == NH2 - 1)
                    i.then_inc(wp_ready.sem, 1)

                def ahead(n):
                    for c in range(4):
                        chunk(n, c)
                    for c in range(3):
                        turn(n, c)
                    scores(n)

                def unit(l, n, m, te):
                    if m is not None:
                        chunk(m, 0)
                        chunk(m, 1)
                        chunk(m, 2)
                    if te is not None:
                        project(te, l)
                    if l is not None:
                        values(l)
                    if m is not None:
                        turn(m, 0)
                        chunk(m, 3)
                        turn(m, 1)
                        turn(m, 2)
                    if n is not None:
                        turn_p(n, te)
                    if m is not None:
                        scores(m)

                skewed_units(pe, ahead, unit)

            @block.scalar
            def _(act):
                act.wait_ge(s_prm, 16)
                for t in range(NT):
                    act.wait_ge(s_xT, t + 1)
                    for k in range(KT):
                        i = act.activation(lnT[:, t, k], pj[t % 2][:, k * P:(k + 1) * P], ACT.Identity,
                                           bias=lnb[:, k:k + 1], scale=lnw[:, k:k + 1])
                    i.then_inc(s_ln, 1)

                def by_input(n):
                    what, a, b = order[n]
                    raw_here(act, n)
                    slot = raw[:, n % NSLOT]
                    if what == "w" and (is_self(a) or b < 2):
                        s = (1 if not is_self(a) else 0, 1 if not is_self(a) else 0, 2, 3)[b]
                        for k in range(KT):
                            i = act.activation(slot[:, k, :], slot[:, k, :], ACT.Copy, scale=insc[:, 2 * s + k:2 * s + k + 1])
                        i.then_inc(s_scaled, 1)

                def high(n):
                    what, a, b = order[n]
                    slot = raw[:, n % NSLOT]
                    if what == "w" and (is_self(a) or b < 2):
                        act.wait_ge(s_scaled, n_scaled(order, n))
                    if centered(what, b):
                        act.wait_ge(s_centered, n_centered(order, n))
                    k = WS if what == "w" and not is_self(a) and b >= 2 else 1.0
                    if what == "w":
                        dst = w2h[:, a, b]
                    elif what == "ctx":
                        dst = ch_[:, :, a * 512:(a + 1) * 512]
                    else:
                        dst = wp[:, a * 4:(a + 1) * 4, :].rearrange("p n c -> p (n c)")
                        slot = slot.rearrange("p k n -> p (k n)")
                    act.activation(dst, slot, ACT.Copy, scale=k).then_inc(s_hi, 1)

                def cut(ns):
                    for j, n in enumerate(ns):
                        if j == 0:
                            by_input(n)
                        if j + 1 < len(ns):
                            by_input(ns[j + 1])
                        high(n)

                def step(n):
                    cut(cuts.get(n, []))
                    cut(proj_cuts.get(n, []))

                cut(chunks("w", 0))

                def mean_square(n, c):
                    q_ready.wait(act, n, c + 1)
                    rq_done.wait(act, n.before(), c + 1)
                    for h in range(4):
                        i = act.activation(sq[:, c, h], pj[c][:, h * P:(h + 1) * P], ACT.Square, scale=P ** -0.5,
                                           accum_out=ms[:, c, h:h + 1])
                    i.then_inc(ms_done.sem, 1)

                def affine(n, c):
                    tq_ready.wait(act, n, c + 1)
                    if c == 0:
                        sc_ready.wait(act, n.before(2), 1)
                    j = (0 if is_self(n.off % UN) else 1) + (2 if c == 2 else 0)
                    if c == 2:
                        dst = kT[:, n.parity].rearrange("p g n -> p (g n)")
                    else:
                        dst = qT[:, n.parity, 2 * c:2 * c + 2].rearrange("p g b h s -> p (g b h s)")
                    act.activation(dst, turned(c)[:], ACT.Identity, bias=lnp[:, 2 * j + 1:2 * j + 2],
                                   scale=lnp[:, 2 * j:2 * j + 1]).then_inc(tq_used.sem, 1)

                def copy_v(n):
                    v_ready.wait(act, n, 1)
                    pv_ready.wait(act, n.before(2), 1)
                    act.activation(V[:, n.parity], pj[0][:], ACT.Copy).then_inc(v_used.sem, 1)

                def ahead(n):
                    for c in range(3):
                        mean_square(n, c)
                    copy_v(n)
                    for c in range(3):
                        affine(n, c)

                def unit(l, n, m, te):
                    if m is not None:
                        mean_square(m, 0)
                        mean_square(m, 1)
                        mean_square(m, 2)
                    if n is not None:
                        sub_done.wait(act, n, 1)
                        act.activation(sc[:, n.parity], sc[:, n.parity], ACT.Exp, scale=QSCALE).then_inc(exp_done.sem, 1)
                    if m is not None:
                        affine(m, 0)
                        affine(m, 1)
                        affine(m, 2)
                        copy_v(m)
                    if n is not None:
                        pt_ready.wait(act, n, 1)
                        pv_ready.wait(act, n.before(), 1)
                        act.activation(PT[:], ptb[:], ACT.Copy).then_inc(pt_used.sem, 1)

                skewed_units(act, ahead, with_setup(step, unit))

            @block.gpsimd
            def _(pool):
                ch = Chain(pool, pch)
                ch(pool.memset(mhalf[:], -0.5))
                pool.wait_ge(s_c2, 1)
                for t in range(NT):
                    pool.wait_ge(s_mv, t + 1)
                    ch(pool.tensor_scalar(rs[:, t], mv[:, t, 1:2], EPS, 1.0, ALU.add, ALU.mult))
                    pool.tensor_tensor(rs[:, t], rs[:, t], mhalf[:, 0:1], ALU.pow).then_inc(s_rs, 1)

                def by_input(t):
                    pool.wait_ge(s_ln, t + 1)
                    for s in range(4):
                        i = pool.tensor_tensor(xq[:, t, s], lnT[:, t], over(rinsc[:, 2 * s:2 * s + 2], 2, [P, KT, P]), ALU.mult)
                    i.then_inc(s_xs, 1)

                def center(ns):
                    for n in ns:
                        if centered(*order[n][::2]):
                            heads = raw[:, n % NSLOT].rearrange("p k (h d) -> p (k h) d", d=P)
                            pool.wait_ge(s_mean, n_centered(order, n))
                            pool.tensor_tensor(heads, heads, over(wmean[:, n % NSLOT], 2, [P, 8, P]),
                                               ALU.add).then_inc(s_centered, 1)

                def step(n):
                    center(cuts.get(n, []))
                    for t in quants.get(n + 1, []):
                        by_input(t)

                by_input(0)
                center(chunks("w", 0))
                pc = TileChain(pool, pun)

                def inv_dev(n, c):
                    ms_done.wait(pool, n, c + 1)
                    j = (0 if is_self(n.off % UN) else 1) + (2 if c == 2 else 0)
                    pc(pool.tensor_tensor(rq[:, c], ms[:, c], epsw[:, j:j + 1].broadcast_to([P, 4]), ALU.add))
                    pool.tensor_tensor(rq[:, c], rq[:, c], mhalf[:], ALU.pow).then_inc(rq_done.sem, 1)

                def ahead(n):
                    pc.start(n)
                    for c in range(3):
                        inv_dev(n, c)

                tc = TileChain(pool, pti)

                def unit(l, n, m, te):
                    if m is not None:
                        pc.start(m)
                        inv_dev(m, 0)
                        inv_dev(m, 1)
                        inv_dev(m, 2)
                    if n is not None:
                        rc_done.wait(pool, n, 1)
                        v = sc[:, n.parity].rearrange("p (g t) -> p g t", t=T)
                        pool.tensor_tensor(v, v, over(rc[:], 2, [P, 8, T]), ALU.mult).then_inc(p_done.sem, 1)
                    if te is not None:
                        tc.start(te)
                        mv_done.wait(pool, te, 1)
                        tc(pool.tensor_tensor(rs[:, 0], mv[:, 0, 1:2], spare[:], ALU.add))
                        pool.tensor_tensor(rs[:, 0], rs[:, 0], mhalf[:, 0:1], ALU.pow).then_inc(rs_done.sem, 1)

                skewed_units(pool, ahead, with_setup(step, unit))

            @block.vector
            def _(v):
                ch = Chain(v, dch)
                v.wait_ge(s_prm, 16)
                v.memset(spare[:], EPS)
                v.reciprocal(rinsc[:], insc)
                v.tensor_tensor(pscale[:], wsc[:, 4:5], wsc[:, 5:6], ALU.mult)
                ch(v.reciprocal(rsm[:], smooth))
                v.tensor_scalar(rsm[:, 16:], rsm[:, 16:], 1 / WS, None, ALU.mult)
                v.tensor_scalar(rsm[:, 0:16], rsm[:, 0:16], wsc[:, 3:4], None, ALU.mult)
                ch(v.tensor_tensor(epsw[:, 0:3], wsc[:, 0:3], wsc[:, 0:3], ALU.mult))
                ch(v.reciprocal(epsw[:, 0:3], epsw[:, 0:3]))
                ch(v.tensor_scalar(epsw[:, 0:3], epsw[:, 0:3], EPS, None, ALU.mult))
                v.memset(epsw[:, 3:4], EPS * WS * WS).then_inc(s_c2, 1)

                def quantise(yv, mg, last):
                    ch2 = last["chain"]
                    ch2(v.tensor_scalar(yv, yv, F8MAX, -F8MAX, ALU.min, ALU.max))
                    ch2(v.tensor_scalar(mg.bitcast(U16), yv.bitcast(U16), 0x7F80, None, ALU.bitwise_and))
                    ch2(v.tensor_scalar(mg, mg, 2.0 ** -6, 24.0, ALU.max, ALU.mult))
                    ch2(v.tensor_tensor(yv, yv, mg, ALU.add))
                    v.tensor_tensor(yv, yv, mg, ALU.subtract).then_inc(last["sem"], 1)

                def quant_x(t):
                    v.wait_ge(s_xs, t + 1)
                    quantise(xq[:, t].rearrange("p s k n -> p (s k) n"), mag[:], {"chain": ch, "sem": s_xq})

                def center(n):
                    what, a, b = order[n]
                    slot = raw[:, n % NSLOT]
                    if not centered(what, b):
                        return
                    if is_self(a) or b < 2:
                        v.wait_ge(s_scaled, n_scaled(order, n))
                    else:
                        raw_here(v, n)
                    heads = slot.rearrange("p k (h d) -> p (k h) d", d=P)
                    ch(v.tensor_reduce(wmean[:, n % NSLOT], heads, AX.X, ALU.add))
                    v.tensor_scalar(wmean[:, n % NSLOT], wmean[:, n % NSLOT], -1.0 / P, None, ALU.mult).then_inc(s_mean, 1)

                def low(n):
                    what, a, b = order[n]
                    v.wait_ge(s_hi, n + 1)
                    k = WS if what == "w" and not is_self(a) and b >= 2 else 1.0
                    hi, lo = (w2h[:, a, b], w2l[:, a, b]) if what == "w" else (
                        ch_[:, :, a * 512:(a + 1) * 512], cl_[:, :, a * 512:(a + 1) * 512])
                    v.scalar_tensor_tensor(lo, raw[:, n % NSLOT], k, hi, ALU.mult, ALU.subtract).then_inc(s_lo, 1)

                def cut(ns):
                    for j, n in enumerate(ns):
                        if j == 0:
                            center(n)
                        if j + 1 < len(ns):
                            center(ns[j + 1])
                        low(n)

                def step(n):
                    cut(cuts.get(n, []))
                    for t in quants.get(n, []):
                        quant_x(t)

                for t in range(NT):
                    ch(v.bn_stats(st[:, t], X[:, t, :]))
                    v.bn_aggr(mv[:, t], st[:, t]).then_inc(s_mv, 1)
                for t in range(NT):
                    v.wait_ge(s_rs, t + 1)
                    v.tensor_scalar(xn[:, t], X[:, t, :], mv[:, t, 0:1], rs[:, t], ALU.subtract, ALU.mult).then_inc(s_xn, 1)
                quant_x(0)
                cut(chunks("w", 0))

                uc, qc, tc = TileChain(v, dun), TileChain(v, dqu), TileChain(v, dti)

                def scale(n, c):
                    rq_done.wait(v, n, c + 1)
                    tq_ready.wait(v, n.before(), c + 1)
                    v.tensor_tensor(qn[:, c].rearrange("p (h d) -> p h d", d=P), pj[c][:].rearrange("p (h d) -> p h d", d=P),
                                    over(rq[:, c], 2, [P, 4, P]), ALU.mult).then_inc(qn_done.sem, 1)

                def ahead(n):
                    for c in range(3):
                        scale(n, c)

                def spread(n):
                    uc.start(n)
                    sc_ready.wait(v, n, 1)
                    s3 = scb[:].rearrange("p (g t) -> p g t", t=T)
                    uc(v.tensor_reduce(mx[:], s3, AX.X, ALU.max))
                    pt_ready.wait(v, n.before(2), 1)
                    v.tensor_tensor(sc[:, n.parity].rearrange("p (g t) -> p g t", t=T), s3, over(mx[:], 2, [P, 8, T]),
                                    ALU.subtract).then_inc(sub_done.sem, 1)

                def inv_sum(n):
                    exp_done.wait(v, n, 1)
                    uc(v.tensor_reduce(sm[:], sc[:, n.parity].rearrange("p (g t) -> p g t", t=T), AX.X, ALU.add))
                    p_done.wait(v, n.before(), 1)
                    v.reciprocal(rc[:], sm[:]).then_inc(rc_done.sem, 1)

                def quant_values(l):
                    qc.start(l)
                    pv_ready.wait(v, l, 1)
                    u = l.off % UN
                    if u == 0:
                        wp_ready.wait(v, Tile(l.off // UN - 1, l.reg, 1), 1)
                    for b in range(2):
                        i = v.tensor_tensor(cat[:, 8 * u:8 * u + 8, b * T:(b + 1) * T],
                                            pv[b][:].rearrange("p (h s) -> p h s", s=T),
                                            over(rsm[:, 8 * u:8 * u + 8], 2, [P, 8, T]), ALU.mult)
                    i.then_inc(y_done.sem, 1)
                    y_done.wait(v, l, 1)
                    quantise(cat[:, 8 * u:8 * u + 8, :], cmag[:], {"chain": qc, "sem": cat_done.sem})

                def unit(l, n, m, te):
                    if n is not None:
                        spread(n)
                    if m is not None:
                        scale(m, 0)
                        scale(m, 1)
                    if n is not None:
                        inv_sum(n)
                    if m is not None:
                        scale(m, 2)
                    if te is not None:
                        tc.start(te)
                        wp_ready.wait(v, te, 1)
                        xt = X[:, bass.ds(te.value(1), 1), :].rearrange("p a d -> p (a d)")
                        v.scalar_tensor_tensor(y[:], ptb[:, 0:D], pscale[:, 0:1], xt, ALU.mult, ALU.add).then_inc(yt_done.sem, 1)
                        yt_done.wait(v, te, 1)
                        tc(v.bn_stats(st[:, 0], y[:]))
                        v.memset(mx[:, 0:1], 0.0)
                        v.bn_aggr(mv[:, 0], st[:, 0]).then_inc(mv_done.sem, 1)
                    if l is not None:
                        quant_values(l)
                    if te is not None:
                        rs_done.wait(v, te, 1)
                        v.tensor_scalar(xt, y[:], mv[:, 0, 0:1], rs[:, 0], ALU.subtract, ALU.mult).then_inc(x2_done.sem, 1)

                skewed_units(v, ahead, with_setup(step, unit))


def n_scaled(order, n):
    return sum(w == "w" and (u < UN // 2 or c < 2) for w, u, c in order[:n + 1])


def n_centered(order, n):
    return sum(w == "w" and c < 3 for w, u, c in order[:n + 1])


E = 8
FE = 176
FC = 2 * FE
NC3 = 6
FF = NC3 * FC
NB3 = -(-FF // P)
NG3 = -(-NB3 // 4)


def skewed_tiles(eng, front):
    front(Tile(0), None)
    front(Tile(1), Tile(0))
    front(Tile(2), Tile(1))
    with eng.Fori(0, (NT - 4) // 2) as i:
        front(Tile(3, i), Tile(2, i))
        front(Tile(4, i), Tile(3, i))
    front(Tile(NT - 1), Tile(NT - 2))
    front(None, Tile(NT - 1))


def stage3(nc, io, X, out):
    with ExitStack() as ctx:
        def sb(name, shape, dt=F32):
            return ctx.enter_context(nc.sbuf_tensor(name, [P] + shape, dt))

        def pb(name):
            return ctx.enter_context(nc.psum_tensor(name, [P, 512], F32))

        def sem(name):
            return ctx.enter_context(nc.semaphore(name))

        def sig(name, per):
            return Signal(sem(name), per)

        NSLOT = 4
        raw = sb("raw3", [NSLOT, 2 * 2 * FC])
        wuh = sb("wuh", [NC3, KT, 2 * FC], F16)
        wul = sb("wul", [NC3, KT, 2 * FC], F16)
        wdh = sb("wdh", [NG3 * 4, D], F16)
        wdl = sb("wdl", [NG3 * 4, D], F16)
        wr32 = sb("wr32", [KT, E + 1])
        wrh = sb("wrh", [KT, E + 1], F16)
        wrl = sb("wrl", [KT, E + 1], F16)
        ident = sb("ident3", [P])
        iota = sb("iota3", [E])
        xh = sb("x3h", [KT, NTOK], F16)
        xl = sb("x3l", [KT, NTOK], F16)
        lg = sb("lg", [NT, E + 1])
        pr = sb("pr", [NT, E])
        mx = sb("mx3", [NT])
        top = sb("top", [NT, 8])
        idx = sb("idx", [NT, 8], U32)
        idf = sb("idf", [NT, 8])
        m1 = sb("m1", [NT, E])
        m2 = sb("m2", [NT, E])
        gate = sb("gate", [NT, E + 1])
        s1 = sb("s1", [2, FC])
        h = sb("h3", [2, NB3 * P])
        hTh = sb("hTh", [2, 512], F16)
        hTl = sb("hTl", [2, 512], F16)
        y = sb("y3", [D])
        st = sb("st3", [6])
        mv = sb("mv3", [2])
        rs = sb("rs3", [1])
        epsc = sb("eps3", [1])
        mhalf = sb("mhalf3", [1])
        spare = sb("spare3", [1])
        ob = sb("ob", [2, D])

        h1b = [pb("h1a"), pb("h1b")]
        h2b = [pb("h2a"), pb("h2b")]
        tb_ = [pb("tA"), pb("tB")]
        yb = [pb("yA"), pb("yB")]

        s_id, s_wr = sem("ident3_loaded"), sem("wr_loaded")
        NU = NC3 + NG3
        s_raw = [sem(f"raw3_loaded{i}") for i in range(NSLOT)]
        s_hi, s_lo, s_wrh, s_wrl = sem("w3_hi"), sem("w3_lo"), sem("wr_hi"), sem("wr_lo")
        s_xT, s_xh, s_xl, s_lg = sem("x3T"), sem("x3_hi"), sem("x3_lo"), sem("logits")
        s_mx, s_e, s_z, s_ze, s_gate, s_zero = (sem("soft_in"), sem("soft_exp"), sem("gate_in"), sem("gate_exp"),
                                                sem("gates_done"), sem("zero3"))
        dch, dti, pti, pch = sem("dve_setup3"), sem("dve_tile3"), sem("pool_tile3"), sem("pool_setup3")
        up_ready, silu_done, h_done = sig("up_ready", NC3), sig("silu3_done", NC3), sig("h_done", NC3)
        t_ready, hi_done, lo_done, down_done = (sig("t_ready", NG3), sig("hi3_done", NG3), sig("lo3_done", NG3),
                                                sig("down_done", NG3))
        yt_done, mv_done, rs_done, out_ready, stored = (sig("y3_done", 1), sig("mv3_done", 1), sig("rs3_done", 1),
                                                        sig("out_ready", 1), sig("out_stored", 16))

        def raw_here(eng, n):
            eng.wait_ge(s_raw[n % NSLOT], 16 * (n // NSLOT + 1))

        def two_before(eng, s, t, k, per):
            if t.reg is not None or t.off * per + k - 1 > 0:
                eng.wait_ge(s.sem, t.value(per, k - 1))

        with nc.Block() as block:
            @block.sync
            def _(sp):
                sp.dma_start(ident[:], io["consts"][:, 0:P]).then_inc(s_id, 16)
                sp.dma_start(iota[:], io["iota"]).then_inc(s_id, 16)
                sp.dma_start(wr32[:], io["wr"].rearrange("(k p) n -> p k n", p=P)).then_inc(s_wr, 16)
                wu = io["wu"].rearrange("(k p) n -> p k n", p=P)
                wd = io["wd"].rearrange("(n p) c -> p n c", p=P)
                for n in range(NU):
                    if n >= NSLOT:
                        sp.wait_ge(s_lo, n - NSLOT + 1)
                    if n < NC3:
                        sp.dma_start(raw[:, n % NSLOT, 0:4 * FC].rearrange("p (k n) -> p k n", k=KT),
                                     wu[:, :, n * 2 * FC:(n + 1) * 2 * FC]).then_inc(s_raw[n % NSLOT], 16)
                    else:
                        b = 4 * (n - NC3)
                        m = min(4, NB3 - b)
                        sp.dma_start(raw[:, n % NSLOT, 0:m * D].rearrange("p (n c) -> p n c", c=D),
                                     wd[:, b:b + m, :]).then_inc(s_raw[n % NSLOT], 16)

                def store(t):
                    ready, before = out_ready.count(sp, t, 1), t.before()
                    landed = stored.count(sp, before, 16) if before.exists else None
                    row = t.value(P) if t.reg is None else sp.snap(t.value(P))
                    sp.wait_ge(out_ready.sem, ready)
                    if before.exists:
                        sp.wait_ge(stored.sem, landed)
                    sp.dma_start(out[bass.ds(row, P), :], ob[:, t.parity]).then_inc(stored.sem, 16)

                def front(t, tb):
                    if tb is not None:
                        store(tb)

                skewed_tiles(sp, front)
                stored.wait(sp, Tile(NT - 1), 16)

            @block.tensor
            def _(pe):
                pe.wait_ge(s_id, 32)
                for t in range(NT):
                    if t >= 2:
                        pe.wait_ge(s_xl, t - 1)
                    for k in range(KT):
                        i = pe.transpose(tb_[t % 2][:, k * P:(k + 1) * P], X[:, t, k * P:(k + 1) * P], ident[:])
                    i.then_inc(s_xT, 1)
                pe.wait_ge(s_xl, NT)
                pe.wait_ge(s_wrl, 1)
                for t in range(NT):
                    tok = slice(t * P, (t + 1) * P)
                    for k in range(KT):
                        for j, (a, b) in enumerate(((xh, wrh), (xl, wrh), (xh, wrl))):
                            i = pe.matmul(yb[0][:, t * (E + 1):(t + 1) * (E + 1)], a[:, k, tok], b[:, k, :],
                                          start=k == 0 and j == 0, stop=k == KT - 1 and j == 2)
                i.then_inc(s_lg, 1)

                def up(t, c):
                    two_before(pe, h_done, t, c, NC3)
                    if t.reg is None and t.off == 0:
                        pe.wait_ge(s_lo, c + 1)
                    tok = bass.ds(t.value(P), P)
                    for bank, w0 in ((h1b[c % 2], 0), (h2b[c % 2], FC)):
                        for k in range(KT):
                            for j, (a, b) in enumerate(((xh, wuh), (xh, wul), (xl, wuh))):
                                i = pe.matmul(bank[:, 0:FC], a[:, k, tok], b[:, c, k, w0:w0 + FC],
                                              start=k == 0 and j == 0, stop=k == KT - 1 and j == 2)
                    i.then_inc(up_ready.sem, 1)

                def turn(t, g):
                    h_done.wait(pe, t, NC3)
                    two_before(pe, lo_done, t, g, NG3)
                    for j in range(min(4, NB3 - 4 * g)):
                        b = 4 * g + j
                        i = pe.transpose(tb_[(t.parity + g) % 2][:, j * P:(j + 1) * P], h[:, t.parity, b * P:(b + 1) * P],
                                         ident[:])
                    i.then_inc(t_ready.sem, 1)

                def down(t, g):
                    lo_done.wait(pe, t, g + 1)
                    if g == 0:
                        yt_done.wait(pe, t.before(2), 1)
                        if t.reg is None and t.off == 0:
                            pe.wait_ge(s_lo, NU)
                            pe.wait_ge(s_gate, 1)
                    q = (t.parity + g) % 2
                    m = min(4, NB3 - 4 * g)
                    for j in range(m):
                        b = 4 * g + j
                        c = slice(j * P, (j + 1) * P)
                        for x, (a, w) in enumerate(((hTh, wdh), (hTh, wdl), (hTl, wdh))):
                            i = pe.matmul(yb[t.parity][:, 0:D], a[:, q, c], w[:, b, :], start=b == 0 and x == 0,
                                          stop=b == NB3 - 1 and x == 2)
                    i.then_inc(down_done.sem, 1)

                def front(t, tb):
                    for c in range(NC3):
                        if t is not None:
                            up(t, c)
                        if tb is not None:
                            if c < NG3:
                                turn(tb, c)
                            if c > 0:
                                down(tb, c - 1)

                skewed_tiles(pe, front)

            @block.scalar
            def _(act):
                act.wait_ge(s_wr, 16)
                act.activation(wrh[:], wr32[:], ACT.Copy, scale=WS).then_inc(s_wrh, 1)

                def cut(n):
                    raw_here(act, n)
                    if n < NC3:
                        dst, src = wuh[:, n].rearrange("p k n -> p (k n)"), raw[:, n % NSLOT, 0:4 * FC]
                    else:
                        b = 4 * (n - NC3)
                        m = min(4, NB3 - b)
                        dst, src = wdh[:, b:b + m].rearrange("p n c -> p (n c)"), raw[:, n % NSLOT, 0:m * D]
                    act.activation(dst, src, ACT.Copy, scale=WS).then_inc(s_hi, 1)

                for t in range(NT):
                    act.wait_ge(s_xT, t + 1)
                    act.activation(xh[:, :, t * P:(t + 1) * P], tb_[t % 2][:, 0:D].rearrange("p (k n) -> p k n", k=KT),
                                   ACT.Copy).then_inc(s_xh, 1)
                    if t < 4:
                        cut(t)
                act.wait_ge(s_mx, 1)
                act.activation(pr[:], pr[:], ACT.Exp).then_inc(s_e, 1)
                act.wait_ge(s_z, 1)
                act.activation(mx[:], lg[:, :, E], ACT.Exp, scale=-1.0).then_inc(s_ze, 1)
                for n in range(4, NU):
                    cut(n)

                def silu(t, c):
                    up_ready.wait(act, t, c + 1)
                    two_before(act, h_done, t, c, NC3)
                    act.activation(s1[:, c % 2], h1b[c % 2][:, 0:FC], ACT.Silu, scale=1 / WS).then_inc(silu_done.sem, 1)

                def high(t, g):
                    t_ready.wait(act, t, g + 1)
                    two_before(act, down_done, t, g, NG3)
                    q, n = (t.parity + g) % 2, min(4, NB3 - 4 * g) * P
                    act.activation(hTh[:, q, 0:n], tb_[q][:, 0:n], ACT.Copy).then_inc(hi_done.sem, 1)

                def front(t, tb):
                    for c in range(NC3):
                        if t is not None:
                            silu(t, c)
                        if tb is not None and c < NG3:
                            high(tb, c)

                skewed_tiles(act, front)

            @block.gpsimd
            def _(pool):
                pool.memset(epsc[:], EPS)
                pool.memset(mhalf[:], -0.5).then_inc(pch, 1)
                pool.memset(h[:, :, FF:], 0.0).then_inc(s_zero, 1)
                pool.wait_ge(pch, 1)
                pc = TileChain(pool, pti)

                def front(t, tb):
                    if tb is not None:
                        pc.start(tb)
                        mv_done.wait(pool, tb, 1)
                        pc(pool.tensor_tensor(rs[:], mv[:, 1:2], epsc[:], ALU.add))
                        pool.tensor_tensor(rs[:], rs[:], mhalf[:], ALU.pow).then_inc(rs_done.sem, 1)

                skewed_tiles(pool, front)

            @block.vector
            def _(v):
                ch = Chain(v, dch)
                v.wait_ge(s_wrh, 1)
                v.scalar_tensor_tensor(wrl[:], wr32[:], WS, wrh[:], ALU.mult, ALU.subtract).then_inc(s_wrl, 1)

                def cut(n):
                    v.wait_ge(s_hi, n + 1)
                    if n < NC3:
                        c = slice(0, 4 * FC)
                        hi, lo = (w[:, n].rearrange("p k n -> p (k n)") for w in (wuh, wul))
                    else:
                        b = 4 * (n - NC3)
                        m = min(4, NB3 - b)
                        c = slice(0, m * D)
                        hi, lo = (w[:, b:b + m].rearrange("p n c -> p (n c)") for w in (wdh, wdl))
                    v.scalar_tensor_tensor(lo, raw[:, n % NSLOT, c], WS, hi, ALU.mult, ALU.subtract).then_inc(s_lo, 1)

                for t in range(NT):
                    v.wait_ge(s_xh, t + 1)
                    tok = slice(t * P, (t + 1) * P)
                    v.tensor_tensor(xl[:, :, tok], tb_[t % 2][:, 0:D].rearrange("p (k n) -> p k n", k=KT), xh[:, :, tok],
                                    ALU.subtract).then_inc(s_xl, 1)
                    if t < 4:
                        cut(t)
                v.wait_ge(s_lg, 1)
                v.tensor_scalar(lg[:].rearrange("p t e -> p (t e)"), yb[0][:, 0:NT * (E + 1)], 1 / WS, None,
                                ALU.mult).then_inc(s_z, 1)
                v.wait_ge(s_z, 1)
                ch(v.tensor_reduce(m1[:, :, 0], lg[:, :, 0:E], AX.X, ALU.max))
                v.tensor_tensor(pr[:], lg[:, :, 0:E], over(m1[:, :, 0], 2, [P, NT, E]), ALU.subtract).then_inc(s_mx, 1)
                v.wait_ge(s_e, 1)
                ch(v.tensor_reduce(m2[:, :, 0], pr[:], AX.X, ALU.add))
                ch(v.reciprocal(m2[:, :, 1], m2[:, :, 0]))
                ch(v.tensor_tensor(pr[:], pr[:], over(m2[:, :, 1], 2, [P, NT, E]), ALU.mult))
                for t in range(NT):
                    i = v.max(top[:, t], pr[:, t])
                ch(i)
                for t in range(NT):
                    i = v.max_index(idx[:, t], top[:, t], pr[:, t])
                ch(i)
                ch(v.tensor_copy(idf[:], idx[:]))
                v.wait_ge(s_id, 32)
                v.tensor_tensor(m1[:], over(iota[:], 1, [P, NT, E]), idf[:, :, 0:1].broadcast_to([P, NT, E]), ALU.is_equal)
                ch(v.tensor_tensor(m2[:], over(iota[:], 1, [P, NT, E]), idf[:, :, 1:2].broadcast_to([P, NT, E]), ALU.is_equal))
                ch(v.tensor_tensor(m1[:], m1[:], m2[:], ALU.add))
                v.scalar_tensor_tensor(gate[:, :, 0:E], pr[:], 1 / WS, m1[:], ALU.mult, ALU.mult)
                v.wait_ge(s_ze, 1)
                ch(v.tensor_scalar(mx[:], mx[:], 1.0, None, ALU.add))
                ch(v.reciprocal(mx[:], mx[:]))
                v.tensor_scalar(gate[:, :, E], mx[:], 1 / WS, None, ALU.mult).then_inc(s_gate, 1)
                for n in range(4, NU):
                    cut(n)
                v.wait_ge(s_gate, 1)
                v.wait_ge(s_zero, 1)
                vc = TileChain(v, dti)

                def gated(t, c):
                    silu_done.wait(v, t, c + 1)
                    if c == 0:
                        t_ready.wait(v, t.before(2), NG3)
                    gt = gate[:, bass.ds(t.value(1), 1), :].rearrange("p a e -> p (a e)")
                    for j in range(2 if c < E // 2 else 1):
                        e, n = (2 * c + j, FE) if c < E // 2 else (E, FC)
                        i = v.scalar_tensor_tensor(h[:, t.parity, c * FC + j * FE:c * FC + j * FE + n],
                                                   h2b[c % 2][:, j * FE:j * FE + n], gt[:, e:e + 1],
                                                   s1[:, c % 2, j * FE:j * FE + n], ALU.mult, ALU.mult)
                    i.then_inc(h_done.sem, 1)

                def low(t, g):
                    hi_done.wait(v, t, g + 1)
                    two_before(v, down_done, t, g, NG3)
                    q, n = (t.parity + g) % 2, min(4, NB3 - 4 * g) * P
                    v.tensor_tensor(hTl[:, q, 0:n], tb_[q][:, 0:n], hTh[:, q, 0:n], ALU.subtract).then_inc(lo_done.sem, 1)

                def finish(t):
                    down_done.wait(v, t, NG3)
                    vc.start(t)
                    xt = X[:, bass.ds(t.value(1), 1), :].rearrange("p a d -> p (a d)")
                    v.scalar_tensor_tensor(y[:], yb[t.parity][:, 0:D], 1 / WS, xt, ALU.mult, ALU.add).then_inc(yt_done.sem, 1)
                    yt_done.wait(v, t, 1)
                    vc(v.bn_stats(st[:], y[:]))
                    v.memset(spare[:], 0.0)
                    v.bn_aggr(mv[:], st[:]).then_inc(mv_done.sem, 1)
                    rs_done.wait(v, t, 1)
                    stored.wait(v, t.before(2), 16)
                    v.tensor_scalar(ob[:, t.parity], y[:], mv[:, 0:1], rs[:, 0:1], ALU.subtract,
                                    ALU.mult).then_inc(out_ready.sem, 1)

                def front(t, tb):
                    for c in range(NC3):
                        if t is not None:
                            gated(t, c)
                        if tb is not None and c < NG3:
                            low(tb, c)
                    if tb is not None:
                        finish(tb)

                skewed_tiles(v, front)


def program(nc, io, outs):
    with ExitStack() as ctx:
        X = ctx.enter_context(nc.sbuf_tensor("X", [P, NT, D], F32))
        stage1(nc, io, X)
        stage2(nc, io, X)
        stage3(nc, io, X, outs[0])


def kernel(**inputs):
    import concourse.bacc as bacc
    from concourse.bass_utils import run_bass_kernel_spmd as run

    A = {k: np.asarray(v) for k, v in inputs.items()}
    L = lambda n: A["L0_attn_" + n]
    rows = lambda a: np.ascontiguousarray(np.broadcast_to(a.reshape(1, -1), (P, a.size)))
    cuts = lambda a: [a[:, h * P:(h + 1) * P] for h in range(H)]
    q, k = cuts(L("Wq")), cuts(L("Wk"))
    cq, ck = [c.reshape(H, P, 4) for c in (L("conv_wq"), L("conv_wk"))]
    w1 = [L("Wb"), L("Wa")]
    cw = []
    for h in range(H):
        w1 += [k[h], q[h]]
        cw += [ck[h], cq[h]]
    w1 += [L("Wv"), L("Wg")]
    cw += list(L("conv_wv").reshape(3, P, 4))
    u = np.arange(P)[:, None]
    s, t = np.arange(P)[None, :], np.arange(T)[None, :]
    consts = np.concatenate([
        u == s, (u > s) & (u // T == s // T), u % T <= t, t >= u % T, t // BLK > (u % T) // BLK,
    ], axis=1).astype(np.float32)
    x = A["x"].reshape(NTOK, D)
    arrays = {
        "x": x, "xT": x.T, "w1": np.concatenate(w1, axis=1), "wo": L("Wo"),
        "convw": np.stack(cw, axis=1),
        "dtb": rows(L("dt_bias")), "alog": rows(L("A_log")), "normw": rows(L("norm_w")),
        "consts": consts, "eyes": (np.arange(BLK * BLK // 2)[None, :] // BLK * 2 + (np.arange(P)[:, None] >= YP)
                 == np.arange(BLK * BLK // 2)[None, :] % BLK).astype(np.float32),
    }
    Y = lambda n: A["L0_xattn_" + n]
    wqT, wqxT, wkT, wvT, wkvxT = (Y(n).T for n in ("wq", "wqx", "wk", "wv", "w_kv_x"))
    w2 = []
    for q_, k_, v_ in ((wqT, wkT, wvT), (wqxT, wkvxT[:, :G * P], wkvxT[:, G * P:])):
        for half in range(2):
            w2 += [q_[:, half * 1024:(half + 1) * 1024], k_[:, half * 512:(half + 1) * 512],
                   v_[:, half * 512:(half + 1) * 512]]
    cols = lambda a, n: a.reshape(n, P).T
    prm2 = [cols(Y("ln_w"), 2), cols(Y("ln_b"), 2)]
    prm2 += [cols(Y(n + "_in_scale"), 2) for n in ("q", "qx", "k", "v")]
    for n in ("q", "qx", "k", "kx"):
        prm2 += [cols(Y(n + "ln_w"), 1), cols(Y(n + "ln_b"), 1)]
    prm2 += [rows(Y(n)) for n in ("wq_scale", "wqx_scale", "wk_scale", "wv_scale", "proj_in_scale", "proj_w_scale")]
    prm2 += [cols(Y("proj_smooth"), NH2)]
    arrays.update({"w2": np.concatenate(w2, axis=1), "wproj": Y("wproj").T, "ctxT": A["ctx_2048"].reshape(NTOK, D).T,
                   "prm2": np.concatenate(prm2, axis=1)})
    Z = lambda n: A["L0_ffn_" + n]
    e1, e2 = Z("expert_fc1").reshape(E * FE, D).T, Z("expert_fc2").reshape(E * FE, D).T
    f1, f2 = np.concatenate([e1, Z("shared_fc1").T], axis=1), np.concatenate([e2, Z("shared_fc2").T], axis=1)
    wu = [w[:, c * FC:(c + 1) * FC] for c in range(NC3) for w in (f1, f2)]
    wd = np.concatenate([Z("expert_proj").transpose(0, 2, 1).reshape(E * FE, D), Z("shared_proj").T,
                         np.zeros((NB3 * P - FF, D), np.float32)])
    arrays.update({"wu": np.concatenate(wu, axis=1), "wd": wd,
                   "wr": np.concatenate([Z("gate_w").T, Z("shared_gate_w").T], axis=1),
                   "iota": rows(np.arange(E, dtype=np.float32))})
    nc = bacc.Bacc("TRN2", target_bir_lowering=False, num_devices=1)
    feed, io = {}, {}
    for n, a in arrays.items():
        a = np.ascontiguousarray(a)
        feed["in_" + n] = a
        io[n] = nc.dram_tensor("in_" + n, a.shape, F32, kind="ExternalInput").ap()
    out = nc.dram_tensor("out_0", (NTOK, D), F32, kind="ExternalOutput").ap()
    program(nc, io, [out])
    r = run(nc, [feed], core_ids=[0])
    return r.results[0]["out_0"].reshape(16, T, D)
```

```python
from contextlib import ExitStack
from itertools import chain

import numpy as np
import concourse.bass as bass
from concourse import mybir

F32 = mybir.dt.float32
F16 = mybir.dt.float16
BF16 = mybir.dt.bfloat16
U16 = mybir.dt.uint16
U32 = mybir.dt.uint32
ALU = mybir.AluOpType
ACT = mybir.ActivationFunctionType
AX = mybir.AxisListType

P = 128
T = 64
D = 256
KT = D // P
NTOK = 1024
NT = NTOK // P
H = 12
DV = 32
HV = H * DV
NPAIR = H // 2
CH1 = 24 + 2 * H * P + 2 * HV
WS = 64.0
BLK = 32
NBLK = P // BLK
YP = NBLK * H
SOLVE = 4
EPS = 1e-5
G = 8
UN = 4
CH2 = 4 * 512
EARLY = UN * 4


class Tile:

    def __init__(self, off, reg=None, stride=2):
        self.off, self.reg, self.stride = off, reg, stride

    def value(self, per, k=0):
        base = self.off * per + k
        return base if self.reg is None else self.reg * (self.stride * per) + base

    def before(self, n=1):
        return Tile(self.off - n, self.reg, self.stride)

    @property
    def exists(self):
        return self.reg is not None or self.off >= 0

    @property
    def parity(self):
        return self.off % 2


class Signal:

    def __init__(self, sem, per):
        self.sem, self.per = sem, per

    def wait(self, eng, t, k):
        if t.exists:
            eng.wait_ge(self.sem, t.value(self.per, k))

    def count(self, eng, t, k):
        if t.reg is None:
            return t.value(self.per, k)
        reg = eng.alloc_register(f"count_{eng.bass.next_id()}")
        eng.reg_mov(reg, t.value(self.per, k))
        return eng.snap(reg, min_val=0)


class Chain:

    def __init__(self, eng, sem):
        self.eng, self.sem, self.n = eng, sem, 0

    def __call__(self, ins):
        self.n += 1
        ins.then_inc(self.sem, 1)
        self.eng.wait_ge(self.sem, self.n)


class TileChain:

    def __init__(self, eng, sem):
        self.eng, self.sem, self.per, self.n, self.t = eng, sem, 0, 0, None

    def start(self, t):
        if self.t is not None and self.per == 0:
            self.per = self.n
        self.t, self.n = t, 0

    def mark(self, ins):
        self.n += 1
        ins.then_inc(self.sem, 1)
        return self.n

    def wait(self, n=None):
        self.eng.wait_ge(self.sem, self.t.value(self.per, self.n if n is None else n))

    def __call__(self, ins):
        self.mark(ins)
        self.wait()


def over(ap, axis, shape):
    return ap.unsqueeze(axis).broadcast_to(shape)


def woven_tiles(eng, front):
    front(Tile(0), None, None)
    front(Tile(1), Tile(0), None)
    front(Tile(2), Tile(1), Tile(0))
    with eng.Fori(0, (NT - 4) // 2) as i:
        front(Tile(3, i), Tile(2, i), Tile(1, i))
        front(Tile(4, i), Tile(3, i), Tile(2, i))
    front(Tile(NT - 1), Tile(NT - 2), Tile(NT - 3))
    front(None, Tile(NT - 1), Tile(NT - 2))
    front(None, None, Tile(NT - 1))


def weave(*programs):
    programs = list(programs)
    while programs:
        for p in list(programs):
            if next(p, "end") == "end":
                programs.remove(p)


class WeightCut:
    NSLOT = 4

    def __init__(self, nc, ctx, io):
        def sb(name, shape):
            return ctx.enter_context(nc.sbuf_tensor(name, [P] + shape, F32))

        def sem(name):
            return ctx.enter_context(nc.semaphore(name))

        self.io = io
        chunk = KT * 512
        halves = UN * 4 * chunk // 2
        self.region = sb("region", [self.NSLOT * chunk + 2 * halves])
        at = self.NSLOT * chunk
        self.raw = self.region[:, 0:at].rearrange("p (s k n) -> p s k n", k=KT, n=512)
        self.w2h, self.w2l = (
            self.region[:, at + i * halves:at + (i + 1) * halves].bitcast(F16).rearrange(
                "p (u c k n) -> p u c k n", u=UN, c=4, k=KT) for i in range(2))
        self.wmean = sb("wmean", [self.NSLOT, 8])
        self.ident = sb("identity", [P])
        self.prm = sb("prm", [12 + 8 + 6 + 32])
        self.insc = self.prm[:, 4:12]
        self.order = [("w", u, c) for u in range(UN) for c in range(4)] + [("ctx", k, 0) for k in range(2)] + \
                     [("wp", k, 0) for k in range(8)]
        self.prm_loaded = sem("prm_loaded")
        self.loaded = [sem(f"raw_loaded{i}") for i in range(self.NSLOT)]
        self.scaled, self.summed, self.mean_done = sem("w_scaled"), sem("w_summed"), sem("w_mean")
        self.centered, self.high_done, self.low_done = sem("w_centered"), sem("w_hi"), sem("w_lo")

    def chunks(self, what, *units):
        return [n for n, k in enumerate(self.order) if k[0] == what and (k[1] in units or not units)]

    def slot(self, n):
        return self.raw[:, n % self.NSLOT]

    def is_scaled(self, n):
        what, u, c = self.order[n]
        return what == "w" and (u < UN // 2 or c < 2)

    def is_centered(self, n):
        what, u, c = self.order[n]
        return what == "w" and c < 3

    def count(self, kind, n):
        return sum(kind(m) for m in range(n + 1))

    def scale_of(self, n):
        return WS if self.order[n][0] == "w" and not self.is_scaled(n) else 1.0

    def wait_loaded(self, eng, n):
        eng.wait_ge(self.loaded[n % self.NSLOT], 16 * (n // self.NSLOT + 1))

    def load(self, sp, n):
        what, a, b = self.order[n]
        if n >= self.NSLOT:
            last = self.order[n - self.NSLOT][0]
            sp.wait_ge(self.high_done if last == "wp" else self.low_done, n - self.NSLOT + 1)
        dst = self.slot(n)
        if what == "w":
            src = self.io["w2"].rearrange("(k p) n -> p k n", p=P)[:, :, a * CH2 + b * 512:a * CH2 + (b + 1) * 512]
        elif what == "ctx":
            src = self.io["ctxT"].rearrange("(k p) n -> p k n", p=P)[:, :, a * 512:(a + 1) * 512]
        else:
            src = self.io["wproj"].rearrange("(n p) c -> p n c", p=P)[:, a * 4:(a + 1) * 4, :]
            dst = dst.rearrange("p k n -> p (k n)").rearrange("p (n c) -> p n c", c=D)
        sp.dma_start(dst, src).then_inc(self.loaded[n % self.NSLOT], 16)

    def by_input(self, act, n):
        self.wait_loaded(act, n)
        if self.is_scaled(n):
            _, u, c = self.order[n]
            s = ((0, 0, 2, 3) if u < UN // 2 else (1, 1))[c]
            for k in range(KT):
                i = act.activation(self.slot(n)[:, k, :], self.slot(n)[:, k, :], ACT.Copy,
                                   scale=self.insc[:, 2 * s + k:2 * s + k + 1])
            i.then_inc(self.scaled, 1)

    def mean(self, v, n):
        if not self.is_centered(n):
            return
        if self.is_scaled(n):
            v.wait_ge(self.scaled, self.count(self.is_scaled, n))
        else:
            self.wait_loaded(v, n)
        means = self.wmean[:, n % self.NSLOT]
        v.tensor_reduce(means, self.slot(n).rearrange("p k (h d) -> p (k h) d", d=P), AX.X, ALU.add).then_inc(self.summed, 1)
        v.wait_ge(self.summed, self.count(self.is_centered, n))
        v.tensor_scalar(means, means, -1.0 / P, None, ALU.mult).then_inc(self.mean_done, 1)

    def center(self, pool, n):
        if self.is_centered(n):
            heads = self.slot(n).rearrange("p k (h d) -> p (k h) d", d=P)
            pool.wait_ge(self.mean_done, self.count(self.is_centered, n))
            pool.tensor_tensor(heads, heads, over(self.wmean[:, n % self.NSLOT], 2, [P, 8, P]), ALU.add).then_inc(self.centered, 1)

    def high(self, act, n, dst):
        src = self.slot(n)
        if self.order[n][0] == "wp":
            src = src.rearrange("p k n -> p (k n)")
        if self.is_scaled(n):
            act.wait_ge(self.scaled, self.count(self.is_scaled, n))
        if self.is_centered(n):
            act.wait_ge(self.centered, self.count(self.is_centered, n))
        act.activation(dst, src, ACT.Copy, scale=self.scale_of(n)).then_inc(self.high_done, 1)

    def low(self, v, n, high, dst):
        v.wait_ge(self.high_done, n + 1)
        v.scalar_tensor_tensor(dst, self.slot(n), self.scale_of(n), high, ALU.mult, ALU.subtract).then_inc(self.low_done, 1)

    def act_step(self, act, n):
        if n + 1 < EARLY:
            self.by_input(act, n + 1)
        _, u, c = self.order[n]
        self.high(act, n, self.w2h[:, u, c])

    def dve_step(self, v, n):
        if n + 1 < EARLY:
            self.mean(v, n + 1)
        _, u, c = self.order[n]
        self.low(v, n, self.w2h[:, u, c], self.w2l[:, u, c])


def stage1(nc, io, X, cut):
    with ExitStack() as ctx:
        def sb(name, shape, dt=F32):
            return ctx.enter_context(nc.sbuf_tensor(name, [P] + shape, dt))

        def pb(name):
            return ctx.enter_context(nc.psum_tensor(name, [P, 512], F32))

        def sem(name):
            return ctx.enter_context(nc.semaphore(name))

        def sig(name, per):
            return Signal(sem(name), per)

        def part(start, words):
            return cut.region[:, start:start + words], start + words

        w32, at = part(0, KT * CH1)
        xT32, at = part(at, KT * NTOK)
        wh, at = part(at, KT * CH1 // 2)
        wl, at = part(at, KT * CH1 // 2)
        xh, at = part(at, KT * NTOK // 2)
        xl, at = part(at, KT * NTOK // 2)
        w32, xT32 = (a.rearrange("p (k n) -> p k n", k=KT) for a in (w32, xT32))
        wh, wl, xh, xl = (a.bitcast(F16).rearrange("p (k n) -> p k n", k=KT) for a in (wh, wl, xh, xl))
        wo32 = sb("wo32", [3, D])
        woh = sb("woh", [3, D], F16)
        wol = sb("wol", [3, D], F16)
        cw = sb("cw", [27, 4])
        consts = sb("consts", [2 * P + 3 * T])
        ident = consts[:, 0:P]
        later = consts[:, P:2 * P]
        upto = consts[:, 2 * P:2 * P + T]
        incl = consts[:, 2 * P + T:2 * P + 2 * T]
        offblk = consts[:, 2 * P + 2 * T:2 * P + 3 * T]
        eyes = sb("eyes", [BLK // 2, BLK])
        dtb = sb("dtb", [H])
        alog = sb("alog", [H])
        normw = sb("normw", [DV])
        ones = sb("ones", [1])
        mhalf = sb("mhalf", [2 * H])
        epsc = sb("epsc", [H])
        spare = sb("spare", [1])
        ba = sb("ba", [NT, 2 * H])
        beta = sb("beta", [NT, H])
        g = sb("g", [NT, H])
        s1a = sb("s1a", [NT, H])
        s1b = sb("s1b", [NT, H])
        s1c = sb("s1c", [NT, H])
        gL = sb("gL", [2, H, T])
        F = sb("F", [NT, H, T])
        acc = sb("acc", [2, 4, P])
        far = sb("far", [2, 4, P])
        kq = sb("kq", [2, 2, 2, P])
        sq = sb("sq", [2, 2, 2, P])
        vT = sb("vT", [3, P])
        UP = sb("UP", [2, H, 2, P])
        Xf = sb("Xf", [H, P])
        Yn = sb("Yn", [BLK // 2, BLK])
        Ue = sb("Ue", [BLK, BLK])
        Yt = sb("Yt", [BLK // 2, BLK])
        n2 = sb("n2", [2, 2 * H])
        rn = sb("rn", [2, 2 * H])
        Bp = sb("Bp", [2, H])
        absk = sb("absk", [2, H])
        V = sb("V", [2, HV])
        w = sb("w", [2, HV])
        gs = sb("gs", [2, HV])
        sqo = sb("sqo", [HV])
        ms = sb("ms", [H])
        rr = sb("rr", [H])
        r2 = sb("r2", [H])
        on = sb("on", [HV])
        onh = sb("onh", [3, P], F16)
        onl = sb("onl", [3, P], F16)
        y = sb("y", [D])
        st = sb("st", [6])
        mv = sb("mv", [2])
        rs = sb("rs", [1])

        proj = [pb("proj0"), pb("proj1")]
        gram = [pb("gram0"), pb("gram1")]
        small = pb("small")
        turn = pb("turn")
        sol = [pb("sol0"), pb("sol1")]
        decay_banks = [gram, sol]

        UD = nc.dram_tensor("ud_dram", (NBLK, H, BLK, BLK), F32, kind="Internal").ap()
        YD = nc.dram_tensor("yd_dram", (NBLK, H, BLK, BLK), F32, kind="Internal").ap()

        s_x, s_X, s_c, s_wo = sem("x_loaded"), sem("xtok_loaded"), sem("consts_loaded"), sem("wo_loaded")
        NW = 4
        wcut = [0, 24 + 512 * 1, 24 + 512 * 3, 24 + 512 * 5, CH1]
        s_w = [sem(f"w1_loaded{i}") for i in range(NW)]
        s_xh, s_xl, s_wh, s_wl = sem("xh_done"), sem("xl_done"), sem("wh_done"), sem("wl_done")
        s_ba, s_ba_ev, s_eb, s_ea, s_g = sem("ba_ready"), sem("ba_done"), sem("expb_done"), sem("expa_done"), sem("g_done")
        s_na, s_ealog = sem("na_done"), sem("expalog_done")
        s_gL, s_D, s_F, s_Fm, s_zero = sem("gL_done"), sem("decay_ready"), sem("decay_exp"), sem("decay_masked"), sem("zero_done")
        s_beta = sem("beta_done")
        dch, dtile, dback, dend = sem("dve_setup"), sem("dve_tile"), sem("dve_back"), sem("dve_end")
        pch, ptile, pend = sem("pool_setup"), sem("pool_tile"), sem("pool_end")
        proj_ready = sig("proj_ready", 7)
        gg_ready, gg_done = sig("gg_ready", 1), sig("gg_done", 1)
        tap_done, conv_done, summed, silu_done = sig("tap_done", 7), sig("conv_done", 7), sig("conv_summed", 7), sig("silu_done", 7)
        sq_done = sig("sq_done", 6)
        gram_ready, gram_used, norm_ready = sig("gram_ready", 6), sig("gram_used", 6), sig("norm_ready", 6)
        n2_done, bp_done, rn_done = sig("n2_done", 1), sig("bp_done", 1), sig("rn_done", 1)
        vt_ready, v_done = sig("vt_ready", 1), sig("v_done", 1)
        u_scaled, u_masked = sig("u_scaled", 2), sig("u_masked", 2)
        ud_stored, ue_loaded = sig("ud_stored", 16 * NBLK), sig("ue_loaded", 32)
        y_done, yd_stored, xf_loaded = sig("y_done", 1), sig("yd_stored", 32), sig("xf_loaded", 16 * NBLK)
        sol_ready, sol_used = sig("sol_ready", SOLVE), sig("sol_used", SOLVE - 1)
        sqo_done, ms_done, rr_done = sig("sqo_done", 1), sig("ms_done", 1), sig("rr_done", 1)
        gsn_done, on_done, onT_ready = sig("gsn_done", 1), sig("on_done", 1), sig("onT_ready", 1)
        onh_done, onl_done, wo_ready = sig("onh_done", 1), sig("onl_done", 1), sig("wo_ready", 1)
        res_done, mv_done, rs_done = sig("res_done", 1), sig("mv_done", 1), sig("rs_done", 1)

        def unit_cols(u):
            return 24 + 512 * u

        GG = 24 + 512 * NPAIR + HV

        with nc.Block() as block:
            @block.sync
            def _(sp):
                sp.dma_start(xT32[:], io["xT"].rearrange("(k p) n -> p k n", p=P)).then_inc(s_x, 16)
                w1 = io["w1"].rearrange("(k p) n -> p k n", p=P)
                for i in range(NW):
                    sp.dma_start(w32[:, :, wcut[i]:wcut[i + 1]], w1[:, :, wcut[i]:wcut[i + 1]]).then_inc(s_w[i], 16)
                    if i == 0:
                        sp.dma_start(consts[:], io["consts"]).then_inc(s_c, 16)
                        for dst, src in ((eyes[:].rearrange("p a b -> p (a b)"), "eyes"), (cw[:], "convw"), (dtb[:], "dtb"),
                                         (alog[:], "alog"), (normw[:], "normw")):
                            sp.dma_start(dst, io[src]).then_inc(s_c, 16)
                sp.dma_start(X[:], io["x"].rearrange("(t p) d -> p t d", p=P)).then_inc(s_X, 16)
                sp.dma_start(wo32[:], io["wo"].rearrange("(k p) n -> p k n", p=P)).then_inc(s_wo, 16)
                sp.dma_start(cut.prm[:], io["prm2"]).then_inc(cut.prm_loaded, 16)
                sp.dma_start(cut.ident[:], io["consts"][:, 0:P]).then_inc(cut.prm_loaded, 16)

                def back(t, while_eliminated=(), while_stored=()):
                    b4 = t.before()
                    waits = [(u_scaled, t, 2), (ue_loaded, b4, 32), (ud_stored, t, 16 * NBLK), (y_done, b4, 1),
                             (y_done, t, 1), (xf_loaded, b4, 16 * NBLK), (yd_stored, t, 32), (sol_ready, b4, SOLVE - 1)]
                    scaled, ue_read, stored, y_before, y_now, xf_before, yd_now, sol_before = (
                        (s.sem, s.count(sp, n, k)) if n.exists else None for s, n, k in waits)
                    sp.wait_ge(*scaled)
                    if b4.exists:
                        sp.wait_ge(*ue_read)
                    for b in range(NBLK):
                        c = b * BLK
                        sp.dma_start(UD[b].rearrange("h s t -> s h t"),
                                     UP[c:c + BLK, t.parity, :, 0, c:c + BLK]).then_inc(ud_stored.sem, 16)
                    sp.wait_ge(*stored)
                    if b4.exists:
                        sp.wait_ge(*y_before)
                    for odd in range(2):
                        sp.dma_start(Ue[odd * YP:(odd + 1) * YP].rearrange("p s t -> p (s t)"),
                                     UD.rearrange("b h s t -> (b h) (s t)")).then_inc(ue_loaded.sem, 16)
                    for n in while_eliminated:
                        cut.load(sp, n)
                    sp.wait_ge(*y_now)
                    if b4.exists:
                        sp.wait_ge(*xf_before)
                    for odd in range(2):
                        sp.dma_start(YD.rearrange("b h (s a) t -> a (b h) s t", a=2)[odd],
                                     Yn[odd * YP:(odd + 1) * YP]).then_inc(yd_stored.sem, 16)
                    for n in while_stored:
                        cut.load(sp, n)
                    sp.wait_ge(*yd_now)
                    if b4.exists:
                        sp.wait_ge(*sol_before)
                    else:
                        sp.wait_ge(s_zero, 3)
                    for b in range(NBLK):
                        c = b * BLK
                        sp.dma_start(Xf[c:c + BLK, :, c:c + BLK],
                                     YD[b].rearrange("h s t -> s h t")).then_inc(xf_loaded.sem, 16)

                def front(t, tb, tf):
                    if t is not None and t.reg is None and t.off == NT - 1:
                        sp.wait_ge(s_wh, NW + 1)
                        sp.wait_ge(s_wl, NW + 1)
                        for n in range(cut.NSLOT):
                            cut.load(sp, n)
                    if tb is not None and t is None:
                        back(tb, range(cut.NSLOT, 7), range(7, 8))
                        for n in range(8, EARLY):
                            cut.load(sp, n)
                    elif tb is not None:
                        back(tb)

                woven_tiles(sp, front)
                ud_stored.wait(sp, Tile(NT - 1), 16 * NBLK)
                yd_stored.wait(sp, Tile(NT - 1), 32)
                xf_loaded.wait(sp, Tile(NT - 1), 16 * NBLK)

            @block.tensor
            def _(pe):
                def split_mm(out, stat_h, stat_l, mov_h, mov_l, start, stop):
                    pe.matmul(out, stat_h, mov_h, start=start, stop=False)
                    pe.matmul(out, stat_h, mov_l, start=False, stop=False)
                    return pe.matmul(out, stat_l, mov_h, start=False, stop=stop)

                pe.wait_ge(s_xh, 1)
                pe.wait_ge(s_xl, 1)
                pe.wait_ge(s_wh, 1)
                pe.wait_ge(s_wl, 1)
                for t in range(NT):
                    tok = slice(t * P, (t + 1) * P)
                    for k in range(KT):
                        mm = split_mm(proj[0][:, t * 24:t * 24 + 24], xh[:, k, tok], xl[:, k, tok],
                                      wh[:, k, 0:24], wl[:, k, 0:24], k == 0, k == KT - 1)
                mm.then_inc(s_ba, 1)
                pe.wait_ge(s_c, 16 * 6)
                for t in range(NT):
                    pe.wait_ge(s_gL, t + 1)
                    if t > 1:
                        pe.wait_ge(s_F, 2 * t - 2)
                    for hh in range(2):
                        pe.matmul(decay_banks[t % 2][hh][:, 0:6 * T], later,
                                  gL[:, t % 2, hh * 6:hh * 6 + 6, :], start=True, stop=True).then_inc(s_D, 1)

                def project(t, u):
                    if u == 0:
                        conv_done.wait(pe, t.before(), 7)
                        if t.reg is None and t.off == 0:
                            pe.wait_ge(s_ba_ev, 1)
                    elif u == 1:
                        gg_done.wait(pe, t.before(), 1)
                    else:
                        conv_done.wait(pe, t, u - 1)
                    if t.reg is None and t.off == 0 and u in (0, 1, 3, 5):
                        n = {0: 1, 1: 2, 3: 3, 5: 4}[u]
                        pe.wait_ge(s_wh, n)
                        pe.wait_ge(s_wl, n)
                    x0 = t.value(P)
                    bank = proj[u % 2]
                    if u == 7:
                        for k in range(KT):
                            mm = split_mm(bank[:, 0:HV], xh[:, k, bass.ds(x0, P)], xl[:, k, bass.ds(x0, P)],
                                          wh[:, k, GG:GG + HV], wl[:, k, GG:GG + HV], k == 0, k == KT - 1)
                        mm.then_inc(gg_ready.sem, 1)
                        return
                    for c in range(4 if u < 6 else 3):
                        w0 = unit_cols(u) + c * P
                        for k in range(KT):
                            mm = split_mm(bank[:, c * P:(c + 1) * P], wh[:, k, w0:w0 + P], wl[:, k, w0:w0 + P],
                                          xh[:, k, bass.ds(x0, P)], xl[:, k, bass.ds(x0, P)],
                                          k == 0, k == KT - 1)
                    mm.then_inc(proj_ready.sem, 1)

                def grams(t, u):
                    silu_done.wait(pe, t, u + 1)
                    (gram_used.wait(pe, t, u - 1) if u >= 2 else gram_used.wait(pe, t.before(), 5 + u))
                    if t.reg is None and t.off == 0 and u == 0:
                        pe.wait_ge(s_F, 2 * NT)
                    for hh in range(2):
                        mm = pe.matmul(gram[u % 2][:, hh * D:(hh + 1) * D], kq[:, u % 2, hh, 0, :],
                                       kq[:, u % 2, hh, :, :].rearrange("p a n -> p (a n)"), start=True, stop=True)
                    mm.then_inc(gram_ready.sem, 1)

                def norms(t, u):
                    sq_done.wait(pe, t, u + 1)
                    if u == 0:
                        v_done.wait(pe, t.before(), 1)
                    for hh in range(2):
                        for a in range(2):
                            col = t.parity * 24 + a * H + 2 * u + hh
                            mm = pe.matmul(small[:, col:col + 1], sq[:, u % 2, hh, a, :], ones[:, 0:1],
                                           start=True, stop=True)
                    mm.then_inc(norm_ready.sem, 1)

                def v_turn(t):
                    silu_done.wait(pe, t, 7)
                    n2_done.wait(pe, t, 1)
                    for c in range(3):
                        mm = pe.transpose(small[:, T + c * P:T + (c + 1) * P], vT[:, c, :], ident)
                    mm.then_inc(vt_ready.sem, 1)

                def solve(t, k):
                    q = t.parity
                    if k == 1:
                        xf_loaded.wait(pe, t, 16 * NBLK)
                        v_done.wait(pe, t, 1)
                        res_done.wait(pe, t.before(), 1)
                    else:
                        sol_used.wait(pe, t, k - 1)
                    if k == 2:
                        u_masked.wait(pe, t, 2)
                        on_done.wait(pe, t.before(), 1)
                    rhs = V if k == 1 else w
                    for h in range(H):
                        lhsT = Xf[:, h, :] if k % 2 else UP[:, q, h, 1 if k == SOLVE else 0, :]
                        r = V[:, q, h * DV:(h + 1) * DV] if k == 1 else w[:, k % 2, h * DV:(h + 1) * DV]
                        mm = pe.matmul(sol[k % 2][:, h * DV:(h + 1) * DV], lhsT, r, start=True, stop=True)
                    mm.then_inc(sol_ready.sem, 1)

                def turn_o(t):
                    on_done.wait(pe, t, 1)
                    onl_done.wait(pe, t.before(), 1)
                    for c in range(3):
                        mm = pe.transpose(turn[:, c * P:(c + 1) * P], on[:, c * P:(c + 1) * P], ident)
                    mm.then_inc(onT_ready.sem, 1)

                def output(t):
                    onh_done.wait(pe, t, 1)
                    onl_done.wait(pe, t, 1)
                    if t.reg is None and t.off == 0:
                        pe.wait_ge(s_wh, 5)
                        pe.wait_ge(s_wl, 5)
                    sol_used.wait(pe, t, SOLVE - 1)
                    for c in range(3):
                        mm = split_mm(sol[1][:, 0:D], onh[:, c, :], onl[:, c, :], woh[:, c, :], wol[:, c, :],
                                      c == 0, c == 2)
                    mm.then_inc(wo_ready.sem, 1)

                def front(t, tb, tf):
                    for u in range(7):
                        if t is not None and u == 0:
                            project(t, 0)
                        if tf is not None and u == 0:
                            solve(tf, 1)
                        if t is not None:
                            project(t, u + 1)
                        if tf is not None and u == 0:
                            solve(tf, 2)
                        if tb is not None and u == 0:
                            v_turn(tb)
                        if tf is not None and u < 2:
                            solve(tf, 3 + u)
                        if tf is not None and u == 4:
                            turn_o(tf)
                        if t is not None and u > 0:
                            grams(t, u - 1)
                            norms(t, u - 1)
                        if tf is not None and u == 5:
                            output(tf)

                woven_tiles(pe, front)

            @block.scalar
            def _(act):
                act.wait_ge(s_x, 16)
                act.activation(xh[:], xT32[:], ACT.Copy).then_inc(s_xh, 1)
                for i in range(NW):
                    act.wait_ge(s_w[i], 16)
                    act.activation(wh[:, :, wcut[i]:wcut[i + 1]], w32[:, :, wcut[i]:wcut[i + 1]], ACT.Copy,
                                   scale=WS).then_inc(s_wh, 1)
                    if i == 0:
                        act.wait_ge(s_c, 16 * 6)
                        act.activation(s1c[:, 0, :], alog[:], ACT.Exp).then_inc(s_ealog, 1)
                        act.wait_ge(s_na, 1)
                        act.activation(s1a[:], s1a[:], ACT.Exp).then_inc(s_ea, 1)
                        act.wait_ge(s_ba_ev, 1)
                        act.activation(beta[:], ba[:, :, 0:H], ACT.Exp, scale=-1.0).then_inc(s_eb, 1)
                act.wait_ge(s_wo, 16)
                act.activation(woh[:], wo32[:], ACT.Copy, scale=WS).then_inc(s_wh, 1)
                for t in range(NT):
                    for hh in range(2):
                        act.wait_ge(s_D, 2 * t + hh + 1)
                        act.activation(F[:, t, hh * 6:hh * 6 + 6, :].rearrange("p h t -> p (h t)"),
                                       decay_banks[t % 2][hh][:, 0:6 * T], ACT.Exp).then_inc(s_F, 1)

                def taps(t, u):
                    proj_ready.wait(act, t, u + 1)
                    (silu_done.wait(act, t, u - 1) if u >= 2 else silu_done.wait(act, t.before(), 7))
                    for dst, tap in ((acc, 0), (far, 3)):
                        for c in range(4 if u < 6 else 3):
                            i = act.activation(dst[:, u % 2, c, :], proj[u % 2][:, c * P:(c + 1) * P], ACT.Copy,
                                               scale=cw[:, 4 * u + c, 3 - tap:4 - tap])
                    i.then_inc(tap_done.sem, 1)

                def silu(t, u):
                    summed.wait(act, t, u + 1)
                    if u < 6:
                        (gram_ready.wait(act, t, u - 1) if u >= 2 else gram_ready.wait(act, t.before(), 5 + u))
                        (sq_done.wait(act, t, u - 1) if u >= 2 else sq_done.wait(act, t.before(), 5 + u))
                        act.activation(kq[:, u % 2].rearrange("p a b n -> p (a b n)"),
                                       acc[:, u % 2].rearrange("p c n -> p (c n)"), ACT.Silu,
                                       scale=1 / WS).then_inc(silu_done.sem, 1)
                    else:
                        vt_ready.wait(act, t.before(), 1)
                        act.activation(vT[:], acc[:, u % 2, 0:3, :], ACT.Silu, scale=1 / WS).then_inc(silu_done.sem, 1)

                def square(t, u):
                    silu_done.wait(act, t, u + 1)
                    (norm_ready.wait(act, t, u - 1) if u >= 2 else norm_ready.wait(act, t.before(), 5 + u))
                    act.activation(sq[:, u % 2], kq[:, u % 2], ACT.Square).then_inc(sq_done.sem, 1)

                def gate(t):
                    gg_ready.wait(act, t, 1)
                    on_done.wait(act, t.before(2), 1)
                    act.activation(gs[:, t.parity, :], proj[1][:, 0:HV], ACT.Silu, scale=1 / WS).then_inc(gg_done.sem, 1)

                def cut_steps(t, tb, point):
                    if t is None:
                        early = {0: (0, 3), 4: (3, 4), 7: (4, 7)} if tb is not None else {0: (7, 13), 4: (13, 14), 7: (14, 16)}
                        for n in range(*early.get(point, (0, 0))):
                            cut.act_step(act, n)

                def front(t, tb, tf):
                    if t is not None:
                        taps(t, 0)
                    if t is None and tb is not None:
                        act.wait_ge(cut.prm_loaded, 32)
                        gg_ready.wait(act, tb, 1)
                        cut.by_input(act, 0)
                    for u in range(7):
                        cut_steps(t, tb, u)
                        if t is not None:
                            if u < 6:
                                taps(t, u + 1)
                            else:
                                gate(t)
                        if tf is not None and u == 4:
                            onT_ready.wait(act, tf, 1)
                            wo_ready.wait(act, tf.before(), 1)
                            act.activation(onh[:].rearrange("p c n -> p (c n)"), turn[:, 0:HV], ACT.Copy).then_inc(onh_done.sem, 1)
                        if t is not None:
                            silu(t, u)
                            if u < 6:
                                square(t, u)
                        if tf is not None and u == 1:
                            sol_ready.wait(act, tf, SOLVE)
                            act.activation(sqo[:], sol[0][:, 0:HV], ACT.Square,
                                           scale=DV ** -0.5).then_inc(sqo_done.sem, 1)
                    cut_steps(t, tb, 7)

                woven_tiles(act, front)

            @block.gpsimd
            def _(pool):
                ch = Chain(pool, pch)
                pool.memset(ones[:], 1.0)
                pool.memset(epsc[:], EPS)
                ch(pool.memset(mhalf[:], -0.5))
                pool.memset(UP[:, 0], 0.0).then_inc(s_zero, 1)
                pool.memset(UP[:, 1], 0.0).then_inc(s_zero, 1)
                pool.memset(Xf[:], 0.0).then_inc(s_zero, 1)
                pool.wait_ge(s_c, 16 * 6)
                for t in range(NT):
                    pool.wait_ge(s_g, 1)
                    if t >= 2:
                        pool.wait_ge(s_D, 2 * t - 2)
                    pool.tensor_tensor(gL[:, t % 2], over(g[:, t, :], 2, [P, H, T]), over(upto, 1, [P, H, T]),
                                       ALU.mult).then_inc(s_gL, 1)
                fc, ec = TileChain(pool, ptile), TileChain(pool, pend)

                def scale_u(tb):
                    gram_used.wait(pool, tb, 6)
                    bp_done.wait(pool, tb, 1)
                    summed.wait(pool, tb, 7)
                    rs_done.wait(pool, tb.before(2), 1)
                    q = tb.parity
                    for b in range(2):
                        r = slice(b * T, (b + 1) * T)
                        pool.tensor_tensor(UP[r, q, :, 0, r], UP[r, q, :, 0, r],
                                           over(Bp[r, q, :], 2, [T, H, T]), ALU.mult).then_inc(u_scaled.sem, 1)
                    u_scaled.wait(pool, tb, 2)

                def sum_taps(t, u):
                    conv_done.wait(pool, t, u + 1)
                    n = 4 if u < 6 else 3
                    a, f = (x[:, u % 2, 0:n].rearrange("p c (b t) -> p (c b) t", b=2) for x in (acc, far))
                    pool.tensor_tensor(a[:, :, 3:], a[:, :, 3:], f[:, :, 0:T - 3], ALU.add).then_inc(summed.sem, 1)

                def head_scales(t):
                    fc.start(t)
                    q = t.parity
                    n2_done.wait(pool, t, 1)
                    fc(pool.tensor_tensor(rn[:, q], n2[:, q], mhalf[:], ALU.pow))
                    pool.tensor_tensor(absk[:, q], n2[:, q, 0:H], rn[:, q, 0:H], ALU.mult).then_inc(rn_done.sem, 1)

                def rms(tf):
                    ec.start(tf)
                    q = tf.parity
                    ms_done.wait(pool, tf, 1)
                    ec(pool.tensor_tensor(r2[:], rn[:, q, H:], rn[:, q, H:], ALU.mult))
                    ec(pool.tensor_tensor(r2[:], r2[:], ms[:], ALU.mult))
                    ec(pool.tensor_tensor(r2[:], r2[:], epsc[:], ALU.add))
                    ec(pool.tensor_tensor(r2[:], r2[:], mhalf[:, 0:H], ALU.pow))
                    pool.tensor_tensor(rr[:], r2[:], rn[:, q, H:], ALU.mult).then_inc(rr_done.sem, 1)

                def deviation(tf):
                    mv_done.wait(pool, tf, 1)
                    ec(pool.tensor_tensor(rs[:], mv[:, 1:2], epsc[:, 0:1], ALU.add))
                    pool.tensor_tensor(rs[:], rs[:], mhalf[:, 0:1], ALU.pow).then_inc(rs_done.sem, 1)

                def front(t, tb, tf):
                    if tb is not None:
                        scale_u(tb)
                        center(t, tb, "first")
                        head_scales(tb)
                    center(t, tb, 0)
                    if t is not None:
                        sum_taps(t, 0)
                        sum_taps(t, 1)
                        sum_taps(t, 2)
                    if tf is not None:
                        rms(tf)
                    center(t, tb, 1)
                    if t is not None:
                        sum_taps(t, 3)
                    if tb is not None:
                        if t is not None:
                            summed.wait(pool, t, 4)
                        else:
                            rr_done.wait(pool, tf, 1)
                        mask_u(tb)
                    center(t, tb, 2)
                    if t is not None:
                        sum_taps(t, 4)
                    if tb is not None:
                        gate_w(tb)
                    if t is not None:
                        sum_taps(t, 5)
                        sum_taps(t, 6)
                    if tf is not None:
                        deviation(tf)
                    center(t, tb, 3)

                def center(t, tb, point):
                    if t is None:
                        early = {"first": (0, 1), 0: (1, 3), 2: (3, 5), 3: (5, 8)} if tb is not None else {0: (8, 14), 1: (14, 16)}
                        for n in range(*early.get(point, (0, 0))):
                            cut.center(pool, n)

                def mask_u(tb):
                    ud_stored.wait(pool, tb, 16 * NBLK)
                    for b in range(2):
                        r = slice(b * T, (b + 1) * T)
                        pool.tensor_tensor(UP[r, tb.parity, :, 0, r], UP[r, tb.parity, :, 0, r],
                                           over(offblk[r, :], 1, [T, H, T]), ALU.mult).then_inc(u_masked.sem, 1)
                    u_masked.wait(pool, tb, 2)

                def gate_w(tb):
                    gg_done.wait(pool, tb, 1)
                    v = gs[:, tb.parity].rearrange("p (h d) -> p h d", h=H)
                    pool.tensor_tensor(v, v, over(normw[:], 1, [P, H, DV]), ALU.mult).then_inc(gsn_done.sem, 1)

                woven_tiles(pool, front)

            @block.vector
            def _(v):
                ch = Chain(v, dch)
                v.wait_ge(s_xh, 1)
                v.tensor_tensor(xl[:], xT32[:], xh[:], ALU.subtract).then_inc(s_xl, 1)

                def w_low(i):
                    v.wait_ge(s_wh, i + 1)
                    c = slice(wcut[i], wcut[i + 1])
                    v.scalar_tensor_tensor(wl[:, :, c], w32[:, :, c], WS, wh[:, :, c], ALU.mult,
                                           ALU.subtract).then_inc(s_wl, 1)

                w_low(0)
                v.wait_ge(s_c, 16 * 6)
                v.wait_ge(s_ba, 1)
                v.tensor_scalar(ba[:].rearrange("p t h -> p (t h)"), proj[0][:, 0:NT * 24], 1 / WS, None,
                                ALU.mult).then_inc(s_ba_ev, 1)
                v.wait_ge(s_ba_ev, 1)
                a = ba[:, :, H:2 * H]
                ch(v.tensor_tensor(a, a, over(dtb[:], 1, [P, NT, H]), ALU.add))
                ch(v.tensor_scalar(s1b[:], a, -1.0, None, ALU.mult))
                v.tensor_tensor(s1a[:], a, s1b[:], ALU.min).then_inc(s_na, 1)
                ch(v.tensor_scalar(g[:], a, 0.0, None, ALU.max))
                v.wait_ge(s_ea, 1)
                ch(v.tensor_scalar(s1b[:], s1a[:], 2.0, None, ALU.add))
                ch(v.reciprocal(s1b[:], s1b[:]))
                ch(v.tensor_tensor(s1a[:], s1a[:], s1b[:], ALU.mult))
                ch(v.tensor_tensor(s1b[:], s1a[:], s1a[:], ALU.mult))
                v.wait_ge(s_ealog, 1)
                ch(v.tensor_scalar(alog[:], s1c[:, 0, :], -1.0, None, ALU.mult))
                ch(v.tensor_scalar(s1c[:], s1b[:], 1 / 17.0, None, ALU.mult))
                for n in (15, 13, 11, 9, 7, 5, 3):
                    ch(v.scalar_tensor_tensor(s1c[:], s1c[:], 1.0 / n, s1b[:], ALU.add, ALU.mult))
                ch(v.scalar_tensor_tensor(s1c[:], s1c[:], 1.0, s1a[:], ALU.add, ALU.mult))
                ch(v.scalar_tensor_tensor(g[:], s1c[:], 2.0, g[:], ALU.mult, ALU.add))
                v.tensor_tensor(g[:], g[:], over(alog[:], 1, [P, NT, H]), ALU.mult).then_inc(s_g, 1)
                v.wait_ge(s_eb, 1)
                ch(v.tensor_scalar(beta[:], beta[:], 1.0, None, ALU.add))
                v.reciprocal(beta[:], beta[:]).then_inc(s_beta, 1)
                for i in range(1, NW):
                    w_low(i)
                v.wait_ge(s_wh, 5)
                v.scalar_tensor_tensor(wol[:], wo32[:], WS, woh[:], ALU.mult, ALU.subtract).then_inc(s_wl, 1)
                for t in range(NT):
                    v.wait_ge(s_F, 2 * t + 2)
                    i = v.tensor_tensor(F[:, t], F[:, t], over(incl, 1, [P, H, T]), ALU.mult)
                i.then_inc(s_Fm, 1)
                v.wait_ge(s_Fm, 1)
                v.wait_ge(s_zero, 3)
                v.wait_ge(s_X, 16)
                v.wait_ge(s_beta, 1)

                cc, bc, ec = TileChain(v, dtile), TileChain(v, dback), TileChain(v, dend)

                def conv(t, u):
                    tap_done.wait(v, t, u + 1)
                    n = 4 if u < 6 else 3
                    marks = [0] * n
                    for tap in range(1, 3):
                        for c in range(n):
                            if tap > 1:
                                cc.wait(marks[c])
                            src = proj[u % 2][:, c * P:(c + 1) * P].rearrange("p (b t) -> p b t", b=2)[:, :, 0:T - tap]
                            dst = acc[:, u % 2, c, :].rearrange("p (b t) -> p b t", b=2)[:, :, tap:T]
                            i = v.scalar_tensor_tensor(dst, src, cw[:, 4 * u + c, 3 - tap:4 - tap], dst, ALU.mult, ALU.add)
                            if tap < 2:
                                marks[c] = cc.mark(i)
                            elif c == n - 1:
                                i.then_inc(conv_done.sem, 1)
                            yield

                def gram_use(t, u):
                    gram_ready.wait(v, t, u + 1)
                    q = t.parity
                    if u == 0:
                        sol_ready.wait(v, t.before(2), SOLVE)
                    for b in range(2):
                        r = slice(b * T, (b + 1) * T)
                        for a in range(2):
                            src = gram[u % 2][r, :].rearrange("p (h a n) -> p h a n", h=2, a=2)[:, :, a, r]
                            i = v.tensor_tensor(UP[r, q, 2 * u:2 * u + 2, a, r], src,
                                                F[r, bass.ds(t.value(1), 1), 2 * u:2 * u + 2, :].rearrange("p a h t -> p (a h) t"),
                                                ALU.mult)
                            if b == a == 1:
                                i.then_inc(gram_used.sem, 1)
                            yield

                def norms_out(t):
                    norm_ready.wait(v, t, 6)
                    q = t.parity
                    v.tensor_scalar(n2[:, q], small[:, q * 24:q * 24 + 24], 1e-6, None, ALU.add).then_inc(n2_done.sem, 1)
                    n2_done.wait(v, t, 1)
                    cc(v.reciprocal(Bp[:, q], n2[:, q, 0:H]))
                    v.tensor_tensor(Bp[:, q], Bp[:, q], beta[:, bass.ds(t.value(1), 1), :].rearrange("p a h -> p (a h)"),
                                    ALU.mult).then_inc(bp_done.sem, 1)

                def v_scale(t):
                    vt_ready.wait(v, t, 1)
                    rn_done.wait(v, t, 1)
                    q = t.parity
                    v.tensor_tensor(V[:, q].rearrange("p (h d) -> p h d", h=H),
                                    small[:, T:T + HV].rearrange("p (h d) -> p h d", h=H),
                                    over(absk[:, q], 2, [P, H, DV]), ALU.mult).then_inc(v_done.sem, 1)

                def eliminate(t, s0, s1):
                    if s0 == 0:
                        ue_loaded.wait(v, t, 32)
                        yd_stored.wait(v, t.before(), 32)
                        bc.mark(v.tensor_copy(Yn[0:2 * YP], eyes[0:2 * YP]))
                        yield
                    for s in range(s0, s1):
                        n, m = s // 2 + 1, BLK - 1 - s
                        bc.wait()
                        bc.mark(v.tensor_tensor(Yt[0:2 * YP, 0:n, 0:m], Yn[0:2 * YP, 0:n, s:s + 1].broadcast_to([2 * YP, n, m]),
                                                Ue[0:2 * YP, s:s + 1, s + 1:].broadcast_to([2 * YP, n, m]), ALU.mult))
                        yield
                        bc.wait()
                        i = v.tensor_tensor(Yn[0:2 * YP, 0:n, s + 1:], Yn[0:2 * YP, 0:n, s + 1:], Yt[0:2 * YP, 0:n, 0:m],
                                            ALU.subtract)
                        if s == BLK - 2:
                            i.then_inc(y_done.sem, 1)
                        else:
                            bc.mark(i)
                        yield

                def sol_use(t, k):
                    sol_ready.wait(v, t, k)
                    q = t.parity
                    src, dst = sol[k % 2][:, 0:HV], w[:, (k + 1) % 2]
                    if k == SOLVE - 1:
                        i = v.tensor_tensor(dst.rearrange("p (h d) -> p h d", h=H), src.rearrange("p (h d) -> p h d", h=H),
                                            over(Bp[:, q], 2, [P, H, DV]), ALU.mult)
                    elif k % 2:
                        i = v.tensor_copy(dst, src)
                    else:
                        i = v.tensor_tensor(dst, V[:, q], src, ALU.subtract)
                    i.then_inc(sol_used.sem, 1)

                def end(t, part):
                    q = t.parity
                    xt = X[:, bass.ds(t.value(1), 1), :].rearrange("p a d -> p (a d)")
                    if part == 1:
                        ec.start(t)
                        sqo_done.wait(v, t, 1)
                        v.tensor_reduce(ms[:], sqo[:].rearrange("p (h d) -> p h d", h=H), AX.X, ALU.add).then_inc(ms_done.sem, 1)
                    elif part == 2:
                        rr_done.wait(v, t, 1)
                        onT_ready.wait(v, t.before(), 1)
                        ec(v.tensor_tensor(on[:].rearrange("p (h d) -> p h d", h=H),
                                           sol[0][:, 0:HV].rearrange("p (h d) -> p h d", h=H),
                                           over(rr[:], 2, [P, H, DV]), ALU.mult))
                        gsn_done.wait(v, t, 1)
                        v.tensor_tensor(on[:], on[:], gs[:, q], ALU.mult).then_inc(on_done.sem, 1)
                    elif part == 3:
                        onh_done.wait(v, t, 1)
                        wo_ready.wait(v, t.before(), 1)
                        v.tensor_tensor(onl[:].rearrange("p c n -> p (c n)"), turn[:, 0:HV],
                                        onh[:].rearrange("p c n -> p (c n)"), ALU.subtract).then_inc(onl_done.sem, 1)
                    elif part == 4:
                        wo_ready.wait(v, t, 1)
                        v.scalar_tensor_tensor(y[:], sol[1][:, 0:D], 1 / WS, xt, ALU.mult, ALU.add).then_inc(res_done.sem, 1)
                        res_done.wait(v, t, 1)
                        ec(v.bn_stats(st[:], y[:]))
                        v.memset(spare[:], 0.0)
                        v.bn_aggr(mv[:], st[:]).then_inc(mv_done.sem, 1)
                    else:
                        rs_done.wait(v, t, 1)
                        v.tensor_scalar(xt, y[:], mv[:, 0:1], rs[:, 0:1], ALU.subtract, ALU.mult)

                def ending(tf, part):
                    if tf is not None:
                        end(tf, part)
                        yield

                def cut_steps(t, tb, point):
                    if t is None:
                        if tb is not None and point == 0:
                            cut.mean(v, 0)
                        early = {"w1": (0, 1), "w3": (1, 2), 1: (2, 3), 6: (3, 4), 7: (4, 7)} if tb is not None else \
                            {"w1": (7, 9), "w2": (9, 11), "w3": (11, 13), 2: (13, 14), 6: (14, 15), 7: (15, 16)}
                        for n in range(*early.get(point, (0, 0))):
                            cut.dve_step(v, n)

                def front(t, tb, tf):
                    elim = {0: (5, 9), 1: (9, 16), 2: (16, 22), 3: (22, 27), 4: (27, 31)}
                    ends = {2: 2, 6: 5}
                    early_ends = {5: 3, 6: 4}
                    if t is not None:
                        cc.start(t)
                    if tb is not None:
                        bc.start(tb)
                    for u in range(7):
                        cut_steps(t, tb, u)
                        if tf is not None and u == 0:
                            sol_use(tf, 1)
                            cut_steps(t, tb, "w1")
                        if t is not None and u == 0:
                            weave(conv(t, 0))
                        if tf is not None and u == 0:
                            sol_use(tf, 2)
                            cut_steps(t, tb, "w2")
                        if u == 0:
                            weave(conv(t, 1) if t is not None else iter(()),
                                  eliminate(tb, 0, 5) if tb is not None else iter(()))
                        if tf is not None and u == 0:
                            sol_use(tf, 3)
                            cut_steps(t, tb, "w3")
                        if tb is not None and u == 0:
                            v_scale(tb)
                        if tf is not None and u in early_ends:
                            end(tf, early_ends[u])
                        work = []
                        if t is not None and u > 0:
                            work.append(chain(conv(t, u + 1) if u < 6 else (), ending(tf, 1) if u == 1 else (),
                                              gram_use(t, u - 1)))
                        elif u == 1:
                            weave(ending(tf, 1))
                        if tb is not None and u in elim:
                            work.append(eliminate(tb, *elim[u]))
                        weave(*work)
                        if t is not None and u == 6:
                            norms_out(t)
                        if tf is not None and u in ends:
                            end(tf, ends[u])
                    cut_steps(t, tb, 7)

                woven_tiles(v, front)


NH2 = 32
F8MAX = 448.0
QSCALE = P ** -0.5


def skewed_units(eng, ahead, unit):
    ahead(Tile(0))

    def whole(n):
        t = n // UN
        unit(Tile(n - 1) if n else None, Tile(n), Tile(n + 1) if n + 1 < UN * NT else None,
             Tile(t - 1) if n % UN == 1 and t else None)

    for n in range(2 * UN):
        whole(n)
    with eng.Fori(0, NT - 3) as i:
        for u in range(2 * UN, 3 * UN):
            unit(Tile(u - 1, i, UN), Tile(u, i, UN), Tile(u + 1, i, UN), Tile(1, i, 1) if u % UN == 1 else None)
    for n in range(UN * (NT - 1), UN * NT):
        whole(n)
    unit(Tile(UN * NT - 1), None, None, None)
    unit(None, None, None, Tile(NT - 1))


def last_unit(t):
    return Tile(t.off * UN + UN - 1, t.reg, UN)


def stage2(nc, io, X, cut, ew):
    with ExitStack() as ctx:
        def sb(name, shape, dt=F32):
            return ctx.enter_context(nc.sbuf_tensor(name, [P] + shape, dt))

        def pb(name):
            return ctx.enter_context(nc.psum_tensor(name, [P, 512], F32))

        def sem(name):
            return ctx.enter_context(nc.semaphore(name))

        def sig(name, per):
            return Signal(sem(name), per)

        w2h, w2l = cut.w2h, cut.w2l
        wp = sb("wp", [NH2, D], F16)
        ch_ = sb("ctxh", [KT, NTOK], F16)
        cl_ = sb("ctxl", [KT, NTOK], F16)
        ident = cut.ident
        prm = cut.prm
        lnw, lnb = prm[:, 0:2], prm[:, 2:4]
        insc = cut.insc
        lnp = prm[:, 12:20]
        wsc = prm[:, 20:26]
        smooth = prm[:, 26:58]
        rinsc = sb("rinsc", [8])
        rsm = sb("rsm", [NH2])
        pscale = sb("pscale", [1])
        epsw = sb("epsw", [4])
        mhalf = sb("mhalf2", [4])
        xn = sb("xn", [NT, D])
        lnT = sb("lnT", [NT, KT, P])
        xq = sb("xq", [NT, 4, KT, P], BF16)
        mag = sb("mag", [8, P], BF16)
        st = sb("st2", [NT, 6])
        mv = sb("mv2", [NT, 2])
        rs = sb("rs2", [NT, 1])
        spare = sb("spare2", [1])
        sq = sb("sq2", [3, 4, P])
        qn = sb("qn", [3, 512])
        ms = sb("ms2", [3, 4])
        rq = sb("rq", [3, 4])
        qT = sb("qT", [2, 4, 2, 2, T])
        kT = sb("kT", [2, 4, P])
        V = sb("V2", [2, 512])
        mx = sb("mx", [8])
        sc = sb("sc", [2, 512])
        sm = sb("sm", [8])
        rc = sb("rc", [8])
        PT = sb("PT", [512])
        cat = sb("cat", [NH2, P], BF16)
        cmag = sb("cmag", [8, P], BF16)
        y = sb("y2", [D])

        pj = [pb("pjA"), pb("pjB"), pb("pjC")]
        tq, scb, ptb = pb("tq"), pb("scb"), pb("ptb")
        pv = [pb("pv0"), pb("pv1")]

        s_xs = sem("x_by_input")
        s_c2 = sem("const2_done")
        s_mv, s_rs, s_xn, s_xT, s_xq = sem("pre_mv"), sem("pre_rs"), sem("pre_xn"), sem("pre_xT"), sem("pre_xq")
        s_ln = sem("pre_ln")
        dch, pch = sem("dve_setup2"), sem("pool_setup2")
        dun, pun, dti, pti = sem("dve_unit"), sem("pool_unit"), sem("dve_tile2"), sem("pool_tile2")
        dqu = sem("dve_quantise")
        q_ready, v_ready = sig("q_ready", 3), sig("v_ready", 1)
        ms_done, rq_done, qn_done = sig("ms2_done", 3), sig("rq_done", 3), sig("qn_done", 3)
        tq_ready, tq_used, v_used = sig("tq_ready", 3), sig("tq_used", 3), sig("v_used", 1)
        sc_ready, sub_done, exp_done, p_done = sig("sc_ready", 1), sig("sub_done", 1), sig("exp_done", 1), sig("p_done", 1)
        rc_done = sig("rc_done", 1)
        pt_ready, pt_used, pv_ready, y_done, cat_done = (sig("pt_ready", 1), sig("pt_used", 1), sig("pv_ready", 1),
                                                         sig("y2_done", 1), sig("cat_done", 1))
        wp_ready, mv_done, rs_done, yt_done = (sig("wp_ready", 1), sig("mv2_done", 1), sig("rs2_done", 1),
                                                        sig("yt_done", 1))

        def turned(c):
            return pj[c] if c else tq

        def is_self(u):
            return u < UN // 2

        cuts = {1: cut.chunks("ctx")}
        cuts.update({3 + j: cut.chunks("wp")[4 * j:4 * j + 4] for j in range(2)})
        quants = {n: [n + 1] for n in range(NT - 1)}

        def with_setup(step, unit):
            def both(l, n, m, te):
                if n is not None and n.reg is None:
                    step(n.off)
                unit(l, n, m, te)
            return both

        with nc.Block() as block:
            @block.sync
            def _(sp):
                for n in range(EARLY, len(cut.order)):
                    cut.load(sp, n)
                sp.wait_ge(cut.high_done, len(cut.order))
                for n in range(ew.first):
                    ew.load(sp, n)
                ew.load_router(sp)
                sp.wait_ge(v_ready.sem, UN * NT)
                for n in range(ew.first, ew.count):
                    ew.load(sp, n)

            @block.tensor
            def _(pe):
                pe.wait_ge(cut.prm_loaded, 32)
                for t in range(NT):
                    pe.wait_ge(s_xn, t + 1)
                    if t >= 2:
                        pe.wait_ge(s_ln, t - 1)
                    for k in range(KT):
                        i = pe.transpose(pj[t % 2][:, k * P:(k + 1) * P], xn[:, t, k * P:(k + 1) * P], ident[:])
                    i.then_inc(s_xT, 1)
                pe.wait_ge(s_ln, NT)

                def chunk(n, c):
                    u = n.off % UN
                    if c == 0:
                        v_used.wait(pe, n.before(), 1)
                    elif c == 3:
                        qn_done.wait(pe, n, 1)
                    else:
                        tq_used.wait(pe, n.before(), c + 1)
                    if n.reg is None and n.off == 2 and c == 2:
                        pe.wait_ge(cut.low_done, EARLY + 2)
                    if n.reg is None and c == 0 and n.off % UN == 0 and n.off <= 2 * UN:
                        pe.wait_ge(s_xq, n.off // UN + 1 if n.off < 2 * UN else NT)
                    tile = tile_of(n)
                    if is_self(u):
                        s = (0, 0, 2, 3)[c]
                        terms = [(xq[:, bass.ds(tile, 1), s, k, :].rearrange("p a n -> p (a n)"), w[:, u, c, k, :])
                                 for k in range(KT) for w in (w2h, w2l)]
                    elif c < 2:
                        terms = [(xq[:, bass.ds(tile, 1), 1, k, :].rearrange("p a n -> p (a n)"), w[:, u, c, k, :])
                                 for k in range(KT) for w in (w2h, w2l)]
                    else:
                        tok = bass.ds(tile * P, P)
                        terms = [(x, w) for k in range(KT) for x, w in (
                            (ch_[:, k, tok], w2h[:, u, c, k, :]), (ch_[:, k, tok], w2l[:, u, c, k, :]),
                            (cl_[:, k, tok], w2h[:, u, c, k, :]))]
                    for j, (x, w) in enumerate(terms):
                        i = pe.matmul(pj[c % 3][:], x, w, start=j == 0, stop=j == len(terms) - 1)
                    i.then_inc((v_ready if c == 3 else q_ready).sem, 1)

                def tile_of(n):
                    return n.off // UN if n.reg is None else n.reg + n.off // UN

                def turn(n, c):
                    qn_done.wait(pe, n, c + 1)
                    if c == 0:
                        tq_used.wait(pe, n.before(), 1)
                    bank = turned(c)
                    for j in range(4):
                        dst = bank[:, j * P:(j + 1) * P]
                        if c < 2:
                            dst = bank[:, j // 2 * D:(j // 2 + 1) * D].rearrange("p (b h s) -> p h b s", b=2, h=2)[:, j % 2]
                        i = pe.transpose(dst, qn[:, c, j * P:(j + 1) * P], ident[:])
                    i.then_inc(tq_ready.sem, 1)

                def scores(n):
                    tq_used.wait(pe, n, 3)
                    sub_done.wait(pe, n.before(), 1)
                    q = n.parity
                    for g in range(4):
                        for b in range(2):
                            s = slice(b * T, (b + 1) * T)
                            i = pe.matmul(scb[:, g * P + b * T:g * P + (b + 1) * T], qT[:, q, g, b].rearrange("p h s -> p (h s)"),
                                          kT[:, q, g, s], start=True, stop=True)
                    i.then_inc(sc_ready.sem, 1)

                def turn_p(n, te):
                    p_done.wait(pe, n, 1)
                    pt_used.wait(pe, n.before(), 1)
                    if te is not None:
                        yt_done.wait(pe, te, 1)
                    for g in range(4):
                        i = pe.transpose(ptb[:, g * P:(g + 1) * P], sc[:, n.parity, g * P:(g + 1) * P], ident[:])
                    i.then_inc(pt_ready.sem, 1)

                def values(n):
                    pt_used.wait(pe, n, 1)
                    v_used.wait(pe, n, 1)
                    y_done.wait(pe, n.before(), 1)
                    for g in range(4):
                        for b in range(2):
                            r = slice(b * T, (b + 1) * T)
                            i = pe.matmul(pv[b][:, g * P:(g + 1) * P], V[r, n.parity, g * P:(g + 1) * P],
                                          PT[r, g * P:(g + 1) * P], start=True, stop=True)
                    i.then_inc(pv_ready.sem, 1)

                def project(te, l):
                    cat_done.wait(pe, last_unit(te), 1)
                    pt_used.wait(pe, last_unit(te) if l is None else l, 1)
                    if te.reg is None and te.off == 0:
                        pe.wait_ge(cut.high_done, len(cut.order))
                    for h in range(NH2):
                        i = pe.matmul(ptb[:, 0:D], cat[:, h, :], wp[:, h, :], start=h == 0, stop=h == NH2 - 1)
                    i.then_inc(wp_ready.sem, 1)

                def ahead(n):
                    for c in range(4):
                        chunk(n, c)
                    for c in range(3):
                        turn(n, c)
                    scores(n)

                def unit(l, n, m, te):
                    if m is not None:
                        chunk(m, 0)
                        chunk(m, 1)
                        chunk(m, 2)
                    if te is not None:
                        project(te, l)
                    if l is not None:
                        values(l)
                    if m is not None:
                        turn(m, 0)
                        chunk(m, 3)
                        turn(m, 1)
                        turn(m, 2)
                    if n is not None:
                        turn_p(n, te)
                    if m is not None:
                        scores(m)

                skewed_units(pe, ahead, unit)

            @block.scalar
            def _(act):
                act.wait_ge(cut.prm_loaded, 32)
                for t in range(NT):
                    act.wait_ge(s_xT, t + 1)
                    for k in range(KT):
                        i = act.activation(lnT[:, t, k], pj[t % 2][:, k * P:(k + 1) * P], ACT.Identity,
                                           bias=lnb[:, k:k + 1], scale=lnw[:, k:k + 1])
                    i.then_inc(s_ln, 1)

                def step(n):
                    for m in cuts.get(n, []):
                        cut.wait_loaded(act, m)
                        what, a, _ = cut.order[m]
                        if what == "ctx":
                            cut.high(act, m, ch_[:, :, a * 512:(a + 1) * 512])
                        else:
                            cut.high(act, m, wp[:, a * 4:(a + 1) * 4, :].rearrange("p n c -> p (n c)"))

                def mean_square(n, c):
                    q_ready.wait(act, n, c + 1)
                    rq_done.wait(act, n.before(), c + 1)
                    for h in range(4):
                        i = act.activation(sq[:, c, h], pj[c][:, h * P:(h + 1) * P], ACT.Square, scale=P ** -0.5,
                                           accum_out=ms[:, c, h:h + 1])
                    i.then_inc(ms_done.sem, 1)

                def affine(n, c):
                    tq_ready.wait(act, n, c + 1)
                    if c == 0:
                        sc_ready.wait(act, n.before(2), 1)
                    j = (0 if is_self(n.off % UN) else 1) + (2 if c == 2 else 0)
                    if c == 2:
                        dst = kT[:, n.parity].rearrange("p g n -> p (g n)")
                    else:
                        dst = qT[:, n.parity, 2 * c:2 * c + 2].rearrange("p g b h s -> p (g b h s)")
                    act.activation(dst, turned(c)[:], ACT.Identity, bias=lnp[:, 2 * j + 1:2 * j + 2],
                                   scale=lnp[:, 2 * j:2 * j + 1]).then_inc(tq_used.sem, 1)

                def copy_v(n):
                    v_ready.wait(act, n, 1)
                    pv_ready.wait(act, n.before(2), 1)
                    act.activation(V[:, n.parity], pj[0][:], ACT.Copy).then_inc(v_used.sem, 1)

                def ahead(n):
                    for c in range(3):
                        mean_square(n, c)
                    copy_v(n)
                    for c in range(3):
                        affine(n, c)

                def unit(l, n, m, te):
                    if m is not None:
                        mean_square(m, 0)
                        mean_square(m, 1)
                        mean_square(m, 2)
                    if n is not None:
                        sub_done.wait(act, n, 1)
                        act.activation(sc[:, n.parity], sc[:, n.parity], ACT.Exp, scale=QSCALE).then_inc(exp_done.sem, 1)
                    if m is not None:
                        affine(m, 0)
                        affine(m, 1)
                        affine(m, 2)
                        copy_v(m)
                    if n is not None:
                        pt_ready.wait(act, n, 1)
                        pv_ready.wait(act, n.before(), 1)
                        act.activation(PT[:], ptb[:], ACT.Copy).then_inc(pt_used.sem, 1)

                skewed_units(act, ahead, with_setup(step, unit))

            @block.gpsimd
            def _(pool):
                ch = Chain(pool, pch)
                ch(pool.memset(mhalf[:], -0.5))
                pool.wait_ge(s_c2, 1)
                def inv_dev_x(t):
                    pool.wait_ge(s_mv, t + 1)
                    ch(pool.tensor_scalar(rs[:, t], mv[:, t, 1:2], EPS, 1.0, ALU.add, ALU.mult))
                    pool.tensor_tensor(rs[:, t], rs[:, t], mhalf[:, 0:1], ALU.pow).then_inc(s_rs, 1)

                def by_input(t):
                    pool.wait_ge(s_ln, t + 1)
                    for s in range(4):
                        i = pool.tensor_tensor(xq[:, t, s], lnT[:, t], over(rinsc[:, 2 * s:2 * s + 2], 2, [P, KT, P]), ALU.mult)
                    i.then_inc(s_xs, 1)

                def step(n):
                    for t in quants.get(n + 1, []):
                        by_input(t)

                for t in range(3):
                    inv_dev_x(t)
                by_input(0)
                for t in range(3, NT):
                    inv_dev_x(t)
                for t in quants[0]:
                    by_input(t)
                pc = TileChain(pool, pun)

                def inv_dev(n, c):
                    ms_done.wait(pool, n, c + 1)
                    j = (0 if is_self(n.off % UN) else 1) + (2 if c == 2 else 0)
                    pc(pool.tensor_tensor(rq[:, c], ms[:, c], epsw[:, j:j + 1].broadcast_to([P, 4]), ALU.add))
                    pool.tensor_tensor(rq[:, c], rq[:, c], mhalf[:], ALU.pow).then_inc(rq_done.sem, 1)

                def ahead(n):
                    pc.start(n)
                    for c in range(3):
                        inv_dev(n, c)

                tc = TileChain(pool, pti)

                def unit(l, n, m, te):
                    if m is not None:
                        pc.start(m)
                        inv_dev(m, 0)
                        inv_dev(m, 1)
                        inv_dev(m, 2)
                    if n is not None:
                        rc_done.wait(pool, n, 1)
                        v = sc[:, n.parity].rearrange("p (g t) -> p g t", t=T)
                        pool.tensor_tensor(v, v, over(rc[:], 2, [P, 8, T]), ALU.mult).then_inc(p_done.sem, 1)
                    if te is not None:
                        tc.start(te)
                        mv_done.wait(pool, te, 1)
                        tc(pool.tensor_tensor(rs[:, 0], mv[:, 0, 1:2], spare[:], ALU.add))
                        pool.tensor_tensor(rs[:, 0], rs[:, 0], mhalf[:, 0:1], ALU.pow).then_inc(rs_done.sem, 1)

                skewed_units(pool, ahead, with_setup(step, unit))

            @block.vector
            def _(v):
                ch = Chain(v, dch)
                v.wait_ge(cut.prm_loaded, 32)
                v.memset(spare[:], EPS)
                v.reciprocal(rinsc[:], insc)
                v.tensor_tensor(pscale[:], wsc[:, 4:5], wsc[:, 5:6], ALU.mult)
                ch(v.reciprocal(rsm[:], smooth))
                v.tensor_scalar(rsm[:, 16:], rsm[:, 16:], 1 / WS, None, ALU.mult)
                v.tensor_scalar(rsm[:, 0:16], rsm[:, 0:16], wsc[:, 3:4], None, ALU.mult)
                ch(v.tensor_tensor(epsw[:, 0:3], wsc[:, 0:3], wsc[:, 0:3], ALU.mult))
                ch(v.reciprocal(epsw[:, 0:3], epsw[:, 0:3]))
                ch(v.tensor_scalar(epsw[:, 0:3], epsw[:, 0:3], EPS, None, ALU.mult))
                v.memset(epsw[:, 3:4], EPS * WS * WS).then_inc(s_c2, 1)

                def quantise(yv, mg, last):
                    ch2 = last["chain"]
                    ch2(v.tensor_scalar(yv, yv, F8MAX, -F8MAX, ALU.min, ALU.max))
                    ch2(v.tensor_scalar(mg.bitcast(U16), yv.bitcast(U16), 0x7F80, None, ALU.bitwise_and))
                    ch2(v.tensor_scalar(mg, mg, 2.0 ** -6, 24.0, ALU.max, ALU.mult))
                    ch2(v.tensor_tensor(yv, yv, mg, ALU.add))
                    v.tensor_tensor(yv, yv, mg, ALU.subtract).then_inc(last["sem"], 1)

                def quant_x(t):
                    v.wait_ge(s_xs, t + 1)
                    quantise(xq[:, t].rearrange("p s k n -> p (s k) n"), mag[:], {"chain": ch, "sem": s_xq})

                def step(n):
                    for m in cuts.get(n, []):
                        what, a, _ = cut.order[m]
                        if what == "ctx":
                            half = slice(a * 512, (a + 1) * 512)
                            cut.low(v, m, ch_[:, :, half], cl_[:, :, half])
                    for t in quants.get(n, []):
                        quant_x(t)

                def stats(t):
                    ch(v.bn_stats(st[:, t], X[:, t, :]))
                    v.bn_aggr(mv[:, t], st[:, t]).then_inc(s_mv, 1)

                def normalise(t):
                    v.wait_ge(s_rs, t + 1)
                    v.tensor_scalar(xn[:, t], X[:, t, :], mv[:, t, 0:1], rs[:, t], ALU.subtract, ALU.mult).then_inc(s_xn, 1)

                for t in range(NT):
                    stats(t)
                    if t >= 2:
                        normalise(t - 2)
                    if t == 4:
                        quant_x(0)
                normalise(NT - 2)
                normalise(NT - 1)

                uc, qc, tc = TileChain(v, dun), TileChain(v, dqu), TileChain(v, dti)

                def scale(n, c):
                    rq_done.wait(v, n, c + 1)
                    tq_ready.wait(v, n.before(), c + 1)
                    v.tensor_tensor(qn[:, c].rearrange("p (h d) -> p h d", d=P), pj[c][:].rearrange("p (h d) -> p h d", d=P),
                                    over(rq[:, c], 2, [P, 4, P]), ALU.mult).then_inc(qn_done.sem, 1)

                def ahead(n):
                    for c in range(3):
                        scale(n, c)

                def spread(n):
                    uc.start(n)
                    sc_ready.wait(v, n, 1)
                    s3 = scb[:].rearrange("p (g t) -> p g t", t=T)
                    uc(v.tensor_reduce(mx[:], s3, AX.X, ALU.max))
                    pt_ready.wait(v, n.before(2), 1)
                    v.tensor_tensor(sc[:, n.parity].rearrange("p (g t) -> p g t", t=T), s3, over(mx[:], 2, [P, 8, T]),
                                    ALU.subtract).then_inc(sub_done.sem, 1)

                def inv_sum(n):
                    exp_done.wait(v, n, 1)
                    uc(v.tensor_reduce(sm[:], sc[:, n.parity].rearrange("p (g t) -> p g t", t=T), AX.X, ALU.add))
                    p_done.wait(v, n.before(), 1)
                    v.reciprocal(rc[:], sm[:]).then_inc(rc_done.sem, 1)

                def quant_values(l):
                    qc.start(l)
                    pv_ready.wait(v, l, 1)
                    u = l.off % UN
                    if u == 0:
                        wp_ready.wait(v, Tile(l.off // UN - 1, l.reg, 1), 1)
                    for b in range(2):
                        i = v.tensor_tensor(cat[:, 8 * u:8 * u + 8, b * T:(b + 1) * T],
                                            pv[b][:].rearrange("p (h s) -> p h s", s=T),
                                            over(rsm[:, 8 * u:8 * u + 8], 2, [P, 8, T]), ALU.mult)
                    i.then_inc(y_done.sem, 1)
                    y_done.wait(v, l, 1)
                    quantise(cat[:, 8 * u:8 * u + 8, :], cmag[:], {"chain": qc, "sem": cat_done.sem})

                def unit(l, n, m, te):
                    if n is not None:
                        spread(n)
                    if m is not None:
                        scale(m, 0)
                        scale(m, 1)
                    if n is not None:
                        inv_sum(n)
                    if m is not None:
                        scale(m, 2)
                    if te is not None:
                        tc.start(te)
                        wp_ready.wait(v, te, 1)
                        xt = X[:, bass.ds(te.value(1), 1), :].rearrange("p a d -> p (a d)")
                        v.scalar_tensor_tensor(y[:], ptb[:, 0:D], pscale[:, 0:1], xt, ALU.mult, ALU.add).then_inc(yt_done.sem, 1)
                        yt_done.wait(v, te, 1)
                        tc(v.bn_stats(st[:, 0], y[:]))
                        v.memset(mx[:, 0:1], 0.0)
                        v.bn_aggr(mv[:, 0], st[:, 0]).then_inc(mv_done.sem, 1)
                    if l is not None:
                        quant_values(l)
                    if te is not None:
                        rs_done.wait(v, te, 1)
                        v.tensor_scalar(xt, y[:], mv[:, 0, 0:1], rs[:, 0], ALU.subtract, ALU.mult)

                skewed_units(v, ahead, with_setup(step, unit))


E = 8
FE = 176
FC = 2 * FE
NC3 = 6
FF = NC3 * FC
NB3 = -(-FF // P)
DVE_DOWN = 3
NG3 = -(-NB3 // 4)


def skewed_tiles(eng, front):
    front(Tile(0), None)
    front(Tile(1), Tile(0))
    front(Tile(2), Tile(1))
    with eng.Fori(0, (NT - 4) // 2) as i:
        front(Tile(3, i), Tile(2, i))
        front(Tile(4, i), Tile(3, i))
    front(Tile(NT - 1), Tile(NT - 2))
    front(None, Tile(NT - 1))


class ExpertWeights:

    def __init__(self, nc, ctx, io, cut):
        self.io = io
        self.size = 4 * FC
        self.count = NC3 + NG3
        self.first = cut.NSLOT * KT * 512 // self.size
        self.raw = cut.region[:, 0:self.count * self.size].rearrange("p (n c) -> p n c", c=self.size)
        self.wr32 = ctx.enter_context(nc.sbuf_tensor("wr32", [P, KT, E + 1], F32))
        self.iota = ctx.enter_context(nc.sbuf_tensor("iota", [P, E], F32))
        self.ident = cut.ident
        self.router_loaded = ctx.enter_context(nc.semaphore("router_loaded"))
        self.groups = [range(n, n + 2) for n in range(0, NC3, 2)] + [range(NC3, self.count)]
        self.loaded = [ctx.enter_context(nc.semaphore(f"expert_w_loaded{n}")) for n in range(len(self.groups))]

    def load_router(self, sp):
        sp.dma_start(self.iota[:], self.io["iota"]).then_inc(self.router_loaded, 16)
        sp.dma_start(self.wr32[:], self.io["wr"].rearrange("(k p) n -> p k n", p=P)).then_inc(self.router_loaded, 16)

    def group(self, n):
        return min(n, NC3) // 2

    def wait_loaded(self, eng, n):
        g = self.group(n)
        eng.wait_ge(self.loaded[g], 16 * len(self.groups[g]))

    def load(self, sp, n):
        if n < NC3:
            src = self.io["wu"].rearrange("(k p) n -> p k n", p=P)[:, :, n * 2 * FC:(n + 1) * 2 * FC]
            dst = self.raw[:, n].rearrange("p (k n) -> p k n", k=KT)
        else:
            b = 4 * (n - NC3)
            m = min(4, NB3 - b)
            src = self.io["wd"].rearrange("(n p) c -> p n c", p=P)[:, b:b + m, :]
            dst = self.raw[:, n, 0:m * D].rearrange("p (n c) -> p n c", c=D)
        sp.dma_start(dst, src).then_inc(self.loaded[self.group(n)], 16)


def stage3(nc, io, X, ew, out):
    with ExitStack() as ctx:
        def sb(name, shape, dt=F32):
            return ctx.enter_context(nc.sbuf_tensor(name, [P] + shape, dt))

        def pb(name):
            return ctx.enter_context(nc.psum_tensor(name, [P, 512], F32))

        def sem(name):
            return ctx.enter_context(nc.semaphore(name))

        def sig(name, per):
            return Signal(sem(name), per)

        raw = ew.raw
        ob = sb("ob", [2, D])
        wuh = sb("wuh", [NC3, KT, 2 * FC], F16)
        wul = sb("wul", [NC3, KT, 2 * FC], F16)
        wdh = sb("wdh", [NG3 * 4, D], F16)
        wdl = sb("wdl", [NG3 * 4, D], F16)
        wr32, ident, iota = ew.wr32, ew.ident, ew.iota
        wrh = sb("wrh", [KT, E + 1], F16)
        wrl = sb("wrl", [KT, E + 1], F16)
        xh = sb("x3h", [KT, NTOK], F16)
        xl = sb("x3l", [KT, NTOK], F16)
        lg = sb("lg", [NT, E + 1])
        pr = sb("pr", [NT, E])
        mx = sb("mx3", [NT])
        top = sb("top", [NT, 8])
        idx = sb("idx", [NT, 8], U32)
        idf = sb("idf", [NT, 8])
        m1 = sb("m1", [NT, E])
        m2 = sb("m2", [NT, E])
        gate = sb("gate", [NT, E + 1])
        s1 = sb("s1", [2, FC])
        h = sb("h3", [2, NB3 * P])
        hTh = sb("hTh", [2, 512], F16)
        hTl = sb("hTl", [2, 512], F16)
        y = sb("y3", [D])
        st = sb("st3", [6])
        mv = sb("mv3", [2])
        rs = sb("rs3", [1])
        epsc = sb("eps3", [1])
        mhalf = sb("mhalf3", [1])
        spare = sb("spare3", [1])

        h1b = [pb("h1a"), pb("h1b")]
        h2b = [pb("h2a"), pb("h2b")]
        tb_ = [pb("tA"), pb("tB")]
        yb = [pb("yA"), pb("yB")]

        NU = ew.count
        s_hi, s_lo, s_dlo, s_wrh, s_wrl = sem("w3_hi"), sem("w3_up_lo"), sem("w3_down_lo"), sem("wr_hi"), sem("wr_lo")
        s_xT, s_xh, s_xl, s_lg = sem("x3T"), sem("x3_hi"), sem("x3_lo"), sem("logits")
        s_mx, s_e, s_z, s_ze, s_gate, s_zero = (sem("soft_in"), sem("soft_exp"), sem("gate_in"), sem("gate_exp"),
                                                sem("gates_done"), sem("zero3"))
        dch, dti, pti, pch = sem("dve_setup3"), sem("dve_tile3"), sem("pool_tile3"), sem("pool_setup3")
        up_ready, silu_done, h_done = sig("up_ready", NC3), sig("silu3_done", NC3), sig("h_done", NC3)
        t_ready, hi_done, lo_done, down_done = (sig("t_ready", NG3), sig("hi3_done", NG3), sig("lo3_done", NG3),
                                                sig("down_done", NG3))
        yt_done, mv_done, rs_done, out_ready, stored = (sig("y3_done", 1), sig("mv3_done", 1), sig("rs3_done", 1),
                                                        sig("out_ready", 1), sig("out_stored", 16))

        def two_before(eng, s, t, k, per):
            if t.reg is not None or t.off * per + k - 1 > 0:
                eng.wait_ge(s.sem, t.value(per, k - 1))

        with nc.Block() as block:
            @block.sync
            def _(sp):
                def store(t):
                    ready, before = out_ready.count(sp, t, 1), t.before()
                    landed = stored.count(sp, before, 16) if before.exists else None
                    row = t.value(P) if t.reg is None else sp.snap(t.value(P))
                    sp.wait_ge(out_ready.sem, ready)
                    if before.exists:
                        sp.wait_ge(stored.sem, landed)
                    sp.dma_start(out[bass.ds(row, P), :], ob[:, t.parity]).then_inc(stored.sem, 16)

                def front(t, tb):
                    if tb is not None:
                        store(tb)

                skewed_tiles(sp, front)
                stored.wait(sp, Tile(NT - 1), 16)

            @block.tensor
            def _(pe):
                for t in range(NT):
                    if t >= 2:
                        pe.wait_ge(s_xl, t - 1)
                    for k in range(KT):
                        i = pe.transpose(tb_[t % 2][:, k * P:(k + 1) * P], X[:, t, k * P:(k + 1) * P], ident[:])
                    i.then_inc(s_xT, 1)
                pe.wait_ge(s_xl, NT)
                pe.wait_ge(s_wrl, 1)
                for t in range(NT):
                    tok = slice(t * P, (t + 1) * P)
                    for k in range(KT):
                        for j, (a, b) in enumerate(((xh, wrh), (xl, wrh), (xh, wrl))):
                            i = pe.matmul(yb[0][:, t * (E + 1):(t + 1) * (E + 1)], a[:, k, tok], b[:, k, :],
                                          start=k == 0 and j == 0, stop=k == KT - 1 and j == 2)
                i.then_inc(s_lg, 1)

                def up(t, c):
                    two_before(pe, h_done, t, c, NC3)
                    if t.reg is None and t.off == 0:
                        pe.wait_ge(s_lo, c + 1)
                    tok = bass.ds(t.value(P), P)
                    for bank, w0 in ((h1b[c % 2], 0), (h2b[c % 2], FC)):
                        for k in range(KT):
                            for j, (a, b) in enumerate(((xh, wuh), (xh, wul), (xl, wuh))):
                                i = pe.matmul(bank[:, 0:FC], a[:, k, tok], b[:, c, k, w0:w0 + FC],
                                              start=k == 0 and j == 0, stop=k == KT - 1 and j == 2)
                    i.then_inc(up_ready.sem, 1)

                def turn(t, g):
                    h_done.wait(pe, t, NC3)
                    two_before(pe, lo_done, t, g, NG3)
                    for j in range(min(4, NB3 - 4 * g)):
                        b = 4 * g + j
                        i = pe.transpose(tb_[(t.parity + g) % 2][:, j * P:(j + 1) * P], h[:, t.parity, b * P:(b + 1) * P],
                                         ident[:])
                    i.then_inc(t_ready.sem, 1)

                def down(t, g):
                    lo_done.wait(pe, t, g + 1)
                    if g == 0:
                        yt_done.wait(pe, t.before(2), 1)
                        if t.reg is None and t.off == 0:
                            pe.wait_ge(s_dlo, NG3)
                            pe.wait_ge(s_gate, 1)
                    q = (t.parity + g) % 2
                    m = min(4, NB3 - 4 * g)
                    for j in range(m):
                        b = 4 * g + j
                        c = slice(j * P, (j + 1) * P)
                        for x, (a, w) in enumerate(((hTh, wdh), (hTh, wdl), (hTl, wdh))):
                            i = pe.matmul(yb[t.parity][:, 0:D], a[:, q, c], w[:, b, :], start=b == 0 and x == 0,
                                          stop=b == NB3 - 1 and x == 2)
                    i.then_inc(down_done.sem, 1)

                def front(t, tb):
                    for c in range(NC3):
                        if t is not None:
                            up(t, c)
                        if tb is not None:
                            if c < NG3:
                                turn(tb, c)
                            if c > 0:
                                down(tb, c - 1)

                skewed_tiles(pe, front)

            @block.scalar
            def _(act):
                act.wait_ge(ew.router_loaded, 32)
                act.activation(wrh[:], wr32[:], ACT.Copy, scale=WS).then_inc(s_wrh, 1)

                def cut(n):
                    ew.wait_loaded(act, n)
                    if n < NC3:
                        dst, src = wuh[:, n].rearrange("p k n -> p (k n)"), raw[:, n]
                    else:
                        b = 4 * (n - NC3)
                        m = min(4, NB3 - b)
                        dst, src = wdh[:, b:b + m].rearrange("p n c -> p (n c)"), raw[:, n, 0:m * D]
                    act.activation(dst, src, ACT.Copy, scale=WS).then_inc(s_hi, 1)

                for t in range(NT):
                    act.wait_ge(s_xT, t + 1)
                    act.activation(xh[:, :, t * P:(t + 1) * P], tb_[t % 2][:, 0:D].rearrange("p (k n) -> p k n", k=KT),
                                   ACT.Copy).then_inc(s_xh, 1)
                    if t < 3:
                        cut(t)
                for n in range(3, NC3):
                    cut(n)
                act.wait_ge(s_mx, 1)
                act.activation(pr[:], pr[:], ACT.Exp).then_inc(s_e, 1)
                act.wait_ge(s_z, 1)
                act.activation(mx[:], lg[:, :, E], ACT.Exp, scale=-1.0).then_inc(s_ze, 1)
                for n in range(NC3, NU):
                    cut(n)

                def silu(t, c):
                    up_ready.wait(act, t, c + 1)
                    two_before(act, h_done, t, c, NC3)
                    act.activation(s1[:, c % 2], h1b[c % 2][:, 0:FC], ACT.Silu, scale=1 / WS).then_inc(silu_done.sem, 1)

                def high(t, g):
                    t_ready.wait(act, t, g + 1)
                    two_before(act, down_done, t, g, NG3)
                    q, n = (t.parity + g) % 2, min(4, NB3 - 4 * g) * P
                    act.activation(hTh[:, q, 0:n], tb_[q][:, 0:n], ACT.Copy).then_inc(hi_done.sem, 1)

                def front(t, tb):
                    for c in range(NC3):
                        if t is not None:
                            silu(t, c)
                        if tb is not None and c < NG3:
                            high(tb, c)

                skewed_tiles(act, front)

            @block.gpsimd
            def _(pool):
                pool.memset(epsc[:], EPS)
                pool.memset(mhalf[:], -0.5).then_inc(pch, 1)
                pool.memset(h[:, :, FF:], 0.0).then_inc(s_zero, 1)
                pool.wait_ge(pch, 1)
                for g in range(DVE_DOWN, NG3):
                    b = 4 * g
                    m = min(4, NB3 - b)
                    pool.wait_ge(s_hi, NC3 + g + 1)
                    hi, lo = (w[:, b:b + m].rearrange("p n c -> p (n c)") for w in (wdh, wdl))
                    w = raw[:, NC3 + g, 0:m * D]
                    pool.tensor_scalar(w, w, WS, None, ALU.mult).then_inc(pch, 1)
                    pool.wait_ge(pch, g - DVE_DOWN + 2)
                    pool.tensor_tensor(lo, w, hi, ALU.subtract).then_inc(s_dlo, 1)
                pc = TileChain(pool, pti)

                def front(t, tb):
                    if tb is not None:
                        pc.start(tb)
                        mv_done.wait(pool, tb, 1)
                        pc(pool.tensor_tensor(rs[:], mv[:, 1:2], epsc[:], ALU.add))
                        pool.tensor_tensor(rs[:], rs[:], mhalf[:], ALU.pow).then_inc(rs_done.sem, 1)

                skewed_tiles(pool, front)

            @block.vector
            def _(v):
                ch = Chain(v, dch)
                v.wait_ge(s_wrh, 1)
                v.scalar_tensor_tensor(wrl[:], wr32[:], WS, wrh[:], ALU.mult, ALU.subtract).then_inc(s_wrl, 1)

                def cut(n):
                    v.wait_ge(s_hi, n + 1)
                    hi, lo = (w[:, n].rearrange("p k n -> p (k n)") for w in (wuh, wul))
                    v.scalar_tensor_tensor(lo, raw[:, n], WS, hi, ALU.mult, ALU.subtract).then_inc(s_lo, 1)

                for t in range(NT):
                    v.wait_ge(s_xh, t + 1)
                    tok = slice(t * P, (t + 1) * P)
                    v.tensor_tensor(xl[:, :, tok], tb_[t % 2][:, 0:D].rearrange("p (k n) -> p k n", k=KT), xh[:, :, tok],
                                    ALU.subtract).then_inc(s_xl, 1)
                    if t < 3:
                        cut(t)
                cut(3)
                v.wait_ge(s_lg, 1)
                v.tensor_scalar(lg[:].rearrange("p t e -> p (t e)"), yb[0][:, 0:NT * (E + 1)], 1 / WS, None,
                                ALU.mult).then_inc(s_z, 1)
                v.wait_ge(s_z, 1)
                ch(v.tensor_reduce(m1[:, :, 0], lg[:, :, 0:E], AX.X, ALU.max))
                v.tensor_tensor(pr[:], lg[:, :, 0:E], over(m1[:, :, 0], 2, [P, NT, E]), ALU.subtract).then_inc(s_mx, 1)
                cut(4)
                v.wait_ge(s_e, 1)
                ch(v.tensor_reduce(m2[:, :, 0], pr[:], AX.X, ALU.add))
                ch(v.reciprocal(m2[:, :, 1], m2[:, :, 0]))
                ch(v.tensor_tensor(pr[:], pr[:], over(m2[:, :, 1], 2, [P, NT, E]), ALU.mult))
                for t in range(NT):
                    i = v.max(top[:, t], pr[:, t])
                ch(i)
                for t in range(NT):
                    i = v.max_index(idx[:, t], top[:, t], pr[:, t])
                ch(i)
                ch(v.tensor_copy(idf[:], idx[:]))
                v.wait_ge(ew.router_loaded, 32)
                v.tensor_tensor(m1[:], over(iota[:], 1, [P, NT, E]), idf[:, :, 0:1].broadcast_to([P, NT, E]), ALU.is_equal)
                ch(v.tensor_tensor(m2[:], over(iota[:], 1, [P, NT, E]), idf[:, :, 1:2].broadcast_to([P, NT, E]), ALU.is_equal))
                ch(v.tensor_tensor(m1[:], m1[:], m2[:], ALU.add))
                v.scalar_tensor_tensor(gate[:, :, 0:E], pr[:], 1 / WS, m1[:], ALU.mult, ALU.mult)
                v.wait_ge(s_ze, 1)
                ch(v.tensor_scalar(mx[:], mx[:], 1.0, None, ALU.add))
                ch(v.reciprocal(mx[:], mx[:]))
                v.tensor_scalar(gate[:, :, E], mx[:], 1 / WS, None, ALU.mult).then_inc(s_gate, 1)
                v.wait_ge(s_gate, 1)
                v.wait_ge(s_zero, 1)
                vc = TileChain(v, dti)

                def gated(t, c):
                    silu_done.wait(v, t, c + 1)
                    if c == 0:
                        t_ready.wait(v, t.before(2), NG3)
                    gt = gate[:, bass.ds(t.value(1), 1), :].rearrange("p a e -> p (a e)")
                    for j in range(2 if c < E // 2 else 1):
                        e, n = (2 * c + j, FE) if c < E // 2 else (E, FC)
                        i = v.scalar_tensor_tensor(h[:, t.parity, c * FC + j * FE:c * FC + j * FE + n],
                                                   h2b[c % 2][:, j * FE:j * FE + n], gt[:, e:e + 1],
                                                   s1[:, c % 2, j * FE:j * FE + n], ALU.mult, ALU.mult)
                    i.then_inc(h_done.sem, 1)

                def cut_down(g):
                    b = slice(4 * g, 4 * g + 4)
                    v.wait_ge(s_hi, NC3 + g + 1)
                    hi, lo = (w[:, b].rearrange("p n c -> p (n c)") for w in (wdh, wdl))
                    v.scalar_tensor_tensor(lo, raw[:, NC3 + g, 0:4 * D], WS, hi, ALU.mult, ALU.subtract).then_inc(s_dlo, 1)

                def low(t, g):
                    hi_done.wait(v, t, g + 1)
                    two_before(v, down_done, t, g, NG3)
                    q, n = (t.parity + g) % 2, min(4, NB3 - 4 * g) * P
                    v.tensor_tensor(hTl[:, q, 0:n], tb_[q][:, 0:n], hTh[:, q, 0:n], ALU.subtract).then_inc(lo_done.sem, 1)

                def finish(t):
                    down_done.wait(v, t, NG3)
                    vc.start(t)
                    xt = X[:, bass.ds(t.value(1), 1), :].rearrange("p a d -> p (a d)")
                    v.scalar_tensor_tensor(y[:], yb[t.parity][:, 0:D], 1 / WS, xt, ALU.mult, ALU.add).then_inc(yt_done.sem, 1)
                    yt_done.wait(v, t, 1)
                    vc(v.bn_stats(st[:], y[:]))
                    v.memset(spare[:], 0.0)
                    v.bn_aggr(mv[:], st[:]).then_inc(mv_done.sem, 1)
                    rs_done.wait(v, t, 1)
                    stored.wait(v, t.before(2), 16)
                    v.tensor_scalar(ob[:, t.parity], y[:], mv[:, 0:1], rs[:, 0:1], ALU.subtract,
                                    ALU.mult).then_inc(out_ready.sem, 1)

                def front(t, tb):
                    for c in range(NC3):
                        if t is not None:
                            gated(t, c)
                        if t is not None and t.reg is None and t.off == 0:
                            if c == 0:
                                cut(NC3 - 1)
                            elif c <= DVE_DOWN:
                                cut_down(c - 1)
                        if tb is not None and c < NG3:
                            low(tb, c)
                    if tb is not None:
                        finish(tb)

                skewed_tiles(v, front)


def program(nc, io, outs):
    with ExitStack() as ctx:
        X = ctx.enter_context(nc.sbuf_tensor("X", [P, NT, D], F32))
        cut = WeightCut(nc, ctx, io)
        ew = ExpertWeights(nc, ctx, io, cut)
        stage1(nc, io, X, cut)
        stage2(nc, io, X, cut, ew)
        stage3(nc, io, X, ew, outs[0])


def kernel(**inputs):
    import concourse.bacc as bacc
    from concourse.bass_utils import run_bass_kernel_spmd as run

    A = {k: np.asarray(v) for k, v in inputs.items()}
    L = lambda n: A["L0_attn_" + n]
    rows = lambda a: np.ascontiguousarray(np.broadcast_to(a.reshape(1, -1), (P, a.size)))
    cuts = lambda a: [a[:, h * P:(h + 1) * P] for h in range(H)]
    q, k = cuts(L("Wq")), cuts(L("Wk"))
    cq, ck = [c.reshape(H, P, 4) for c in (L("conv_wq"), L("conv_wk"))]
    w1 = [L("Wb"), L("Wa")]
    cw = []
    for h in range(H):
        w1 += [k[h], q[h]]
        cw += [ck[h], cq[h]]
    w1 += [L("Wv"), L("Wg")]
    cw += list(L("conv_wv").reshape(3, P, 4))
    u = np.arange(P)[:, None]
    s, t = np.arange(P)[None, :], np.arange(T)[None, :]
    consts = np.concatenate([
        u == s, (u > s) & (u // T == s // T), u % T <= t, t >= u % T, t // BLK > (u % T) // BLK,
    ], axis=1).astype(np.float32)
    x = A["x"].reshape(NTOK, D)
    arrays = {
        "x": x, "xT": x.T, "w1": np.concatenate(w1, axis=1), "wo": L("Wo"),
        "convw": np.stack(cw, axis=1),
        "dtb": rows(L("dt_bias")), "alog": rows(L("A_log")), "normw": rows(L("norm_w")),
        "consts": consts, "eyes": (np.arange(BLK * BLK // 2)[None, :] // BLK * 2 + (np.arange(P)[:, None] >= YP)
                 == np.arange(BLK * BLK // 2)[None, :] % BLK).astype(np.float32),
    }
    Y = lambda n: A["L0_xattn_" + n]
    wqT, wqxT, wkT, wvT, wkvxT = (Y(n).T for n in ("wq", "wqx", "wk", "wv", "w_kv_x"))
    w2 = []
    for q_, k_, v_ in ((wqT, wkT, wvT), (wqxT, wkvxT[:, :G * P], wkvxT[:, G * P:])):
        for half in range(2):
            w2 += [q_[:, half * 1024:(half + 1) * 1024], k_[:, half * 512:(half + 1) * 512],
                   v_[:, half * 512:(half + 1) * 512]]
    cols = lambda a, n: a.reshape(n, P).T
    prm2 = [cols(Y("ln_w"), 2), cols(Y("ln_b"), 2)]
    prm2 += [cols(Y(n + "_in_scale"), 2) for n in ("q", "qx", "k", "v")]
    for n in ("q", "qx", "k", "kx"):
        prm2 += [cols(Y(n + "ln_w"), 1), cols(Y(n + "ln_b"), 1)]
    prm2 += [rows(Y(n)) for n in ("wq_scale", "wqx_scale", "wk_scale", "wv_scale", "proj_in_scale", "proj_w_scale")]
    prm2 += [cols(Y("proj_smooth"), NH2)]
    arrays.update({"w2": np.concatenate(w2, axis=1), "wproj": Y("wproj").T, "ctxT": A["ctx_2048"].reshape(NTOK, D).T,
                   "prm2": np.concatenate(prm2, axis=1)})
    Z = lambda n: A["L0_ffn_" + n]
    e1, e2 = Z("expert_fc1").reshape(E * FE, D).T, Z("expert_fc2").reshape(E * FE, D).T
    f1, f2 = np.concatenate([e1, Z("shared_fc1").T], axis=1), np.concatenate([e2, Z("shared_fc2").T], axis=1)
    wu = [w[:, c * FC:(c + 1) * FC] for c in range(NC3) for w in (f1, f2)]
    wd = np.concatenate([Z("expert_proj").transpose(0, 2, 1).reshape(E * FE, D), Z("shared_proj").T,
                         np.zeros((NB3 * P - FF, D), np.float32)])
    arrays.update({"wu": np.concatenate(wu, axis=1), "wd": wd,
                   "wr": np.concatenate([Z("gate_w").T, Z("shared_gate_w").T], axis=1),
                   "iota": rows(np.arange(E, dtype=np.float32))})
    nc = bacc.Bacc("TRN2", target_bir_lowering=False, num_devices=1)
    feed, io = {}, {}
    for n, a in arrays.items():
        a = np.ascontiguousarray(a)
        feed["in_" + n] = a
        io[n] = nc.dram_tensor("in_" + n, a.shape, F32, kind="ExternalInput").ap()
    out = nc.dram_tensor("out_0", (NTOK, D), F32, kind="ExternalOutput").ap()
    program(nc, io, [out])
    r = run(nc, [feed], core_ids=[0])
    return r.results[0]["out_0"].reshape(16, T, D)
```
